# Optimizing a Trainium2 kernel written in Bass

```python
import numpy as np
import jax
import jax.numpy as jnp

def _softmax(x, axis=-1):
    return jax.nn.softmax(x, axis=axis)

def _gelu(x):
    return jax.nn.gelu(x, approximate=True)

def _silu(x):
    return jax.nn.silu(x)

def _sigmoid(x):
    return jax.nn.sigmoid(x)

def _layernorm(x, axis=-1, eps=1e-05):
    m = jnp.mean(x, axis=axis, keepdims=True)
    v = jnp.var(x, axis=axis, keepdims=True)
    return (x - m) / jnp.sqrt(v + eps)

def _scatter_add(tgt, idx, src, axis=0):
    return tgt.at[idx].add(src)

def _segment_sum(src, seg, n):
    return jax.ops.segment_sum(src, seg, n)
kernel_name = 'mk_adaln_d1_jaxref_r4_93bb07'

def setup_inputs(seed: int=0):
    np.random.seed(seed)
    _w = jnp.asarray

    def _L0_attn_setup():
        import jax, jax.numpy as jnp
        import numpy as np
        B, T = (4, 1024)
        D_MODEL, N_HEADS = (256, 16)
        N_SINKS, WINDOW = (4, 128)
        D_HEAD = D_MODEL // N_HEADS
        key = jax.random.key(seed)
        k1, k2, k3, k4, k5 = jax.random.split(key, 5)
        s = D_MODEL ** (-0.5)
        x = jax.random.normal(k1, (B, T, D_MODEL), dtype=jnp.float32)
        Wq = jax.random.normal(k2, (D_MODEL, D_MODEL), dtype=jnp.float32) * s
        Wk = jax.random.normal(k3, (D_MODEL, D_MODEL), dtype=jnp.float32) * s
        Wv = jax.random.normal(k4, (D_MODEL, D_MODEL), dtype=jnp.float32) * s
        Wo = jax.random.normal(k5, (D_MODEL, D_MODEL), dtype=jnp.float32) * s
        return {'x': x, 'Wq': Wq, 'Wk': Wk, 'Wv': Wv, 'Wo': Wo}
    _L0_attn_in = _L0_attn_setup()

    def _L0_ffn_setup():
        import jax, jax.numpy as jnp
        import numpy as np
        H = 256
        M = 128
        E = 16
        TOP_K = 2
        SCALE = 2.5
        NORM_TOPK = True
        B, S = (1, 256)

        def _moe(x, gate_w, w_gate, w_up, w_down, ws_gate, ws_up, ws_down):
            T = x.shape[0]
            shared = jax.nn.silu(x @ ws_gate) * (x @ ws_up) @ ws_down
            scores = jax.nn.sigmoid(x.astype(jnp.float32) @ gate_w.T.astype(jnp.float32))
            topk_w, topk_idx = jax.lax.top_k(scores, TOP_K)
            if NORM_TOPK and TOP_K > 1:
                topk_w = topk_w / (topk_w.sum(-1, keepdims=True) + 1e-20)
            topk_w = topk_w * SCALE
            route = jnp.zeros((T, E), topk_w.dtype).at[jnp.arange(T)[:, None], topk_idx].set(topk_w)
            g = jnp.einsum('th,ehm->etm', x, w_gate)
            u = jnp.einsum('th,ehm->etm', x, w_up)
            eo = jnp.einsum('etm,emh->eth', jax.nn.silu(g) * u, w_down)
            routed = jnp.einsum('te,eth->th', route.astype(x.dtype), eo)
            return routed + shared
        key = jax.random.key(seed)
        ks = jax.random.split(key, 8)
        std = 0.02
        return {'hidden_states': jax.random.normal(ks[0], (B, S, H), jnp.float32), 'gate_w': jax.random.normal(ks[1], (E, H), jnp.float32) * std, 'w_gate': jax.random.normal(ks[2], (E, H, M), jnp.float32) * std, 'w_up': jax.random.normal(ks[3], (E, H, M), jnp.float32) * std, 'w_down': jax.random.normal(ks[4], (E, M, H), jnp.float32) * std, 'ws_gate': jax.random.normal(ks[5], (H, M), jnp.float32) * std, 'ws_up': jax.random.normal(ks[6], (H, M), jnp.float32) * std, 'ws_down': jax.random.normal(ks[7], (M, H), jnp.float32) * std}
    _L0_ffn_in = _L0_ffn_setup()
    _L0_c = _w((lambda *s: np.random.randn(*s).astype(np.float32) * 0.05)(4, 256))
    _L0_wmod = _w((lambda *s: np.random.randn(*s).astype(np.float32) * 0.05)(256, 6 * 256) * 256 ** (-0.5))
    _d = {'L0_attn_x': _L0_attn_in['x'], 'L0_attn_Wq': _L0_attn_in['Wq'], 'L0_attn_Wk': _L0_attn_in['Wk'], 'L0_attn_Wv': _L0_attn_in['Wv'], 'L0_attn_Wo': _L0_attn_in['Wo'], 'L0_ffn_gate_w': _L0_ffn_in['gate_w'], 'L0_ffn_w_gate': _L0_ffn_in['w_gate'], 'L0_ffn_w_up': _L0_ffn_in['w_up'], 'L0_ffn_w_down': _L0_ffn_in['w_down'], 'L0_ffn_ws_gate': _L0_ffn_in['ws_gate'], 'L0_ffn_ws_up': _L0_ffn_in['ws_up'], 'L0_ffn_ws_down': _L0_ffn_in['ws_down'], 'L0_c': _L0_c, 'L0_wmod': _L0_wmod}
    _x0 = _d['L0_attn_x']
    _d['L0_attn_x'] = jax.random.normal(jax.random.fold_in(jax.random.key(seed), 1), (4, 1024, 256), dtype=_x0.dtype)
    del _x0
    return _d

def reference(L0_attn_x, L0_attn_Wq, L0_attn_Wk, L0_attn_Wv, L0_attn_Wo, L0_ffn_gate_w, L0_ffn_w_gate, L0_ffn_w_up, L0_ffn_w_down, L0_ffn_ws_gate, L0_ffn_ws_up, L0_ffn_ws_down, L0_c, L0_wmod):

    def _L0_attn_ref(x, Wq, Wk, Wv, Wo):
        import jax, jax.numpy as jnp
        import numpy as np
        B, T = (4, 1024)
        D_MODEL, N_HEADS = (256, 16)
        N_SINKS, WINDOW = (4, 128)
        D_HEAD = D_MODEL // N_HEADS
        b, t, d = x.shape

        def split_heads(h):
            return h.reshape(b, t, N_HEADS, D_HEAD).transpose(0, 2, 1, 3)
        q = split_heads(x @ Wq)
        k = split_heads(x @ Wk)
        v = split_heads(x @ Wv)
        sink_k, sink_v = (k[:, :, :N_SINKS], v[:, :, :N_SINKS])
        win_k = k[:, :, N_SINKS:][:, :, -WINDOW:]
        win_v = v[:, :, N_SINKS:][:, :, -WINDOW:]
        ctx_k = jnp.concatenate([sink_k, win_k], axis=2)
        ctx_v = jnp.concatenate([sink_v, win_v], axis=2)
        t_ctx = ctx_k.shape[2]
        scale = D_HEAD ** (-0.5)
        logits = jnp.einsum('bhqd,bhkd->bhqk', q, ctx_k) * scale
        rows = jnp.arange(t)[:, None]
        cols = jnp.arange(t_ctx)[None, :]
        mask = cols <= rows + (t_ctx - t)
        logits = jnp.where(mask, logits, -jnp.inf)
        w = jax.nn.softmax(logits, axis=-1)
        w = jnp.where(jnp.isnan(w), jnp.zeros_like(w), w)
        out = jnp.einsum('bhqk,bhkd->bhqd', w, ctx_v)
        out = out.transpose(0, 2, 1, 3).reshape(b, t, d)
        return out @ Wo

    def _L0_ffn_ref(hidden_states, gate_w, w_gate, w_up, w_down, ws_gate, ws_up, ws_down):
        import jax, jax.numpy as jnp
        import numpy as np
        H = 256
        M = 128
        E = 16
        TOP_K = 2
        SCALE = 2.5
        NORM_TOPK = True
        B, S = (1, 256)

        def _moe(x, gate_w, w_gate, w_up, w_down, ws_gate, ws_up, ws_down):
            T = x.shape[0]
            shared = jax.nn.silu(x @ ws_gate) * (x @ ws_up) @ ws_down
            scores = jax.nn.sigmoid(x.astype(jnp.float32) @ gate_w.T.astype(jnp.float32))
            topk_w, topk_idx = jax.lax.top_k(scores, TOP_K)
            if NORM_TOPK and TOP_K > 1:
                topk_w = topk_w / (topk_w.sum(-1, keepdims=True) + 1e-20)
            topk_w = topk_w * SCALE
            route = jnp.zeros((T, E), topk_w.dtype).at[jnp.arange(T)[:, None], topk_idx].set(topk_w)
            g = jnp.einsum('th,ehm->etm', x, w_gate)
            u = jnp.einsum('th,ehm->etm', x, w_up)
            eo = jnp.einsum('etm,emh->eth', jax.nn.silu(g) * u, w_down)
            routed = jnp.einsum('te,eth->th', route.astype(x.dtype), eo)
            return routed + shared
        b, s, h = hidden_states.shape
        x = hidden_states.reshape(-1, h)
        out = _moe(x, gate_w, w_gate, w_up, w_down, ws_gate, ws_up, ws_down)
        return out.reshape(b, s, h)
    x = L0_attn_x
    mod = (_silu(L0_c) @ L0_wmod).reshape(L0_c.shape[0], 6, 1, -1)
    sa, ca, ga, sb, cb, gb = (mod[:, 0], mod[:, 1], mod[:, 2], mod[:, 3], mod[:, 4], mod[:, 5])
    ga = (2 * (ga >= 0) - 1) * jnp.maximum(jnp.abs(ga), 0.25)
    gb = (2 * (gb >= 0) - 1) * jnp.maximum(jnp.abs(gb), 0.25)
    h = _layernorm(x, axis=-1) * (1 + ca) + sa
    x = x + ga * _L0_attn_ref(h, L0_attn_Wq, L0_attn_Wk, L0_attn_Wv, L0_attn_Wo)
    h = _layernorm(x, axis=-1) * (1 + cb) + sb
    x = x + gb * _L0_ffn_ref(h, L0_ffn_gate_w, L0_ffn_w_gate, L0_ffn_w_up, L0_ffn_w_down, L0_ffn_ws_gate, L0_ffn_ws_up, L0_ffn_ws_down)
    return x

_drawn_inputs = setup_inputs


def setup_inputs(seed=0):
    import zlib

    import numpy as np

    out = dict(_drawn_inputs(seed))
    spreads = {}
    factors = {'L0_attn_Wq': 3.3,
     'L0_attn_Wk': 3.25,
     'L0_ffn_gate_w': 8.0,
     'L0_ffn_w_gate': 8.0,
     'L0_ffn_w_up': 8.0,
     'L0_ffn_w_down': 8.0,
     'L0_ffn_ws_gate': 8.0,
     'L0_ffn_ws_up': 8.0,
     'L0_ffn_ws_down': 8.0}
    for name, (base, spread) in spreads.items():
        noise = np.random.default_rng([zlib.crc32(name.encode()), seed]).standard_normal(out[name].shape)
        drawn = base * np.exp(spread * noise) if base else spread * noise
        out[name] = jnp.asarray(drawn.astype(out[name].dtype))
    for name, factor in factors.items():
        out[name] = (out[name] * factor).astype(out[name].dtype)
    return out
```

```python
from contextlib import ExitStack

import concourse.bass as bass
from concourse import mybir

ALU = mybir.AluOpType
ACT = mybir.ActivationFunctionType
AX = mybir.AxisListType
F32 = mybir.dt.float32
BF16 = mybir.dt.bfloat16
I32 = mybir.dt.int32
U32 = mybir.dt.uint32
ds = bass.ds

P = 128
MASKED = -1e30
EPS = 1e-5
SATURATED = 16.6355
UNROLL = 4
SPARE = 2 * UNROLL


def bass_adaln_attention_moe(nc, x, wq, wk, wv, wo, gate_w, w_gate, w_up, w_down, ws_gate, ws_up,
                             ws_down, cond, w_mod, out):
    B, T, D = x.shape
    NE, _, M = w_gate.shape
    H, SINKS, WINDOW = 16, 4, 128
    DH = D // H
    SCALE = DH ** -0.5
    TOPK, ROUTE_SCALE = 2, 2.5
    C = D // P
    HG = H * 32 // P
    TPB = T // P
    TILES = B * TPB
    GROUP = 4
    GPB = TPB // GROUP
    CAP = B * T // P + 1
    MAX_TILES = (B * T * TOPK - NE) // P + NE
    MAX_TILES += -MAX_TILES % UNROLL
    MIN_TILES = B * T * TOPK // P
    TABLE = MAX_TILES + UNROLL
    ROWS = (NE * CAP + SPARE) * P
    NB = B * SINKS
    DA = DH + 1
    DX = D + 2
    PAD = 2.0 ** 20
    NR = NE + 2 * M
    assert WINDOW == P and D == 2 * P and M == P and H * SINKS == 64

    with ExitStack() as ctx:
        def sb(name, shape, dt=F32):
            return ctx.enter_context(nc.sbuf_tensor(name, shape, dt))

        def sem(name):
            return ctx.enter_context(nc.semaphore(name))

        slots = nc.dram_tensor("slots", (ROWS, DX), F32, kind="Internal").ap()
        ys = nc.dram_tensor("ys", (TOPK * B * T + TABLE * P, D), F32, kind="Internal").ap()

        bank = [ctx.enter_context(nc.psum_tensor(f"bank{i}", [P, 512], F32)) for i in range(8)]

        ident = sb("ident", [P, P])
        ident_b = sb("ident_b", [P, P], BF16)
        before_b = sb("before_b", [P, P], BF16)
        ones_b = sb("ones_b", [P, P], BF16)
        causal_b = sb("causal_b", [P, P], BF16)
        small_mask_b = sb("small_mask_b", [NB, B * H * SINKS], BF16)
        head_block = sb("head_block", [H * SINKS, H])
        quarter = sb("quarter", [P, 4])
        pick = sb("pick", [B, B, P])
        pick_rows = sb("pick_rows", [B, NB])
        expert_no = sb("expert_no", [P, NE])
        expert_row = sb("expert_row", [P, NE])
        minus_half = sb("minus_half", [P, 8])
        pads = sb("pads", [P, DX])
        token2 = sb("token2", [P, TILES])
        pad_row = sb("pad_row", [P, TABLE])
        h_sb = sb("h_sb", [P, TPB, DX])
        ht = sb("ht", [P, UNROLL, C, P])
        h_flat = h_sb[:].rearrange("p j d -> p (j d)")
        wq_in, wk_in = [h_flat[:, n * C * D:(n + 1) * C * D].rearrange("p (c d) -> p c d", c=C) for n in range(2)]
        gabs, gsign = [h_flat[0:B, (4 + 2 * n) * D:(6 + 2 * n) * D].rearrange("p (s d) -> p s d", s=2)
                       for n in range(2)]
        ht_flat = ht[:].rearrange("p k c n -> p (k c n)")
        sm_in, sm_xn = [ht_flat[0:2 * NB, n * D:(n + 1) * D] for n in range(2)]
        sm_q, sm_x1 = [ht_flat[0:NB, n * D:(n + 1) * D] for n in range(2, 4)]
        wq_pad = sb("wq_pad", [P, C, H * 32])
        wk_pad = sb("wk_pad", [P, C, H * 32])
        wv_sb = sb("wv_sb", [P, C, D])
        wo_sb = sb("wo_sb", [P, C, D])
        gate_in = sb("gate_in", [NE, D])
        w_route = sb("w_route", [P, C, NR])
        wsd_sb = sb("wsd_sb", [P, D])
        wsd_gated = sb("wsd_gated", [P, D])
        w_gu = sb("w_gu", [P, NE * C * 2 * M])
        w_dn = sb("w_dn", [P, NE * D])
        cond_in = sb("cond_in", [B, D])
        cond_act = sb("cond_act", [B, D])
        cond_t = sb("cond_t", [P, C, B])
        wmod_sb = sb("wmod_sb", [P, C, 6 * D])
        wmod_flat = wmod_sb[:].rearrange("p c n -> p (c n)")
        kt_flat = wmod_flat[:, 0:HG * 4 * P]
        kt_bd = kt_flat.rearrange("p (g i n) -> p g i n", g=HG, i=4)
        mod_col = sb("mod_col", [P, 2 * C * B])
        GA, SB_, CB, GB = range(4)
        NORMED = slice(0, 2), slice(2, TPB - 1), slice(TPB - 1, TPB)
        PT_BANK = 6, 6, 4, 6, 5
        mod_bc = sb("mod_bc", [P, B * 4 * D])
        xs = sb("xs", [P, TILES * D])
        sm_stats = sb("sm_stats", [2 * NB, 6])
        sm_mv = sb("sm_mv", [2 * NB, 2])
        sm_rstd = sb("sm_rstd", [2 * NB, 2])
        sm_h = sb("sm_h", [P, C, 2, B, SINKS])
        sm_q_t = sb("sm_q_t", [P, HG, NB])
        sink_kt = sb("sink_kt", [P, HG, 4, NB])
        sink_v = sb("sink_v", [H * SINKS, B * H * DA])
        sm_m = sb("sm_m", [NB, H])
        sm_p = sb("sm_p", [NB, B, H, SINKS])
        sm_pt = sb("sm_pt", [H * SINKS, B, NB])
        sm_r = sb("sm_r", [NB, H])
        sm_o = sb("sm_o", [NB, H, DH])
        sm_ot = sb("sm_ot", [P, C, NB])
        sm_ga = sb("sm_ga", [NB, D])
        at_stats = sb("at_stats", [P, 6])
        at_mv = sb("at_mv", [P, 2])
        at_rs = sb("at_rs", [P, 2])
        at_xn_sb = sb("at_xn_sb", [P, D])
        at_ht = sb("at_ht", [P, C, P])
        qt = sb("qt", [P, HG, P])
        v_aug = sb("v_aug", [P, H, DA])
        m_sink = sb("m_sink", [P, H])
        m_win = sb("m_win", [P, H])
        m_all = sb("m_all", [P, H])
        p_sink = sb("p_sink", [P, H, SINKS])
        p_win = sb("p_win", [P, H, P])
        p_flat = p_win[:].rearrange("p h n -> p (h n)")
        mod = p_flat[0:B, 0:6 * D]
        pt_sink = sb("pt_sink", [H * SINKS, P])
        pt_win = sb("pt_win", [P, H, P])
        rden = sb("rden", [P, H])
        o_n = sb("o_n", [P, H, DH])
        o_t = sb("o_t", [P, C, P])
        o_g = sb("o_g", [P, D])
        st = sb("st", [P, TPB, 6])
        mv = sb("mv", [P, TPB, 2])
        veps = sb("veps", [P, TPB])
        rstd = sb("rstd", [P, TPB])
        centred = sb("centred", [P, 2, D])
        sm_hrep = centred[:].rearrange("p a d -> p (a d)")
        sg = sb("sg", [P, UNROLL, M])
        act_sb = sb("act_sb", [P, UNROLL, M])
        act_t = sb("act_t", [P, UNROLL, P])
        logit = sb("logit", [P, TPB, NE])
        top_v = sb("top_v", [P, TPB, 8])
        top_i = sb("top_i", [P, TPB, 8], U32)
        top_if = sb("top_if", [P, GROUP, TOPK])
        hot = sb("hot", [P, TOPK, GROUP, NE])
        mask_b = sb("mask_b", [P, GROUP, NE], BF16)
        mask_sum = sb("mask_sum", [P, NE])
        counted_b = sb("counted_b", [P, 2, NE], BF16)
        place = sb("place", [P, GROUP, NE])
        at_place = sb("at_place", [P, TOPK, GROUP, NE])
        slot_f = sb("slot_f", [P, TOPK, GROUP])
        slot_i = sb("slot_i", [P, TOPK, TPB], I32)
        val_all = sb("val_all", [P, TOPK, TILES])
        e_neg = sb("e_neg", [P, TOPK * TILES])
        score = sb("score", [P, TOPK, TILES])
        total = sb("total", [P, TILES])
        w_tok = sb("w_tok", [P, TOPK * TILES])
        steps_no = sb("steps_no", [P, TABLE])
        row_no = sb("row_no", [P, CAP - 1])
        n_e = sb("n_e", [P, NE])
        over = sb("over", [P, NE, CAP - 1])
        nt_e = sb("nt_e", [P, NE])
        ones_row = sb("ones_row", [P, NE])
        end_e = sb("end_e", [P, NE])
        tile_e = sb("tile_e", [P, TABLE])
        jump = sb("jump", [1, NE])
        past = wmod_flat[:, 0:TABLE * NE].rearrange("p (t e) -> p t e", e=NE)
        past_jump = wmod_flat[0:1, TABLE * NE:2 * TABLE * NE].rearrange("p (t e) -> p t e", e=NE)
        tab_f = sb("tab_f", [1, 2, TABLE])
        n_over = sb("n_over", [1, MAX_TILES // UNROLL])
        misc_f = sb("misc_f", [1, NE + 1])
        tab = sb("tab", [1, 2 * TABLE], I32)
        misc = sb("misc", [1, NE + 1], I32)
        xt = p_flat[:, 0:UNROLL * DX].rearrange("p (k d) -> p k d", d=DX)
        pt_flat = pt_win[:].rearrange("p h n -> p (h n)")
        y_sb = pt_flat[:, 0:UNROLL * D].rearrange("p (k d) -> p k d", d=D)
        row_f = sb("row_f", [P, UNROLL])
        row_i = sb("row_i", [P, UNROLL], I32)
        got = wmod_flat[:, 0:UNROLL * TOPK * D].rearrange("p (k n d) -> p k n d", n=TOPK, d=D)

        names = """
        ld_cond ld_wmod ld_small ld_smallq ld_wqk ld_wv ld_wo ld_gate ld_ws ld_wsd ld_exp x_small pad_dmas
        const eye wq_ready wk_ready sc_t ct_ready cond_ready gate_t mod_ps mod_rows gate_chain mod_ready col_ps
        col_ready bc_ps bc_sb
        sm_veps sm_rs sm_xnr sm_chain sm_t sm_hr sm_proj sm_vps sm_kqr sm_vr sm_log sm_sub sm_exp sm_ptp sm_ptr
        sm_ops sm_or sm_otp sm_otr sm_out sm_gaps sm_gar sm_done
        at_ch at_veps at_rstd at_xn at_xnt at_h at_q at_k at_v at_qs at_ks at_kas at_vs at_log at_mx at_sub
        at_exp at_pt at_pts at_o at_on at_ot at_ots at_out at_x
        ln_ch ln_veps ln_rstd h_cent h_ready wsd_ready kt_zero
        tr_ps tr_sb gu_ps tanh_ready act_ch act_ready aps_ready act_t_sb y_ps y_added lg_ready top_ch rt_ch masks rank_ps
        rank_read slots_ready
        cnt_ps tb tables ex_tr ex_ht ex_gu ex_silu ex_act ex_ap ex_at ex_y ex_ysb
        row_ch row_ready waited_apart w_ch e_ready w_ready part_ready both_ready gated_ready out_ready saved
        """.split()
        S = {n: sem(n) for n in names}
        ld_x = [sem(f"ld_x{b}") for b in range(B)]
        xt_in = [sem(f"xt_in{i}") for i in range(UNROLL)]
        y_out = [sem(f"y_out{i}") for i in range(UNROLL)]
        scattered = [sem(f"scattered{j}") for j in range(TPB)]
        got_in = [sem(f"got_in{i}") for i in range(UNROLL)]

        def xcols(t):
            return xs[:, ds(t * D, D)]

        def mbc(b, kind, n=1):
            return mod_bc[:, ds(b * (4 * D) + kind * D, n * D)]

        class Chain:

            def __init__(self, eng, s, i=0, per=0, at=0):
                self.eng, self.s, self.i, self.per, self.n = eng, s, i, per, at

            def done(self, ins, alone=False):
                ins.then_inc(self.s, 1)
                self.n += 1
                wait = wait_apart if alone else type(self.eng).wait_ge
                wait(self.eng, self.s, self.i * self.per + self.n)

        def wait_apart(eng, s, value):
            eng.wait_ge(s, value)
            eng.sem_inc(S["waited_apart"], 1)

        block = ctx.enter_context(nc.Block())

        @block.sync
        def _(sp):
            chunks = lambda w: w.rearrange("(c p) n -> p c n", p=P)
            sp.dma_start(cond_in[:], cond).then_inc(S["ld_cond"], 16)
            for b in range(B):
                sp.dma_start(sm_in[b * SINKS:(b + 1) * SINKS, :], x[b, 0:SINKS, :]).then_inc(S["ld_small"], 16)
                late = x[b, T - P - SINKS:T - P, :]
                sp.dma_start(sm_in[NB + b * SINKS:NB + (b + 1) * SINKS, :], late).then_inc(S["ld_small"], 16)
                sp.dma_start(sm_q[b * SINKS:(b + 1) * SINKS, :], late).then_inc(S["ld_smallq"], 16)
            sp.dma_start(wmod_sb[:], chunks(w_mod)).then_inc(S["ld_wmod"], 16)
            sp.dma_start(wq_in, chunks(wq)).then_inc(S["ld_wqk"], 16)
            sp.dma_start(wk_in, chunks(wk)).then_inc(S["ld_wqk"], 16)
            sp.dma_start(wv_sb[:], chunks(wv)).then_inc(S["ld_wv"], 16)
            sp.dma_start(wo_sb[:], chunks(wo)).then_inc(S["ld_wo"], 16)
            sp.dma_start(gate_in[:], gate_w).then_inc(S["ld_gate"], 16)
            for b in range(B):
                dst = xs[:, b * TPB * D:(b + 1) * TPB * D].rearrange("p (j d) -> p j d", d=D)
                sp.dma_start(dst, x[b].rearrange("(j p) d -> p j d", p=P)).then_inc(ld_x[b], 16)
                if b == 0:
                    sp.dma_start(w_route[:, :, NE:NE + M], chunks(ws_gate)).then_inc(S["ld_ws"], 16)
                    sp.dma_start(w_route[:, :, NE + M:NR], chunks(ws_up)).then_inc(S["ld_ws"], 16)
                    sp.dma_start(wsd_sb[:], ws_down).then_inc(S["ld_wsd"], 16)
            sp.wait_ge(S["sm_done"], 1)
            for b in range(B):
                sp.wait_ge(ld_x[b], 16)
                j = b * TPB + TPB - 2
                sp.dma_start(xs[P - SINKS:P, j * D:(j + 1) * D],
                             sm_x1[b * SINKS:(b + 1) * SINKS, :]).then_inc(S["x_small"], 16)
            gu = w_gu[:].rearrange("p (e c m) -> p e c m", c=C, m=2 * M)
            for n, w in enumerate((w_gate, w_up)):
                for c in range(C):
                    sp.dma_start(gu[:, :, c, n * M:(n + 1) * M],
                                 w[:, c * P:(c + 1) * P, :].rearrange("e p m -> p e m")).then_inc(S["ld_exp"], 16)
            sp.dma_start(w_dn[:].rearrange("p (e n) -> p e n", n=D),
                         w_down.rearrange("e p n -> p e n")).then_inc(S["ld_exp"], 16)
            sp.wait_ge(S["const"], N_CONST)
            for s in range(SPARE):
                r = (NE * CAP + s) * P
                sp.dma_start(slots[r:r + P, :], pads[:]).then_inc(S["pad_dmas"], 16)

            sp.wait_ge(S["tables"], 1)
            with sp.Fori(0, NE) as e:
                row = sp.value_load(misc[0:1, ds(e, 1)], min_val=0, max_val=ROWS - P)
                sp.dma_start(slots[ds(row, P), :], pads[:]).then_inc(S["pad_dmas"], 16)
            last4 = sp.value_load(misc[0:1, NE:NE + 1], min_val=MIN_TILES // UNROLL - 1, max_val=MAX_TILES // UNROLL - 1)
            fours = last4 + 1
            sp.wait_ge(S["pad_dmas"], 16 * (SPARE + NE))
            for j in range(TPB):
                sp.wait_ge(scattered[j], 16 * TOPK * B)

            def load(t, k):
                blk = sp.value_load(tab[0:1, ds(t + TABLE, 1)], min_val=0, max_val=ROWS // P - 1)
                sp.dma_start(xt[:, k, :], slots[ds(blk * P, P), :]).then_inc(xt_in[k], 16)

            for k in range(UNROLL):
                load(k, k)
            with sp.Fori(0, fours) as u:
                for k in range(UNROLL):
                    wait_apart(sp, S["ex_tr"], u * UNROLL + k + 1)
                    wait_apart(sp, S["row_ready"], u * UNROLL + k + 1)
                    load(u * UNROLL + k + UNROLL, k)
            for k in range(UNROLL):
                wait_apart(sp, y_out[k], fours * 16)
                wait_apart(sp, xt_in[k], fours * 16 + 16)

            def load_pair(t, k):
                sp.dma_start(got[:, k, :, :].rearrange("p n d -> p (n d)"),
                             ys[ds(t * (TOPK * P), TOPK * P), :].rearrange("(p n) d -> p (n d)", n=TOPK))\
                    .then_inc(got_in[k], 16)

            def save(t):
                sp.dma_start(out.rearrange("b t d -> (b t) d")[ds(t * P, P), :], xcols(t)).then_inc(S["saved"], 16)

            for k in range(UNROLL):
                load_pair(k, k)
            with sp.Fori(0, TILES // UNROLL - 1) as u:
                for k in range(UNROLL):
                    wait_apart(sp, S["out_ready"], u * UNROLL + k + 1)
                    load_pair(u * UNROLL + k + UNROLL, k)
                    save(u * UNROLL + k)
            for t in range(TILES - UNROLL, TILES):
                sp.wait_ge(S["out_ready"], t + 1)
                save(t)
            sp.wait_ge(S["saved"], 16 * TILES)

        @block.gpsimd
        def _(pool):
            eye = Chain(pool, S["eye"])
            eye.done(pool.memset(ident[:], 0.0))
            eye.done(pool.affine_select(out=ident[:], in_=ident[:], pattern=[[-1, P]], compare_op=ALU.not_equal,
                                        fill=1.0, base=0, channel_multiplier=1))
            eye.done(pool.memset(minus_half[:], -0.5))
            c = Chain(pool, S["const"])
            c.done(pool.memset(wq_pad[:], 0.0))
            c.done(pool.memset(wk_pad[:], 0.0))
            pool.wait_ge(S["ld_wqk"], 32)
            for src, dst, s in ((wq_in, wq_pad, "wq_ready"), (wk_in, wk_pad, "wk_ready")):
                for k in range(C):
                    pool.tensor_copy(dst[:, k, :].rearrange("p (g i s) -> p i g s", i=4, s=32)[:, :, :, 0:DH],
                                     src[:, k, :].rearrange("p (i g s) -> p i g s", i=4, s=DH)).then_inc(S[s], 1)
            pool.wait_ge(S["sm_veps"], 1)
            pool.tensor_tensor(sm_rstd[:, 1:2], sm_rstd[:, 0:1], minus_half[0:2 * NB, 0:1], ALU.pow)\
                .then_inc(S["sm_rs"], 1)
            c.done(pool.memset(head_block[:], 1.0))
            c.done(pool.affine_select(out=head_block[:], in_=head_block[:], pattern=[[-SINKS, H]],
                                      compare_op=ALU.is_ge, fill=0.0, base=0, channel_multiplier=1))
            c.done(pool.affine_select(out=head_block[:], in_=head_block[:], pattern=[[SINKS, H]],
                                      compare_op=ALU.is_ge, fill=0.0, base=SINKS - 1, channel_multiplier=-1))
            c.done(pool.memset(quarter[:], 1.0))
            c.done(pool.affine_select(out=quarter[:], in_=quarter[:], pattern=[[-32, 4]],
                                      compare_op=ALU.is_ge, fill=0.0, base=0, channel_multiplier=1))
            c.done(pool.affine_select(out=quarter[:], in_=quarter[:], pattern=[[32, 4]],
                                      compare_op=ALU.is_ge, fill=0.0, base=31, channel_multiplier=-1))
            c.done(pool.tensor_copy(ident_b[:], ident[:]))
            c.done(pool.memset(small_mask_b[:], 0.0))
            c.done(pool.affine_select(out=small_mask_b[:], in_=small_mask_b[:],
                                      pattern=[[-SINKS, B], [0, H], [-1, SINKS]], compare_op=ALU.is_ge,
                                      fill=MASKED, base=0, channel_multiplier=1))
            c.done(pool.affine_select(out=small_mask_b[:], in_=small_mask_b[:],
                                      pattern=[[SINKS, B], [0, H], [0, SINKS]], compare_op=ALU.is_ge,
                                      fill=MASKED, base=SINKS - 1, channel_multiplier=-1))
            c.done(pool.memset(causal_b[:], 0.0))
            c.done(pool.affine_select(out=causal_b[:], in_=causal_b[:], pattern=[[-1, P]], compare_op=ALU.is_ge,
                                      fill=MASKED, base=0, channel_multiplier=1))
            c.done(pool.memset(pick[:], 0.0))
            c.done(pool.affine_select(out=pick[:], in_=pick[:], pattern=[[-1, B], [0, P]],
                                      compare_op=ALU.not_equal, fill=1.0, base=0, channel_multiplier=1))
            c.done(pool.memset(pick_rows[:], 0.0))
            c.done(pool.affine_select(out=pick_rows[:], in_=pick_rows[:], pattern=[[-1, B], [0, SINKS]],
                                      compare_op=ALU.not_equal, fill=1.0, base=0, channel_multiplier=1))
            c.done(pool.memset(before_b[:], 0.0))
            c.done(pool.affine_select(out=before_b[:], in_=before_b[:], pattern=[[-1, P]], compare_op=ALU.is_ge,
                                      fill=1.0, base=0, channel_multiplier=1))
            c.done(pool.memset(ones_b[:], 1.0))
            c.done(pool.memset(v_aug[:], 1.0))
            c.done(pool.memset(counted_b[:], 0.0))
            c.done(pool.memset(pads[:], 0.0))
            c.done(pool.memset(pads[:, D:D + 1], PAD))
            c.done(pool.iota(token2[:], pattern=[[2 * P, TILES]], base=0, channel_multiplier=2,
                             allow_small_or_imprecise_dtypes=True))
            c.done(pool.iota(pad_row[:], pattern=[[P, TABLE]], base=TOPK * B * T, channel_multiplier=1,
                             allow_small_or_imprecise_dtypes=True))
            c.done(pool.memset(ones_row[:], 1.0))
            c.done(pool.iota(expert_no[:], pattern=[[1, NE]], base=0, channel_multiplier=0,
                             allow_small_or_imprecise_dtypes=True))
            c.done(pool.iota(expert_row[:], pattern=[[CAP * P, NE]], base=0, channel_multiplier=0,
                             allow_small_or_imprecise_dtypes=True))
            c.done(pool.iota(steps_no[:], pattern=[[1, TABLE]], base=0, channel_multiplier=0,
                             allow_small_or_imprecise_dtypes=True))
            c.done(pool.iota(row_no[:], pattern=[[P, CAP - 1]], base=0, channel_multiplier=0,
                             allow_small_or_imprecise_dtypes=True))
            assert c.n == N_CONST

            pool.wait_ge(S["mod_ps"], 1)
            pool.memset(kt_flat, 0.0).then_inc(S["kt_zero"], 1)
            pool.wait_ge(S["ld_wsd"], 16)
            pool.wait_ge(S["bc_sb"], 2 * B)

            def rsqrt(b, n, r):
                pool.wait_ge(S["ln_veps"], b * 3 + n + 1)
                pool.tensor_tensor(rstd[:, r], veps[:, r], minus_half[:, r], ALU.pow).then_inc(S["ln_rstd"], 1)

            def scatter(j):
                for k in range(TOPK):
                    pool.indirect_dma_start(
                        out=slots, out_offset=bass.IndirectOffsetOnAxis(ap=slot_i[:, k, j:j + 1], axis=0),
                        in_=h_sb[:, j, :], in_offset=None).then_inc(scattered[j], 16)

            def route_batch(b, first=False):
                pool.wait_ge(S["at_veps"], b + 1)
                pool.tensor_tensor(at_rs[:, 1:2], at_rs[:, 0:1], minus_half[:, 0:1], ALU.pow)\
                    .then_inc(S["at_rstd"], 1)
                rsqrt(b, 0, NORMED[0])
                rsqrt(b, 1, NORMED[1])
                if not first:
                    wait_apart(pool, S["slots_ready"], b * GPB)
                    scatter(GROUP)
                    scatter(GROUP + 1)
                    pool.wait_ge(S["y_ps"], b * TPB)
                pool.tensor_tensor(wsd_gated[:], wsd_sb[:], mbc(b, GB), ALU.mult).then_inc(S["wsd_ready"], 1)
                if not first:
                    scatter(GROUP + 2)
                    scatter(GROUP + 3)
                wait_apart(pool, S["slots_ready"], b * GPB + 1)
                scatter(0)
                scatter(1)
                rsqrt(b, 2, NORMED[2])
                scatter(2)
                scatter(3)

            route_batch(0, first=True)
            with pool.Fori(1, B) as b:
                route_batch(b)
            pool.wait_ge(S["slots_ready"], B * GPB)
            for j in range(GROUP, TPB):
                scatter(j)

            pool.wait_ge(S["tables"], 1)
            last4 = pool.value_load(misc[0:1, NE:NE + 1], min_val=MIN_TILES // UNROLL - 1, max_val=MAX_TILES // UNROLL - 1)
            fours = last4 + 1

            def put(t, k):
                wait_apart(pool, S["ex_ysb"], t + 1)
                wait_apart(pool, S["row_ready"], t + 1)
                pool.indirect_dma_start(out=ys, out_offset=bass.IndirectOffsetOnAxis(ap=row_i[:, k:k + 1], axis=0),
                                        in_=y_sb[:, k, :], in_offset=None).then_inc(y_out[k], 16)

            with pool.Fori(0, fours) as u:
                for k in range(UNROLL):
                    put(u * UNROLL + k, k)

            with pool.Fori(0, TILES // UNROLL) as u:
                for k in range(UNROLL):
                    t = u * UNROLL + k
                    wait_apart(pool, S["gated_ready"], t + 1)
                    pool.tensor_tensor(xcols(t), xcols(t), got[:, k, 0, :], ALU.add).then_inc(S["out_ready"], 1)

        @block.scalar
        def _(act):
            copy = lambda o, i: act.activation(o, i, ACT.Copy)
            act.wait_ge(S["ld_cond"], 16)
            act.activation(cond_act[:], cond_in[:], ACT.Silu).then_inc(S["cond_ready"], 1)
            act.wait_ge(S["sc_t"], 1)
            copy(cond_t[:].rearrange("p c b -> p (c b)"), bank[0][:, 0:C * B]).then_inc(S["ct_ready"], 1)
            for n in range(2 * B):
                act.wait_ge(S["bc_ps"], n + 1)
                copy(mod_bc[:, n * 2 * D:(n + 1) * 2 * D], bank[4 + n % 2][:]).then_inc(S["bc_sb"], 1)
            act.wait_ge(S["sm_gaps"], 1)
            copy(sm_ga[:], bank[6][0:NB, 0:D]).then_inc(S["sm_gar"], 1)
            act.wait_ge(S["sm_sub"], 1)
            act.activation(sm_p[:], sm_p[:], ACT.Exp, scale=SCALE).then_inc(S["sm_exp"], 1)
            act.wait_ge(S["sm_ptp"], 1)
            copy(sm_pt[:].rearrange("p b n -> p (b n)"), bank[5][0:H * SINKS, 0:B * NB]).then_inc(S["sm_ptr"], 1)
            act.wait_ge(S["sm_otp"], 1)
            copy(sm_ot[:].rearrange("p c n -> p (c n)"), bank[7][:, 0:C * NB]).then_inc(S["sm_otr"], 1)
            act.wait_ge(S["const"], N_CONST)

            def tanh(b, j):
                act.wait_ge(S["gu_ps"], b * TPB + j)
                act.activation(sg[:, (j - 1) % UNROLL, :], bank[1][:, NE:NE + M], ACT.Tanh, scale=0.5)\
                    .then_inc(S["tanh_ready"], 1)

            def act_copy(b, j):
                act.wait_ge(S["aps_ready"], b * TPB + j - 1)
                copy(act_t[:, (j - 2) % UNROLL, :], bank[2][:, 0:P]).then_inc(S["act_t_sb"], 1)

            def h_copy(b, j):
                act.wait_ge(S["tr_ps"], b * TPB + j + 1)
                copy(ht[:, j % UNROLL, :, :].rearrange("p c n -> p (c n)"), bank[0][:, 0:D]).then_inc(S["tr_sb"], 1)

            def at_exp(b, g):
                act.wait_ge(S["at_sub"], b * (HG + 1) + g + 1)
                p = p_win[:, 4 * g:4 * g + 4, :] if g < HG else p_sink[:]
                act.activation(p, p, ACT.Exp, scale=SCALE).then_inc(S["at_exp"], 1)

            def at_probs(b, g):
                act.wait_ge(S["at_pt"], b * (HG + 1) + g + 1)
                if g < HG:
                    copy(pt_win[:, 4 * g:4 * g + 4, :].rearrange("p h n -> p (h n)"), bank[PT_BANK[g]][:])\
                        .then_inc(S["at_pts"], 1)
                else:
                    copy(pt_sink[:], bank[PT_BANK[g]][0:H * SINKS, 0:P]).then_inc(S["at_pts"], 1)

            def batch(b, first=False):
                if not first:
                    tanh(b, 0)
                    act_copy(b, 0)
                h_copy(b, 0)
                tanh(b, 1)
                act.wait_ge(S["at_q"], b + 1)
                copy(qt[:].rearrange("p g n -> p (g n)"), bank[4][:]).then_inc(S["at_qs"], 1)
                act.wait_ge(S["at_k"], b + 1)
                for i in (2, 3):
                    r = slice(32 * i, 32 * i + 32)
                    copy(kt_bd[r, :, i, :], bank[5][r, :].rearrange("p (g n) -> p g n", g=HG)).then_inc(S["at_kas"], 1)
                if not first:
                    act_copy(b, 1)
                act.wait_ge(S["at_v"], b + 1)
                copy(v_aug[:, :, 0:DH], bank[6][:, 0:D].rearrange("p (h s) -> p h s", s=DH)).then_inc(S["at_vs"], 1)
                h_copy(b, 1)
                tanh(b, 2)
                act_copy(b, 2)
                h_copy(b, 2)
                at_exp(b, 0)
                tanh(b, 3)
                at_probs(b, 0)
                act_copy(b, 3)
                at_exp(b, 1)
                h_copy(b, 3)
                at_exp(b, 2)
                tanh(b, 4)
                at_probs(b, 1)
                act_copy(b, 4)
                h_copy(b, 4)
                at_exp(b, 3)
                at_exp(b, 4)
                at_probs(b, 2)
                tanh(b, 5)
                at_probs(b, 3)
                at_probs(b, 4)
                act_copy(b, 5)
                h_copy(b, 5)
                tanh(b, 6)
                act.wait_ge(S["at_ot"], b + 1)
                copy(o_t[:].rearrange("p c n -> p (c n)"), bank[6][:, 0:D]).then_inc(S["at_ots"], 1)
                act_copy(b, 6)
                h_copy(b, 6)
                tanh(b, 7)
                act_copy(b, 7)
                h_copy(b, 7)

            batch(0, first=True)
            with act.Fori(1, B) as b:
                batch(b)
            tanh(B, 0)
            act_copy(B, 0)
            act_copy(B, 1)

            act.wait_ge(S["tables"], 1)
            act.activation(e_neg[:], val_all[:].rearrange("p k t -> p (k t)"), ACT.Exp, scale=-1.0)\
                .then_inc(S["e_ready"], 1)
            last4 = act.value_load(misc[0:1, NE:NE + 1], min_val=MIN_TILES // UNROLL - 1, max_val=MAX_TILES // UNROLL - 1)
            fours = last4 + 1

            def ex_h(t, k):
                act.wait_ge(S["ex_tr"], t + 1)
                copy(ht[:, k, :, :].rearrange("p c n -> p (c n)"), bank[k % 2][:, 0:D]).then_inc(S["ex_ht"], 1)

            def ex_silu(t, k):
                act.wait_ge(S["ex_gu"], t + 1)
                act.activation(sg[:, k, :], bank[2 + k % 2][:, 0:M], ACT.Silu).then_inc(S["ex_silu"], 1)

            ex_h(0, 0)
            with act.Fori(0, fours) as u:
                for k in range(UNROLL):
                    t = u * UNROLL + k
                    ex_h(t + 1, (k + 1) % UNROLL)
                    ex_silu(t, k)

            with act.Fori(0, TILES // UNROLL) as u:
                for k in range(UNROLL):
                    t = u * UNROLL + k
                    wait_apart(act, got_in[k], u * 16 + 16)
                    act.activation(got[:, k, 0, :], got[:, k, 0, :], ACT.Copy, scale=w_tok[:, ds(t, 1)])\
                        .then_inc(S["part_ready"], 1)

        @block.tensor
        def _(pe):
            mm = nc.tensor.matmul

            def transpose(o, i):
                n = i.shape[0]
                return nc.tensor.transpose(o, i, ident[0:n, 0:n])

            pe.wait_ge(S["eye"], 3)
            pe.wait_ge(S["cond_ready"], 1)
            for k in range(C):
                last = transpose(bank[0][:, k * B:(k + 1) * B], cond_act[:, k * P:(k + 1) * P])
            last.then_inc(S["sc_t"], 1)
            pe.wait_ge(S["ld_gate"], 16)
            for k in range(C):
                last = transpose(bank[1][:, k * NE:(k + 1) * NE], gate_in[:, k * P:(k + 1) * P])
            last.then_inc(S["gate_t"], 1)
            pe.wait_ge(S["ct_ready"], 1)
            pe.wait_ge(S["ld_wmod"], 16)
            for s in range(2 * C):
                for k in range(C):
                    last = mm(bank[2][:, s * B:(s + 1) * B], wmod_sb[:, k, s * P:(s + 1) * P], cond_t[:, k, :],
                              start=(k == 0), stop=(k == C - 1))
            last.then_inc(S["col_ps"], 1)
            for n in range(3):
                for k in range(C):
                    last = mm(bank[4 + n][0:B, :], cond_t[:, k, :], wmod_sb[:, k, n * 2 * D:(n + 1) * 2 * D],
                              start=(k == 0), stop=(k == C - 1))
            last.then_inc(S["mod_ps"], 1)
            pe.wait_ge(S["sm_xnr"], 1)
            for k in range(C):
                last = transpose(bank[0][:, k * 2 * NB:(k + 1) * 2 * NB], sm_xn[:, k * P:(k + 1) * P])
            last.then_inc(S["sm_t"], 1)
            pe.wait_ge(S["sm_hr"], C * B)
            pe.wait_ge(S["wq_ready"], C)
            pe.wait_ge(S["wk_ready"], C)
            pe.wait_ge(S["gate_chain"], 1)
            for n, w in enumerate((wk_pad, wq_pad)):
                for g in range(HG):
                    o = (n * HG + g) * NB
                    for k in range(C):
                        last = mm(bank[1][:, o:o + NB], w[:, k, g * P:(g + 1) * P],
                                  sm_h[:, k, n, :, :].rearrange("p b i -> p (b i)"), start=(k == 0),
                                  stop=(k == C - 1))
            last.then_inc(S["sm_proj"], 1)
            pe.wait_ge(S["ld_wv"], 16)
            pe.wait_ge(S["sm_hr"], C * B + C)
            for b in range(B):
                for k in range(C):
                    last = mm(bank[2 + b // 2][0:H * SINKS, (b % 2) * D:(b % 2 + 1) * D],
                              sm_hrep[:, (k * B + b) * H * SINKS:(k * B + b + 1) * H * SINKS], wv_sb[:, k, :],
                              start=(k == 0), stop=(k == C - 1))
            last.then_inc(S["sm_vps"], 1)
            pe.wait_ge(S["mod_ready"], 1)
            pe.wait_ge(S["const"], N_CONST)
            for n in range(2 * B):
                if n >= 2:
                    pe.wait_ge(S["bc_sb"], n - 1)
                mm(bank[4 + n % 2][:], pick[:, n // 2, :], mod[:, (2 + 2 * (n % 2)) * D:(4 + 2 * (n % 2)) * D],
                   start=True, stop=True).then_inc(S["bc_ps"], 1)
            mm(bank[6][0:NB, 0:D], pick_rows[:], mod[:, 2 * D:3 * D], start=True, stop=True)\
                .then_inc(S["sm_gaps"], 1)
            pe.wait_ge(S["bc_sb"], 2 * B)
            pe.wait_ge(S["sm_kqr"], 1 + HG)
            logits = bank[4][0:NB, 0:B * H * SINKS].rearrange("q (b h k) -> q b h k", b=B, h=H)
            mm(bank[4][0:NB, 0:B * H * SINKS], ident_b[0:NB, 0:NB], small_mask_b[:], start=True, stop=False,
               skip_group_check=True)
            for g in range(HG):
                last = mm(logits.rearrange("q b (i g) k -> q g i b k", g=HG)[:, g], sm_q_t[:, g, :],
                          sink_kt[:, g, :, :].rearrange("p i (b k) -> p i b k", b=B), start=False,
                          stop=(g == HG - 1), skip_group_check=True)
            last.then_inc(S["sm_log"], 1)
            pe.wait_ge(S["sm_exp"], 1)
            for b in range(B):
                last = transpose(bank[5][0:H * SINKS, b * NB:(b + 1) * NB], sm_p[:, b, :, :].rearrange("q h k -> q (h k)"))
            last.then_inc(S["sm_ptp"], 1)
            pe.wait_ge(S["sm_ptr"], 1)
            pe.wait_ge(S["sm_vr"], B + 1)
            pe.wait_ge(S["sm_gar"], 1)
            for b in range(B):
                last = mm(bank[6][0:NB, 0:H * DA], sm_pt[:, b, :], sink_v[:, b * H * DA:(b + 1) * H * DA],
                          start=(b == 0), stop=(b == B - 1))
            last.then_inc(S["sm_ops"], 1)
            pe.wait_ge(S["sm_or"], 1)
            for k in range(C):
                last = transpose(bank[7][:, k * NB:(k + 1) * NB],
                                 sm_o[:].rearrange("q h s -> q (h s)")[:, k * P:(k + 1) * P])
            last.then_inc(S["sm_otp"], 1)
            pe.wait_ge(S["sm_otr"], 1)
            pe.wait_ge(S["ld_wo"], 16)
            for k in range(C):
                last = mm(bank[7][0:NB, 0:D], sm_ot[:, k, :], wo_sb[:, k, :], start=(k == 0), stop=(k == C - 1))
            last.then_inc(S["sm_out"], 1)

            pe.wait_ge(S["ld_ws"], 32)
            def at_tr(b):
                pe.wait_ge(S["at_xn"], b + 1)
                for k in range(C):
                    last = transpose(bank[7][:, k * P:(k + 1) * P], at_xn_sb[:, k * P:(k + 1) * P])
                last.then_inc(S["at_xnt"], 1)

            def at_qkv(b):
                pe.wait_ge(S["at_h"], b * C + C)
                for w, o, s in ((wq_pad, bank[4], "at_q"), (wk_pad, bank[5], "at_k")):
                    for g in range(HG):
                        for k in range(C):
                            last = mm(o[:, g * P:(g + 1) * P], w[:, k, g * P:(g + 1) * P], at_ht[:, k, :],
                                      start=(k == 0), stop=(k == C - 1))
                    last.then_inc(S[s], 1)
                for k in range(C):
                    last = mm(bank[6][:, 0:D], at_ht[:, k, :], wv_sb[:, k, :], start=(k == 0), stop=(k == C - 1))
                last.then_inc(S["at_v"], 1)

            def at_sinks(b):
                pe.wait_ge(S["at_qs"], b + 1)
                for g in range(HG):
                    last = mm(bank[7][:, g * 4 * SINKS:(g + 1) * 4 * SINKS], qt[:, g, :],
                              sink_kt[:, g, :, ds(b * SINKS, SINKS)], start=True, stop=True)
                last.then_inc(S["at_log"], 1)

            def at_logits(b, g):
                o = bank[4 + g % 2][:]
                if g >= 2:
                    pe.wait_ge(S["at_sub"], b * (HG + 1) + g - 1)
                mm(o, ident_b[:], causal_b[:].unsqueeze(1).to_broadcast([P, 4, P]), start=True, stop=False,
                   skip_group_check=True)
                mm(o, qt[:, g, :], kt_bd[:, g, :, :].rearrange("p i n -> p (i n)"), start=False, stop=True,
                   skip_group_check=True).then_inc(S["at_log"], 1)

            def at_probs_t(b, g):
                (wait_apart if g == HG else type(pe).wait_ge)(pe, S["at_exp"], b * (HG + 1) + g + 1)
                if g in (1, 3):
                    pe.wait_ge(S["at_pts"], b * (HG + 1) + (g + 1) // 2)
                if g == HG:
                    transpose(bank[PT_BANK[g]][0:H * SINKS, 0:P], p_sink[:].rearrange("q h k -> q (h k)"))\
                        .then_inc(S["at_pt"], 1)
                    return
                for i in range(4):
                    last = transpose(bank[PT_BANK[g]][:, i * P:(i + 1) * P], p_win[:, 4 * g + i, :])
                last.then_inc(S["at_pt"], 1)

            def at_values(b):
                wait_apart(pe, S["at_pts"], b * (HG + 1) + HG + 1)
                mm(bank[7][:, 0:H * DA], pt_sink[:], sink_v[:, ds(b * (H * DA), H * DA)], start=True, stop=False,
                   skip_group_check=True)
                for n in range(H):
                    h = 4 * (n % 4) + n // 4
                    last = mm(bank[7][:, h * DA:(h + 1) * DA], pt_win[:, n, :], v_aug[:, h, :], start=False,
                              stop=(n == H - 1), skip_group_check=True)
                last.then_inc(S["at_o"], 1)

            def at_out_t(b):
                pe.wait_ge(S["at_on"], b + 1)
                for k in range(C):
                    last = transpose(bank[6][:, k * P:(k + 1) * P],
                                     o_n[:].rearrange("q h s -> q (h s)")[:, k * P:(k + 1) * P])
                last.then_inc(S["at_ot"], 1)

            def at_project(b):
                pe.wait_ge(S["at_ots"], b + 1)
                for k in range(C):
                    last = mm(bank[5][:, 0:D], o_t[:, k, :], wo_sb[:, k, :], start=(k == 0), stop=(k == C - 1))
                last.then_inc(S["at_out"], 1)

            def tr(b, j):
                pe.wait_ge(S["h_ready"], b * TPB + j + 1)
                for k in range(C):
                    last = transpose(bank[0][:, k * P:(k + 1) * P], h_sb[:, j, k * P:(k + 1) * P])
                last.then_inc(S["tr_ps"], 1)

            def gate_up(b, j, first=False):
                pe.wait_ge(S["tr_sb"], b * TPB + j)
                if not first or j >= 2:
                    pe.wait_ge(S["act_ready"], b * TPB + j - 1)
                    pe.wait_ge(S["lg_ready"], b * TPB + j - 1)
                for k in range(C):
                    last = mm(bank[1][:, 0:NR], ht[:, (j - 1) % UNROLL, k, :], w_route[:, k, :],
                              start=(k == 0), stop=(k == C - 1))
                last.then_inc(S["gu_ps"], 1)

            def act_tr(b, j, first=False):
                pe.wait_ge(S["act_ready"], b * TPB + j - 1)
                if not first or j >= 3:
                    pe.wait_ge(S["act_t_sb"], b * TPB + j - 2)
                transpose(bank[2][:, 0:P], act_sb[:, (j - 2) % UNROLL, :]).then_inc(S["aps_ready"], 1)

            def down(b, j, first=False):
                pe.wait_ge(S["act_t_sb"], b * TPB + j - 2)
                if j == 3:
                    pe.wait_ge(S["wsd_ready"], b + 1)
                if not first or j >= 4:
                    pe.wait_ge(S["y_added"], b * TPB + j - 3)
                if j == 2 or j == GROUP + 2:
                    pe.wait_ge(S["rank_read"], b * GPB + j // GROUP)
                mm(bank[3][:, 0:D], act_t[:, (j - 3) % UNROLL, :], wsd_gated[:], start=True, stop=True)\
                    .then_inc(S["y_ps"], 1)

            def rank(b, j):
                g = 1 if j == 1 else 0
                pe.wait_ge(S["masks"], b * GPB + 1 - g)
                pe.wait_ge(S["y_added"], b * TPB + j - 3)
                o = bank[3][:, D:D + GROUP * NE]
                mm(o, ones_b[:], counted_b[:, g, :].unsqueeze(1).to_broadcast([P, GROUP, NE]), start=True,
                   stop=False, skip_group_check=True)
                last = mm(o, before_b[:], mask_b[:].rearrange("p t e -> p (t e)"), start=False, stop=False,
                          skip_group_check=True)
                for i in range(GROUP - 1):
                    last = mm(bank[3][:, D + (i + 1) * NE:D + GROUP * NE], ones_b[:],
                              mask_b[:, i:i + 1, :].to_broadcast([P, GROUP - 1 - i, NE]), start=False,
                              stop=(i == GROUP - 2), skip_group_check=True)
                last.then_inc(S["rank_ps"], 1)

            def batch(b, first=False):
                for j in range(TPB):
                    before = not first
                    if before or j >= 1:
                        gate_up(b, j, first)
                    if j == 1:
                        at_qkv(b)
                    elif j == 2:
                        at_sinks(b)
                        pe.wait_ge(S["at_ks"], b * 2 + 2)
                        pe.wait_ge(S["at_kas"], b * 2 + 2)
                        at_logits(b, 0)
                        at_logits(b, 1)
                    elif j == 3:
                        at_logits(b, 2)
                        pe.wait_ge(S["at_vs"], b + 1)
                        at_probs_t(b, 0)
                    elif j == 4:
                        at_logits(b, 3)
                        at_probs_t(b, 1)
                    elif j == 5:
                        at_probs_t(b, 3)
                        at_probs_t(b, 4)
                    elif j == 6:
                        at_out_t(b)
                    if before or j >= 2:
                        act_tr(b, j, first)
                    if (before and j == 1) or j == GROUP + 1:
                        rank(b, j)
                    if j == 6:
                        at_project(b)
                    late = j in (0, TPB - 1)
                    if late and (before or j >= 3):
                        down(b, j, first)
                    if j == 0:
                        at_tr(b)
                    tr(b, j)
                    if not late and (before or j >= 3):
                        down(b, j, first)
                    if j == 4:
                        at_probs_t(b, 2)
                    elif j == 5:
                        at_values(b)

            batch(0, first=True)
            with pe.Fori(1, B) as b:
                batch(b)
            gate_up(B, 0)
            act_tr(B, 0)
            down(B, 0)
            act_tr(B, 1)
            rank(B, 1)
            down(B, 1)
            down(B, 2)

            pe.wait_ge(S["rank_read"], B * GPB)
            pe.wait_ge(S["rt_ch"], RT_CH * GPB * B)
            mm(bank[0][:, 0:NE], ones_b[:], counted_b[:, 0, :], start=True, stop=True).then_inc(S["cnt_ps"], 1)

            pe.wait_ge(S["tables"], 1)
            pe.wait_ge(S["ld_exp"], 16 * (2 * C + 1))
            last4 = pe.value_load(misc[0:1, NE:NE + 1], min_val=MIN_TILES // UNROLL - 1, max_val=MAX_TILES // UNROLL - 1)
            fours = last4 + 1

            def which(t):
                return pe.value_load(tab[0:1, ds(t, 1)], min_val=0, max_val=NE - 1)

            def ex_tr(t, k, first=False):
                pe.wait_ge(xt_in[k], (t - k) * 4 + 16 if first is False else 16)
                if not first:
                    pe.wait_ge(S["ex_ht"], t - 1)
                for c in range(C):
                    last = transpose(bank[k % 2][:, c * P:(c + 1) * P], xt[:, k, c * P:(c + 1) * P])
                last.then_inc(S["ex_tr"], 1)

            def ex_gu(t, k, first=False):
                e = which(t)
                pe.wait_ge(S["ex_ht"], t + 1)
                if not first:
                    pe.wait_ge(S["ex_act"], t - 1)
                for c in range(C):
                    last = mm(bank[2 + k % 2][:, 0:2 * M], ht[:, k, c, :],
                              w_gu[:, ds(e * (C * 2 * M) + c * 2 * M, 2 * M)], start=(c == 0), stop=(c == C - 1))
                last.then_inc(S["ex_gu"], 1)

            def ex_at(t, k, first=False):
                pe.wait_ge(S["ex_act"], t + 1)
                if not first:
                    pe.wait_ge(S["ex_at"], t - 1)
                transpose(bank[4 + k % 2][:, 0:P], act_sb[:, k, :]).then_inc(S["ex_ap"], 1)

            def ex_dn(t, k, first=False):
                e = which(t)
                pe.wait_ge(S["ex_at"], t + 1)
                if not first:
                    pe.wait_ge(S["ex_ysb"], t - 1)
                mm(bank[6 + k % 2][:, 0:D], act_t[:, k, :], w_dn[:, ds(e * D, D)], start=True, stop=True)\
                    .then_inc(S["ex_y"], 1)

            ex_tr(0, 0, True)
            ex_tr(1, 1, True)
            ex_gu(0, 0, True)
            ex_tr(2, 2)
            ex_gu(1, 1, True)
            ex_at(0, 0, True)
            for t in (2, 3):
                ex_tr(t + 1, (t + 1) % UNROLL)
                ex_gu(t, t)
                ex_at(t - 1, t - 1, t == 2)
                ex_dn(t - 2, t - 2, True)
            with pe.Fori(1, fours) as u:
                for k in range(UNROLL):
                    t = u * UNROLL + k
                    ex_tr(t + 1, (k + 1) % UNROLL)
                    ex_gu(t, k)
                    ex_at(t - 1, (k - 1) % UNROLL)
                    ex_dn(t - 2, (k - 2) % UNROLL)
            ex_at(last4 * UNROLL + UNROLL - 1, UNROLL - 1)
            ex_dn(last4 * UNROLL + UNROLL - 2, UNROLL - 2)
            ex_dn(last4 * UNROLL + UNROLL - 1, UNROLL - 1)

        @block.vector
        def _(dve):
            v = nc.vector
            dve.wait_ge(S["ld_small"], 32 * B)
            ch = Chain(dve, S["sm_chain"])
            ch.done(v.bn_stats(sm_stats[:], sm_in))
            ch.done(v.bn_aggr(sm_mv[:], sm_stats[:]))
            v.tensor_scalar(sm_rstd[:, 0:1], sm_mv[:, 1:2], EPS, None, ALU.add).then_inc(S["sm_veps"], 1)
            dve.wait_ge(S["sm_rs"], 1)
            v.tensor_scalar(sm_xn, sm_in, sm_mv[:, 0:1], sm_rstd[:, 1:2], ALU.subtract, ALU.mult)\
                .then_inc(S["sm_xnr"], 1)
            dve.wait_ge(S["gate_t"], 1)
            v.tensor_copy(w_route[:, :, 0:NE], bank[1][:, 0:C * NE].rearrange("p (c e) -> p c e", c=C))\
                .then_inc(S["gate_chain"], 1)
            dve.wait_ge(S["col_ps"], 1)
            v.tensor_copy(mod_col[:, 0:C * B], bank[2][:, 0:C * B]).then_inc(S["col_ready"], 1)
            v.tensor_scalar(mod_col[:, C * B:2 * C * B], bank[2][:, C * B:2 * C * B], 1.0, None, ALU.add)\
                .then_inc(S["col_ready"], 1)
            dve.wait_ge(S["col_ready"], 2)
            dve.wait_ge(S["sm_t"], 1)
            for k in range(C):
                view = bank[0][:, k * 2 * NB:(k + 1) * 2 * NB].rearrange("p (n b i) -> p n b i", n=2, b=B)
                for b in range(B):
                    v.tensor_scalar(sm_h[:, k, :, b, :], view[:, :, b, :],
                                    mod_col[:, (C + k) * B + b:(C + k) * B + b + 1],
                                    mod_col[:, k * B + b:k * B + b + 1], ALU.mult, ALU.add).then_inc(S["sm_hr"], 1)
            dve.wait_ge(S["sm_hr"], C * B)
            for k in range(C):
                rep = sm_hrep[:, k * B * H * SINKS:(k + 1) * B * H * SINKS]
                v.tensor_copy(rep.rearrange("p (b h i) -> p b h i", b=B, h=H),
                              sm_h[:, k, 0, :, :].unsqueeze(2).to_broadcast([P, B, H, SINKS]))\
                    .then_inc(S["sm_hr"], 1)
            dve.wait_ge(S["mod_ps"], 1)
            for n in range(3):
                v.tensor_copy(mod[:, n * 2 * D:(n + 1) * 2 * D], bank[4 + n][0:B, :]).then_inc(S["mod_rows"], 1)
            dve.wait_ge(S["mod_rows"], 3)
            g = Chain(dve, S["mod_rows"], at=3)
            gates = mod.rearrange("b (s d) -> b s d", d=D)[:, 2::3, :]
            g.done(v.scalar_tensor_tensor(gabs, gates, -1.0, gates, ALU.mult, ALU.max))
            g.done(v.tensor_scalar(gsign, gates, 0.0, 2.0, ALU.is_ge, ALU.mult))
            g.done(v.tensor_scalar(gabs, gabs, 0.25, None, ALU.max))
            g.done(v.scalar_tensor_tensor(gates, gsign, -1.0, gabs, ALU.add, ALU.mult))
            v.tensor_scalar(mod[:, 4 * D:5 * D], mod[:, 4 * D:5 * D], 1.0, None, ALU.add)\
                .then_inc(S["mod_ready"], 1)
            dve.wait_ge(S["sm_proj"], 1)
            dve.wait_ge(S["const"], N_CONST)
            v.tensor_copy(sm_q_t[:].rearrange("p g q -> p (g q)"), bank[1][:, HG * NB:2 * HG * NB])\
                .then_inc(S["sm_kqr"], 1)
            for g in range(HG):
                v.tensor_tensor(sink_kt[:, g, :, :],
                                bank[1][:, g * NB:(g + 1) * NB].unsqueeze(1).to_broadcast([P, 4, NB]),
                                quarter[:].unsqueeze(2).to_broadcast([P, 4, NB]), ALU.mult)\
                    .then_inc(S["sm_kqr"], 1)
            dve.wait_ge(S["sm_vps"], 1)
            dve.wait_ge(S["const"], N_CONST)
            sv = sink_v[:].rearrange("p (b h s) -> p b h s", b=B, h=H)
            for b in range(B):
                src = bank[2 + b // 2][0:H * SINKS, (b % 2) * D:(b % 2 + 1) * D]
                v.tensor_tensor(sv[:, b, :, 0:DH], src.rearrange("p (h s) -> p h s", h=H),
                                head_block[:].unsqueeze(2).to_broadcast([H * SINKS, H, DH]), ALU.mult)\
                    .then_inc(S["sm_vr"], 1)
            v.tensor_copy(sv[:, :, :, DH], head_block[:].unsqueeze(1).to_broadcast([H * SINKS, B, H]))\
                .then_inc(S["sm_vr"], 1)
            dve.wait_ge(S["sm_log"], 1)
            lg = bank[4][0:NB, 0:B * H * SINKS].rearrange("q (b h k) -> q b h k", b=B, h=H)
            ch.done(v.tensor_reduce(sm_m[:], lg.rearrange("q b h k -> q h b k"), AX.XY, ALU.max))
            for b in range(B):
                last = v.tensor_tensor(sm_p[:, b, :, :], lg[:, b, :, :],
                                       sm_m[:].unsqueeze(2).to_broadcast([NB, H, SINKS]), ALU.subtract)
                if b < B - 1:
                    ch.done(last)
            last.then_inc(S["sm_sub"], 1)
            dve.wait_ge(S["sm_ops"], 1)
            so = bank[6][0:NB, 0:H * DA].rearrange("q (h s) -> q h s", h=H)
            ch.done(v.reciprocal(sm_r[:], so[:, :, DH]))
            v.tensor_tensor(sm_o[:], so[:, :, 0:DH], sm_r[:].unsqueeze(2).to_broadcast([NB, H, DH]), ALU.mult)\
                .then_inc(S["sm_or"], 1)
            dve.wait_ge(S["sm_out"], 1)
            dve.wait_ge(S["sm_gar"], 1)
            dve.wait_ge(S["ld_smallq"], 16 * B)
            ch.done(v.tensor_tensor(sm_x1, bank[7][0:NB, 0:D], sm_ga[:], ALU.mult))
            v.tensor_tensor(sm_x1, sm_x1, sm_q, ALU.add).then_inc(S["sm_done"], 1)
            dve.wait_ge(S["bc_sb"], 2 * B)
            dve.wait_ge(S["ld_wsd"], 16)
            for b in range(B):
                dve.wait_ge(ld_x[b], 16)
            dve.wait_ge(S["x_small"], 16 * B)

            ls = bank[7][:, 0:H * SINKS].rearrange("q (n k) -> q n k", n=H)
            lws = [bank[4 + g % 2][:].rearrange("q (h k) -> q h k", h=4) for g in range(HG)]

            def at_norm(b, at):
                at.done(v.bn_stats(at_stats[:], xcols(b * TPB + TPB - 1)), alone=True)
                at.done(v.bn_aggr(at_mv[:], at_stats[:]))
                v.tensor_scalar(at_rs[:, 0:1], at_mv[:, 1:2], EPS, None, ALU.add).then_inc(S["at_veps"], 1)

            def at_xn(b):
                dve.wait_ge(S["at_rstd"], b + 1)
                v.tensor_scalar(at_xn_sb[:], xcols(b * TPB + TPB - 1), at_mv[:, 0:1], at_rs[:, 1:2], ALU.subtract,
                                ALU.mult).then_inc(S["at_xn"], 1)

            def at_modulate(b):
                dve.wait_ge(S["at_xnt"], b + 1)
                for k in range(C):
                    v.tensor_scalar(at_ht[:, k, :], bank[7][:, k * P:(k + 1) * P],
                                    mod_col[:, ds(b + (C + k) * B, 1)], mod_col[:, ds(b + k * B, 1)],
                                    ALU.mult, ALU.add).then_inc(S["at_h"], 1)

            def at_keys(b):
                dve.wait_ge(S["kt_zero"], 1)
                dve.wait_ge(S["at_k"], b + 1)
                for i in (0, 1):
                    r = slice(32 * i, 32 * i + 32)
                    v.tensor_copy(kt_bd[r, :, i, :], bank[5][r, :].rearrange("p (g n) -> p g n", g=HG))\
                        .then_inc(S["at_ks"], 1)

            def at_sink_max(b, at):
                dve.wait_ge(S["at_log"], b * (HG + 1) + 1)
                at.done(v.tensor_reduce(m_sink[:], ls, AX.X, ALU.max))

            def at_less_max(b, g, at):
                dve.wait_ge(S["at_log"], b * (HG + 1) + g + 2)
                hs = slice(4 * g, 4 * g + 4)
                at.done(v.tensor_reduce(m_win[:, hs], lws[g], AX.X, ALU.max))
                at.done(v.tensor_tensor(m_all[:, hs], m_win[:, hs], m_sink[:, hs], ALU.max))
                v.tensor_tensor(p_win[:, hs, :], lws[g], m_all[:, hs].unsqueeze(2).to_broadcast([P, 4, P]),
                                ALU.subtract).then_inc(S["at_sub"], 1)

            def at_sinks_less_max(b):
                v.tensor_tensor(p_sink[:].rearrange("q (i g) k -> q g i k", g=HG),
                                bank[7][:, 0:H * SINKS].rearrange("q (g i k) -> q g i k", g=HG, i=4),
                                m_all[:].rearrange("q (g i) -> q g i", g=HG).unsqueeze(3)
                                .to_broadcast([P, HG, 4, SINKS]), ALU.subtract).then_inc(S["at_sub"], 1)

            def at_normalise(b, at):
                dve.wait_ge(S["at_o"], b + 1)
                ob = bank[7][:, 0:H * DA].rearrange("q (h s) -> q h s", h=H)
                at.done(v.reciprocal(rden[:], ob[:, :, DH]))
                v.tensor_tensor(o_n[:], ob[:, :, 0:DH], rden[:].unsqueeze(2).to_broadcast([P, H, DH]), ALU.mult)\
                    .then_inc(S["at_on"], 1)

            def at_add(b, at):
                dve.wait_ge(S["at_out"], b + 1)
                at.done(v.tensor_tensor(o_g[:], bank[5][:, 0:D], mbc(b, GA), ALU.mult))
                tail = xcols(b * TPB + TPB - 1)
                v.tensor_tensor(tail, tail, o_g[:], ALU.add).then_inc(S["at_x"], 1)
                assert at.n == AT_CH, at.n

            def norm_stats(b, n, ln):
                r = range(TPB)[NORMED[n]]
                for j in r:
                    v.bn_stats(st[:, j, :], xcols(b * TPB + j)).then_inc(S["ln_ch"], 1)
                    ln.n += 1
                wait_apart(dve, S["ln_ch"], b * (2 * TPB) + ln.n)
                for j in r:
                    v.bn_aggr(mv[:, j, :], st[:, j, :]).then_inc(S["ln_ch"], 1)
                    ln.n += 1
                dve.wait_ge(S["ln_ch"], b * (2 * TPB) + ln.n)
                v.tensor_scalar(veps[:, NORMED[n]], mv[:, NORMED[n], 1], EPS, None, ALU.add)\
                    .then_inc(S["ln_veps"], 1)

            def h_tile(b, j, first):
                dve.wait_ge(S["ln_rstd"], b * 3 + (1 if j < 2 else 2 if j < TPB - 1 else 3))
                v.scalar_tensor_tensor(centred[:, j % 2, :], xcols(b * TPB + j), mv[:, j, 0:1], mbc(b, CB),
                                       ALU.subtract, ALU.mult).then_inc(S["h_cent"], 1)
                if not first:
                    dve.wait_ge(scattered[j], b * (16 * TOPK))
                wait_apart(dve, S["h_cent"], b * TPB + j + 1)
                v.scalar_tensor_tensor(h_sb[:, j, 0:D], centred[:, j % 2, :], rstd[:, j:j + 1], mbc(b, SB_),
                                       ALU.mult, ALU.add).then_inc(S["h_ready"], 1)

            def activation(b, j):
                k = (j - 1) % TPB
                dve.wait_ge(S["tanh_ready"], b * TPB + j)
                v.scalar_tensor_tensor(act_sb[:, k % UNROLL, :], sg[:, k % UNROLL, :], 1.0, bank[1][:, NE + M:NR],
                                       ALU.add, ALU.mult).then_inc(S["act_ch"], 1)
                v.tensor_scalar(logit[:, k, :], bank[1][:, 0:NE], SATURATED, None, ALU.min)\
                    .then_inc(S["lg_ready"], 1)
                wait_apart(dve, S["act_ch"], b * TPB + j)
                v.scalar_tensor_tensor(act_sb[:, k % UNROLL, :], bank[1][:, NE:NE + M], 0.5,
                                       act_sb[:, k % UNROLL, :], ALU.mult, ALU.mult).then_inc(S["act_ready"], 1)
                wait_apart(dve, S["lg_ready"], b * TPB + j)
                v.max(top_v[:, k, :], logit[:, k, :]).then_inc(S["top_ch"], 1)
                wait_apart(dve, S["top_ch"], b * (2 * TPB) + 2 * j - 1)
                v.max_index(top_i[:, k, :], top_v[:, k, :], logit[:, k, :]).then_inc(S["top_ch"], 1)

            def add_y(b, j):
                dve.wait_ge(S["y_ps"], b * TPB + j - 2)
                x = xcols(b * TPB + j - 3)
                v.tensor_tensor(x, x, bank[3][:, 0:D], ALU.add).then_inc(S["y_added"], 1)

            def chosen(b, j):
                first = b * TPB + j - GROUP
                g = 1 if j == 0 else 0
                r = slice(g * GROUP, (g + 1) * GROUP)
                rt = Chain(dve, S["rt_ch"], b, GPB * RT_CH, -g * RT_CH)
                dve.wait_ge(S["top_ch"], b * (2 * TPB) + 2 * j)
                v.tensor_copy(val_all[:, :, ds(first, GROUP)], top_v[:, r, 0:TOPK].rearrange("p t k -> p k t"))\
                    .then_inc(S["rt_ch"], 1)
                rt.n += 1
                rt.done(v.tensor_copy(top_if[:], top_i[:, r, 0:TOPK]))
                for n in range(TOPK):
                    rt.done(v.tensor_tensor(hot[:, n, :, :], expert_no[:].unsqueeze(1).to_broadcast([P, GROUP, NE]),
                                            top_if[:, :, n:n + 1].to_broadcast([P, GROUP, NE]), ALU.is_equal))
                for col, src in ((D, token2[:, ds(first, GROUP)]), (D + 1, top_if[:, :, 0])):
                    v.tensor_copy(h_sb[:, r, col], src).then_inc(S["rt_ch"], 1)
                    rt.n += 1
                v.tensor_tensor(mask_b[:], hot[:, 0, :, :], hot[:, 1, :, :], ALU.add).then_inc(S["masks"], 1)
                dve.wait_ge(S["masks"], b * GPB + 1 - g)
                rt.done(v.tensor_reduce(mask_sum[:], mask_b[:].rearrange("p t e -> p e t"), AX.X, ALU.add))
                return rt

            def placed(b, j, rt):
                g = 1 if j == 1 else 0
                dve.wait_ge(S["rank_ps"], b * GPB + 1 - g)
                wait_apart(dve, S["y_ps"], b * TPB + j - 2)
                v.tensor_tensor(place[:], bank[3][:, D:D + GROUP * NE].rearrange("p (t e) -> p t e", e=NE),
                                expert_row[:].unsqueeze(1).to_broadcast([P, GROUP, NE]), ALU.add)\
                    .then_inc(S["rank_read"], 1)
                rt.done(v.tensor_tensor(counted_b[:, 1 - g, :], counted_b[:, g, :], mask_sum[:], ALU.add))
                dve.wait_ge(S["rank_read"], b * GPB + 1 - g)
                for n in range(TOPK):
                    rt.done(v.tensor_tensor(at_place[:, n, :, :], place[:], hot[:, n, :, :], ALU.mult))
                rt.done(v.tensor_reduce(slot_f[:], at_place[:], AX.X, ALU.add))
                r = slice(g * GROUP, (g + 1) * GROUP)
                v.tensor_copy(slot_i[:, :, r], slot_f[:]).then_inc(S["slots_ready"], 1)

            def batch(b, first=False):
                at = Chain(dve, S["at_ch"], b, AT_CH)
                ln = Chain(dve, S["ln_ch"], b, 2 * TPB)
                at_norm(b, at)
                norm_stats(b, 0, ln)
                at_xn(b)
                h_tile(b, 0, first)
                if not first:
                    activation(b, 0)
                    add_y(b, 0)
                at_modulate(b)
                if not first:
                    rt = chosen(b, 0)
                h_tile(b, 1, first)
                norm_stats(b, 1, ln)
                activation(b, 1)
                at_keys(b)
                if not first:
                    placed(b, 1, rt)
                    add_y(b, 1)
                h_tile(b, 2, first)
                activation(b, 2)
                at_sink_max(b, at)
                at_less_max(b, 0, at)
                if not first:
                    add_y(b, 2)
                h_tile(b, 3, first)
                at_less_max(b, 1, at)
                activation(b, 3)
                at_less_max(b, 2, at)
                add_y(b, 3)
                h_tile(b, 4, first)
                activation(b, 4)
                at_less_max(b, 3, at)
                at_sinks_less_max(b)
                add_y(b, 4)
                rt = chosen(b, 4)
                h_tile(b, 5, first)
                activation(b, 5)
                placed(b, 5, rt)
                add_y(b, 5)
                h_tile(b, 6, first)
                at_normalise(b, at)
                activation(b, 6)
                at_add(b, at)
                add_y(b, 6)
                wait_apart(dve, S["at_x"], b + 1)
                norm_stats(b, 2, ln)
                activation(b, 7)
                h_tile(b, 7, first)
                add_y(b, 7)

            batch(0, first=True)
            with dve.Fori(1, B) as b:
                batch(b)
            activation(B, 0)
            add_y(B, 0)
            rt = chosen(B, 0)
            placed(B, 1, rt)
            add_y(B, 1)
            add_y(B, 2)

            dve.wait_ge(S["cnt_ps"], 1)
            dve.wait_ge(S["slots_ready"], B * GPB)
            tb = Chain(dve, S["tb"])
            tb.done(v.tensor_copy(n_e[:], bank[0][:, 0:NE]))
            tb.done(v.tensor_tensor(over[:], n_e[:].unsqueeze(2).to_broadcast([P, NE, CAP - 1]),
                                    row_no[:].unsqueeze(1).to_broadcast([P, NE, CAP - 1]), ALU.is_gt))
            tb.done(v.tensor_reduce(nt_e[:], over[:], AX.X, ALU.add))
            tb.done(v.tensor_tensor_scan(end_e[:], ones_row[:], nt_e[:], 0.0, ALU.mult, ALU.add))
            tb.done(v.tensor_scalar(jump[:], nt_e[0:1, :], -1.0, float(CAP), ALU.mult, ALU.add))
            tb.done(v.tensor_tensor(past, steps_no[:].unsqueeze(2).to_broadcast([P, TABLE, NE]),
                                    end_e[:].unsqueeze(1).to_broadcast([P, TABLE, NE]), ALU.is_ge))
            tb.done(v.tensor_tensor(past_jump, past[0:1, :, :], jump[:].unsqueeze(1).to_broadcast([1, TABLE, NE]),
                                    ALU.mult))
            tb.done(v.tensor_reduce(tile_e[:], past, AX.X, ALU.add))
            tb.done(v.tensor_reduce(tab_f[:, 1, :], past_jump, AX.X, ALU.add))
            tb.done(v.tensor_scalar(tile_e[:], tile_e[:], float(NE - 1), None, ALU.min))
            tb.done(v.tensor_copy(tab_f[:, 0, :], tile_e[0:1, :]))
            tb.done(v.tensor_tensor(tab_f[:, 1, :], tab_f[:, 1, :], steps_no[0:1, :], ALU.add))
            tb.done(v.tensor_copy(tab[:], tab_f[:].rearrange("p n t -> p (n t)")))
            tb.done(v.tensor_tensor(misc_f[:, 0:NE], n_e[0:1, :], expert_row[0:1, :], ALU.add))
            tb.done(v.tensor_tensor(n_over[:], end_e[0:1, NE - 1:NE].to_broadcast([1, MAX_TILES // UNROLL]),
                                    steps_no[0:1, 0:MAX_TILES:UNROLL], ALU.is_gt))
            tb.done(v.tensor_reduce(misc_f[:, NE:NE + 1], n_over[:], AX.X, ALU.add))
            tb.done(v.tensor_scalar(misc_f[:, NE:NE + 1], misc_f[:, NE:NE + 1], -1.0, None, ALU.add))
            v.tensor_copy(misc[:], misc_f[:]).then_inc(S["tables"], 1)
            dve.wait_ge(S["e_ready"], 1)
            w = Chain(dve, S["w_ch"])
            sc = score[:].rearrange("p k t -> p (k t)")
            w.done(v.tensor_scalar(e_neg[:], e_neg[:], 1.0, None, ALU.add))
            w.done(v.reciprocal(sc, e_neg[:]))
            w.done(v.tensor_tensor(total[:], score[:, 0, :], score[:, 1, :], ALU.add))
            w.done(v.tensor_scalar(total[:], total[:], 1e-20, None, ALU.add))
            w.done(v.reciprocal(total[:], total[:]))
            for n in range(TOPK):
                w.done(v.scalar_tensor_tensor(w_tok[:, n * TILES:(n + 1) * TILES], score[:, n, :], ROUTE_SCALE,
                                              total[:], ALU.mult, ALU.mult))
            dve.wait_ge(S["tables"], 1)
            last4 = dve.value_load(misc[0:1, NE:NE + 1], min_val=MIN_TILES // UNROLL - 1, max_val=MAX_TILES // UNROLL - 1)
            fours = last4 + 1

            def ex_act(t, k):
                dve.wait_ge(S["ex_silu"], t + 1)
                v.tensor_tensor(act_sb[:, k, :], bank[2 + k % 2][:, M:2 * M], sg[:, k, :], ALU.mult)\
                    .then_inc(S["ex_act"], 1)

            def ex_at(t, k):
                dve.wait_ge(S["ex_ap"], t + 1)
                v.tensor_copy(act_t[:, k, :], bank[4 + k % 2][:, 0:P]).then_inc(S["ex_at"], 1)

            def ex_y(t, k):
                dve.wait_ge(S["ex_y"], t + 1)
                v.tensor_copy(y_sb[:, k, :], bank[6 + k % 2][:, 0:D]).then_inc(S["ex_ysb"], 1)

            def rows(t, k, stored):
                dve.wait_ge(xt_in[k], (t - k) * 4 + 16)
                if stored is not None:
                    wait_apart(dve, y_out[k], stored * 16)
                v.scalar_tensor_tensor(row_f[:, k:k + 1], xt[:, k, D + 1:DX], tile_e[:, ds(t, 1)],
                                       xt[:, k, D:D + 1], ALU.not_equal, ALU.add).then_inc(S["row_ch"], 1)
                wait_apart(dve, S["row_ch"], t + 1)
                v.tensor_tensor(row_i[:, k:k + 1], row_f[:, k:k + 1], pad_row[:, ds(t, 1)], ALU.min)\
                    .then_inc(S["row_ready"], 1)

            for t in range(UNROLL):
                rows(t, t, None)
                ex_act(t, t)
                if t >= 1:
                    ex_at(t - 1, t - 1)
                if t >= 2:
                    ex_y(t - 2, t - 2)
            with dve.Fori(1, fours) as u:
                for k in range(UNROLL):
                    t = u * UNROLL + k
                    rows(t, k, u)
                    ex_act(t, k)
                    ex_at(t - 1, (k - 1) % UNROLL)
                    ex_y(t - 2, (k - 2) % UNROLL)
            ex_at(last4 * UNROLL + UNROLL - 1, UNROLL - 1)
            ex_y(last4 * UNROLL + UNROLL - 2, UNROLL - 2)
            ex_y(last4 * UNROLL + UNROLL - 1, UNROLL - 1)

            with dve.Fori(0, B) as b:
                for j in range(TPB):
                    t = b * TPB + j
                    k = j % UNROLL
                    dve.wait_ge(S["part_ready"], t + 1)
                    v.scalar_tensor_tensor(got[:, k, 1, :], got[:, k, 1, :], w_tok[:, ds(t + TILES, 1)],
                                           got[:, k, 0, :], ALU.mult, ALU.add).then_inc(S["both_ready"], 1)
                    dve.wait_ge(S["both_ready"], t + 1)
                    v.tensor_tensor(got[:, k, 0, :], got[:, k, 1, :], mbc(b, GB), ALU.mult)\
                        .then_inc(S["gated_ready"], 1)


N_CONST = 32
AT_CH = 13
RT_CH = 11

_INS = ["L0_attn_x", "L0_attn_Wq", "L0_attn_Wk", "L0_attn_Wv", "L0_attn_Wo", "L0_ffn_gate_w", "L0_ffn_w_gate",
        "L0_ffn_w_up", "L0_ffn_w_down", "L0_ffn_ws_gate", "L0_ffn_ws_up", "L0_ffn_ws_down", "L0_c", "L0_wmod"]
_OUTS = [((4, 1024, 256), "float32")]


def kernel(**inputs):
    import numpy as _np
    import concourse.bacc as _bacc
    from concourse import mybir as _mybir
    from concourse.bass_utils import run_bass_kernel_spmd as _run

    nc = _bacc.Bacc("TRN2", target_bir_lowering=False, num_devices=1)
    arrays, args = {}, []
    for name in _INS:
        a = _np.ascontiguousarray(inputs[name])
        arrays[f"in_{name}_dram"] = a
        args.append(nc.dram_tensor(f"in_{name}_dram", a.shape, _mybir.dt.from_np(a.dtype), kind="ExternalInput").ap())
    for i, (shape, dtype) in enumerate(_OUTS):
        dt = _mybir.dt.from_np(_np.dtype(dtype))
        args.append(nc.dram_tensor(f"out_{i}_dram", shape, dt, kind="ExternalOutput").ap())
    bass_adaln_attention_moe(nc, *args)
    r = _run(nc, [arrays], core_ids=[0])
    got = tuple(r.results[0][f"out_{i}_dram"] for i in range(len(_OUTS)))
    return got[0]
```

```python
from contextlib import ExitStack

import concourse.bass as bass
from concourse import mybir

ALU = mybir.AluOpType
ACT = mybir.ActivationFunctionType
AX = mybir.AxisListType
F32 = mybir.dt.float32
BF16 = mybir.dt.bfloat16
I32 = mybir.dt.int32
U32 = mybir.dt.uint32
ds = bass.ds
SP, PE = mybir.EngineType.SP, mybir.EngineType.PE

P = 128
MASKED = -1e30
EPS = 1e-5
SATURATED = 16.6355
UNROLL = 4
SPARE = 2 * UNROLL


def bass_adaln_attention_moe(nc, x, wq, wk, wv, wo, gate_w, w_gate, w_up, w_down, ws_gate, ws_up,
                             ws_down, cond, w_mod, out):
    B, T, D = x.shape
    NE, _, M = w_gate.shape
    H, SINKS, WINDOW = 16, 4, 128
    DH = D // H
    SCALE = DH ** -0.5
    TOPK, ROUTE_SCALE = 2, 2.5
    C = D // P
    HG = H * 32 // P
    TPB = T // P
    TILES = B * TPB
    GROUP = 4
    GPB = TPB // GROUP
    CAP = B * T // P + 1
    MAX_TILES = (B * T * TOPK - NE) // P + NE
    MAX_TILES += -MAX_TILES % UNROLL
    MIN_TILES = B * T * TOPK // P
    TABLE = MAX_TILES + UNROLL
    ROWS = (NE * CAP + SPARE) * P
    NB = B * SINKS
    DA = DH + 1
    DX = D + 2
    PAD = 2.0 ** 20
    NR = NE + 2 * M
    assert WINDOW == P and D == 2 * P and M == P and H * SINKS == 64

    with ExitStack() as ctx:
        def sb(name, shape, dt=F32):
            return ctx.enter_context(nc.sbuf_tensor(name, shape, dt))

        def sem(name):
            return ctx.enter_context(nc.semaphore(name))

        slots = nc.dram_tensor("slots", (ROWS, DX), F32, kind="Internal").ap()
        ys = nc.dram_tensor("ys", (TOPK * B * T + TABLE * P, D), F32, kind="Internal").ap()

        bank = [ctx.enter_context(nc.psum_tensor(f"bank{i}", [P, 512], F32)) for i in range(8)]

        ident = sb("ident", [P, P])
        ident_b = sb("ident_b", [P, P], BF16)
        before_b = sb("before_b", [P, P], BF16)
        ones_b = sb("ones_b", [P, P], BF16)
        causal_b = sb("causal_b", [P, P], BF16)
        small_mask_b = sb("small_mask_b", [NB, B * H * SINKS], BF16)
        head_block = sb("head_block", [H * SINKS, H])
        quarter = sb("quarter", [P, 4])
        pick = sb("pick", [B, B, P])
        pick_rows = sb("pick_rows", [B, NB])
        expert_no = sb("expert_no", [P, NE])
        expert_row = sb("expert_row", [P, NE])
        minus_half = sb("minus_half", [P, 8])
        pads = sb("pads", [P, DX])
        token2 = sb("token2", [P, TILES])
        pad_row = sb("pad_row", [P, TABLE])
        h_sb = sb("h_sb", [P, TPB, DX])
        ht = sb("ht", [P, UNROLL, C, P])
        h_flat = h_sb[:].rearrange("p j d -> p (j d)")
        wq_in, wk_in = [h_flat[:, n * C * D:(n + 1) * C * D].rearrange("p (c d) -> p c d", c=C) for n in range(2)]
        gabs, gsign = [h_flat[0:B, (4 + 2 * n) * D:(6 + 2 * n) * D].rearrange("p (s d) -> p s d", s=2)
                       for n in range(2)]
        ht_flat = ht[:].rearrange("p k c n -> p (k c n)")
        sm_in, sm_xn = [ht_flat[0:2 * NB, n * D:(n + 1) * D] for n in range(2)]
        sm_q, sm_x1 = [ht_flat[0:NB, n * D:(n + 1) * D] for n in range(2, 4)]
        wq_pad = sb("wq_pad", [P, C, H * 32])
        wk_pad = sb("wk_pad", [P, C, H * 32])
        wv_sb = sb("wv_sb", [P, C, D])
        wo_sb = sb("wo_sb", [P, C, D])
        gate_in = sb("gate_in", [NE, D])
        w_route = sb("w_route", [P, C, NR])
        wsd_sb = sb("wsd_sb", [P, D])
        wsd_gated = sb("wsd_gated", [P, D])
        w_gu = sb("w_gu", [P, NE * C * 2 * M])
        w_dn = sb("w_dn", [P, NE * D])
        cond_in = sb("cond_in", [B, D])
        cond_act = sb("cond_act", [B, D])
        cond_t = sb("cond_t", [P, C, B])
        wmod_sb = sb("wmod_sb", [P, C, 6 * D])
        wmod_flat = wmod_sb[:].rearrange("p c n -> p (c n)")
        kt_flat = wmod_flat[:, 0:HG * 4 * P]
        kt_bd = kt_flat.rearrange("p (g i n) -> p g i n", g=HG, i=4)
        mod_col = sb("mod_col", [P, 2 * C * B])
        GA, SB_, CB, GB = range(4)
        NORMED = slice(0, 2), slice(2, TPB - 1), slice(TPB - 1, TPB)
        PT_BANK = 6, 6, 4, 6, 5
        mod_bc = sb("mod_bc", [P, B * 4 * D])
        xs = sb("xs", [P, TILES * D])
        sm_stats = sb("sm_stats", [2 * NB, 6])
        sm_mv = sb("sm_mv", [2 * NB, 2])
        sm_rstd = sb("sm_rstd", [2 * NB, 2])
        sm_h = sb("sm_h", [P, C, 2, B, SINKS])
        sm_q_t = sb("sm_q_t", [P, HG, NB])
        sink_kt = sb("sink_kt", [P, HG, 4, NB])
        sink_v = sb("sink_v", [H * SINKS, B * H * DA])
        sm_m = sb("sm_m", [NB, H])
        sm_p = sb("sm_p", [NB, B, H, SINKS])
        sm_pt = sb("sm_pt", [H * SINKS, B, NB])
        sm_r = sb("sm_r", [NB, H])
        sm_o = sb("sm_o", [NB, H, DH])
        sm_ot = sb("sm_ot", [P, C, NB])
        sm_ga = sb("sm_ga", [NB, D])
        at_stats = sb("at_stats", [P, 6])
        at_mv = sb("at_mv", [P, 2])
        at_rs = sb("at_rs", [P, 2])
        at_xn_sb = sb("at_xn_sb", [P, D])
        at_ht = sb("at_ht", [P, C, P])
        qt = sb("qt", [P, HG, P])
        v_aug = sb("v_aug", [P, H, DA])
        m_sink = sb("m_sink", [P, H])
        m_win = sb("m_win", [P, H])
        m_all = sb("m_all", [P, H])
        p_sink = sb("p_sink", [P, H, SINKS])
        p_win = sb("p_win", [P, H, P])
        p_flat = p_win[:].rearrange("p h n -> p (h n)")
        mod = p_flat[0:B, 0:6 * D]
        pt_sink = sb("pt_sink", [H * SINKS, P])
        pt_win = sb("pt_win", [P, H, P])
        rden = sb("rden", [P, H])
        o_n = sb("o_n", [P, H, DH])
        o_t = sb("o_t", [P, C, P])
        o_g = sb("o_g", [P, D])
        st = sb("st", [P, TPB, 6])
        mv = sb("mv", [P, TPB, 2])
        veps = sb("veps", [P, TPB])
        rstd = sb("rstd", [P, TPB])
        centred = sb("centred", [P, 2, D])
        sm_hrep = centred[:].rearrange("p a d -> p (a d)")
        sg = sb("sg", [P, UNROLL, M])
        act_sb = sb("act_sb", [P, UNROLL, M])
        act_t = sb("act_t", [P, UNROLL, P])
        logit = sb("logit", [P, TPB, NE])
        top_v = sb("top_v", [P, TPB, 8])
        top_i = sb("top_i", [P, TPB, 8], U32)
        top_if = sb("top_if", [P, GROUP, TOPK])
        hot = sb("hot", [P, TOPK, GROUP, NE])
        mask_b = sb("mask_b", [P, GROUP, NE], BF16)
        mask_sum = sb("mask_sum", [P, NE])
        counted_b = sb("counted_b", [P, 2, NE], BF16)
        place = sb("place", [P, GROUP, NE])
        at_place = sb("at_place", [P, TOPK, GROUP, NE])
        slot_f = sb("slot_f", [P, TOPK, GROUP])
        slot_i = sb("slot_i", [P, TOPK, TPB], I32)
        val_all = sb("val_all", [P, TOPK, TILES])
        e_neg = sb("e_neg", [P, TOPK * TILES])
        score = sb("score", [P, TOPK, TILES])
        total = sb("total", [P, TILES])
        w_tok = sb("w_tok", [P, TOPK * TILES])
        steps_no = sb("steps_no", [P, TABLE])
        row_no = sb("row_no", [P, CAP - 1])
        n_e = sb("n_e", [P, NE])
        over = sb("over", [P, NE, CAP - 1])
        nt_e = sb("nt_e", [P, NE])
        ones_row = sb("ones_row", [P, NE])
        end_e = sb("end_e", [P, NE])
        tile_e = sb("tile_e", [P, TABLE])
        jump = sb("jump", [1, NE])
        past = wmod_flat[:, 0:TABLE * NE].rearrange("p (t e) -> p t e", e=NE)
        past_jump = wmod_flat[0:1, TABLE * NE:2 * TABLE * NE].rearrange("p (t e) -> p t e", e=NE)
        past_rows = sb("past_rows", [1, TABLE])
        n_over = sb("n_over", [1, MAX_TILES // UNROLL])
        n_fours = sb("n_fours", [1, 1])
        tab = sb("tab", [1, 2 * TABLE], I32)
        misc = sb("misc", [1, NE + 1], I32)
        xt = p_flat[:, 0:UNROLL * DX].rearrange("p (k d) -> p k d", d=DX)
        pt_flat = pt_win[:].rearrange("p h n -> p (h n)")
        y_sb = pt_flat[:, 0:UNROLL * D].rearrange("p (k d) -> p k d", d=D)
        row_f = sb("row_f", [P, UNROLL])
        row_all = sb("row_all", [P, TABLE], I32)
        row_i = sb("row_i", [P, UNROLL], I32)
        QUAD = 4
        RING = NE * C * 2 * M // (QUAD * TOPK * D)
        got = w_gu[:].rearrange("p (t n d) -> p t n d", n=TOPK, d=D)

        names = """
        ld_cond ld_wmod ld_small ld_wqk ld_wv ld_ws ld_exp x_small pad_dmas
        const w_padded setup_t cond_ready mod_ps mod_rows mod_ready col_ps
        col_ready bc_ps bc_sb
        sm_veps sm_rs sm_xnr sm_chain sm_hr sm_proj sm_vps sm_kqr sm_vr sm_log sm_sub sm_exp sm_ptp sm_ptr
        sm_ops sm_or sm_otp sm_otr sm_out sm_done
        at_ch at_xn at_xnt at_h at_q at_k at_v at_qs at_ks at_kas at_vs at_log at_sub
        at_exp at_pt at_pts at_o at_on at_ot at_ots at_out at_x
        ln_ch ln_veps ln_rstd h_cent h_ready wsd_ready 
        tr_ps tr_sb gu_ps tanh_ready act_ch act_ready aps_ready act_t_sb y_ps y_added lg_ready top_ch rt_ch masks rank_ps
        rank_read slots_ready
        cnt_ps tb tables row_copied waited_apart e_ready part_ready both_ready gated_ready out_ready saved
        """.split()
        S = {n: sem(n) for n in names}
        ld_x = [sem(f"ld_x{b}") for b in range(B)]
        (xt_in, ex_tr_ps, ex_ht, ex_gu_ps, ex_silu, ex_act_sb, ex_at_ps, ex_at_sb, ex_y_ps, ex_y_sb, row_ready,
         y_out, got_in) = [
            [sem(f"{n}{k}") for k in range(UNROLL)] for n in """
            xt_in ex_tr_ps ex_ht ex_gu_ps ex_silu ex_act_sb ex_at_ps ex_at_sb ex_y_ps ex_y_sb row_ready
            y_out got_in""".split()]
        scattered = [sem(f"scattered{j}") for j in range(0, TPB, 2)]

        def xcols(t):
            return xs[:, ds(t * D, D)]

        def mbc(b, kind, n=1):
            return mod_bc[:, ds(b * (4 * D) + kind * D, n * D)]

        class Chain:

            def __init__(self, eng, s, i=0, per=0, at=0):
                self.eng, self.s, self.i, self.per, self.n = eng, s, i, per, at

            def done(self, ins, alone=False):
                ins.then_inc(self.s, 1)
                self.n += 1
                wait = wait_apart if alone else type(self.eng).wait_ge
                wait(self.eng, self.s, self.i * self.per + self.n)

        def wait_apart(eng, s, value):
            eng.wait_ge(s, value)
            eng.sem_inc(S["waited_apart"], 1)

        def pad_experts(eng, engine, first):
            rows = nc.values_load_multi_w_load_instructions(
                misc[0:1, first:first + NE // 2], (engine,), min_val=0, max_val=ROWS - P,
                skip_runtime_bounds_check_because="a count of at most all tokens, on its expert's first row")[1]
            for row in rows:
                eng.dma_start(slots[ds(row, P), :], pads[:]).then_inc(S["pad_dmas"], 16)

        def tile_count(eng):
            last4 = eng.value_load(misc[0:1, NE:NE + 1], min_val=MIN_TILES // UNROLL - 1,
                                   max_val=MAX_TILES // UNROLL - 1)
            return last4, eng.snap(last4 + 1)

        def table(engine, first, n, top):
            return nc.values_load_multi_w_load_instructions(
                tab[0:1, ds(first, n)], (engine,), min_val=0, max_val=top,
                skip_runtime_bounds_check_because="the experts' numbers and tiles are clamped where the table is made")[1]

        block = ctx.enter_context(nc.Block())

        @block.sync
        def _(sp):
            chunks = lambda w: w.rearrange("(c p) n -> p c n", p=P)
            sp.dma_start(cond_in[:], cond).then_inc(S["ld_cond"], 16)
            for b in range(B):
                sp.dma_start(sm_in[b * SINKS:(b + 1) * SINKS, :], x[b, 0:SINKS, :]).then_inc(S["ld_small"], 16)
                late = x[b, T - P - SINKS:T - P, :]
                sp.dma_start(sm_in[NB + b * SINKS:NB + (b + 1) * SINKS, :], late).then_inc(S["ld_small"], 16)
            sp.dma_start(wq_in, chunks(wq)).then_inc(S["ld_wqk"], 16)
            sp.dma_start(wk_in, chunks(wk)).then_inc(S["ld_wqk"], 16)
            sp.dma_start(wv_sb[:], chunks(wv)).then_inc(S["ld_wv"], 16)
            sp.dma_start(wo_sb[:], chunks(wo)).then_inc(S["ld_wv"], 16)
            sp.dma_start(gate_in[:], gate_w).then_inc(S["ld_wqk"], 16)
            for b in range(B):
                dst = xs[:, b * TPB * D:(b + 1) * TPB * D].rearrange("p (j d) -> p j d", d=D)
                sp.dma_start(dst, x[b].rearrange("(j p) d -> p j d", p=P)).then_inc(ld_x[b], 16)
                if b == 0:
                    sp.dma_start(w_route[:, :, NE:NE + M], chunks(ws_gate)).then_inc(S["ld_ws"], 16)
                    sp.dma_start(w_route[:, :, NE + M:NR], chunks(ws_up)).then_inc(S["ld_ws"], 16)
                    sp.dma_start(wsd_sb[:], ws_down).then_inc(S["ld_ws"], 16)
            sp.wait_ge(S["sm_done"], 1)
            for b in range(B):
                sp.wait_ge(ld_x[b], 16)
                j = b * TPB + TPB - 2
                sp.dma_start(xs[P - SINKS:P, j * D:(j + 1) * D],
                             sm_x1[b * SINKS:(b + 1) * SINKS, :]).then_inc(S["x_small"], 16)
            gu = w_gu[:].rearrange("p (c e m) -> p e c m", c=C, m=2 * M)
            for n, w in enumerate((w_gate, w_up)):
                for c in range(C):
                    sp.dma_start(gu[:, :, c, n * M:(n + 1) * M],
                                 w[:, c * P:(c + 1) * P, :].rearrange("e p m -> p e m")).then_inc(S["ld_exp"], 16)
            sp.dma_start(w_dn[:].rearrange("p (e n) -> p e n", n=D),
                         w_down.rearrange("e p n -> p e n")).then_inc(S["ld_exp"], 16)
            sp.wait_ge(S["const"], N_CONST)
            for s in range(SPARE):
                r = (NE * CAP + s) * P
                sp.dma_start(slots[r:r + P, :], pads[:]).then_inc(S["pad_dmas"], 16)

            sp.wait_ge(S["tables"], 1)
            pad_experts(sp, SP, 0)
            sp.wait_ge(S["tables"], 2)
            last4, fours = tile_count(sp)
            sp.wait_ge(S["pad_dmas"], 16 * (SPARE + NE))
            for s in scattered:
                sp.wait_ge(s, 2 * 16 * TOPK * B)

            def load(row, k):
                sp.dma_start(xt[:, k, :], slots[ds(row, P), :]).then_inc(xt_in[k], 16)

            for k, row in enumerate(table(SP, TABLE, UNROLL, ROWS - P)):
                load(row, k)
            with sp.Fori(0, fours) as u:
                rows = table(SP, u * UNROLL + TABLE + UNROLL, UNROLL, ROWS - P)
                n = sp.snap(u + 1)
                for k in range(UNROLL):
                    wait_apart(sp, ex_tr_ps[k], n)
                    wait_apart(sp, row_ready[k], n * 2)
                    load(rows[k], k)
            for k in range(UNROLL):
                wait_apart(sp, y_out[k], fours * 16)
                wait_apart(sp, xt_in[k], fours * 16 + 16)

            def load_rows(q):
                at = q % RING * QUAD
                sp.dma_start(got[:, at:at + QUAD, :, :],
                             ys[q * QUAD * TOPK * P:(q + 1) * QUAD * TOPK * P, :]
                             .rearrange("(t p n) d -> p t n d", t=QUAD, n=TOPK)).then_inc(got_in[q % RING], 16)

            for q in range(RING):
                load_rows(q)
            for q in range(TILES // QUAD):
                sp.wait_ge(S["out_ready"], (q + 1) * QUAD)
                b, j = divmod(q * QUAD, TPB)
                sp.dma_start(out[b, j * P:(j + QUAD) * P, :].rearrange("(t p) d -> p t d", p=P),
                             xs[:, q * QUAD * D:(q + 1) * QUAD * D].rearrange("p (t d) -> p t d", d=D))\
                    .then_inc(S["saved"], 16)
                if q + RING < TILES // QUAD:
                    load_rows(q + RING)
            sp.wait_ge(S["saved"], 16 * TILES // QUAD)

        @block.gpsimd
        def _(pool):
            c = Chain(pool, S["const"])
            c.done(pool.memset(ident[:], 0.0))
            c.done(pool.affine_select(out=ident[:], in_=ident[:], pattern=[[-1, P]], compare_op=ALU.not_equal,
                                        fill=1.0, base=0, channel_multiplier=1))
            c.done(pool.memset(minus_half[:], -0.5))
            c.done(pool.memset(wq_pad[:], 0.0))
            c.done(pool.memset(wk_pad[:], 0.0))
            pool.wait_ge(S["sm_veps"], 1)
            pool.tensor_tensor(sm_rstd[:, 1:2], sm_rstd[:, 0:1], minus_half[0:2 * NB, 0:1], ALU.pow)\
                .then_inc(S["sm_rs"], 1)
            pool.wait_ge(S["ld_wqk"], 48)
            for src, dst in ((wq_in, wq_pad), (wk_in, wk_pad)):
                for k in range(C):
                    pool.tensor_copy(dst[:, k, :].rearrange("p (g i s) -> p i g s", i=4, s=32)[:, :, :, 0:DH],
                                     src[:, k, :].rearrange("p (i g s) -> p i g s", i=4, s=DH)).then_inc(S["w_padded"], 1)
            c.done(pool.memset(head_block[:], 1.0))
            c.done(pool.affine_select(out=head_block[:], in_=head_block[:], pattern=[[-SINKS, H]],
                                      compare_op=ALU.is_ge, fill=0.0, base=0, channel_multiplier=1))
            c.done(pool.affine_select(out=head_block[:], in_=head_block[:], pattern=[[SINKS, H]],
                                      compare_op=ALU.is_ge, fill=0.0, base=SINKS - 1, channel_multiplier=-1))
            c.done(pool.memset(quarter[:], 1.0))
            c.done(pool.affine_select(out=quarter[:], in_=quarter[:], pattern=[[-32, 4]],
                                      compare_op=ALU.is_ge, fill=0.0, base=0, channel_multiplier=1))
            c.done(pool.affine_select(out=quarter[:], in_=quarter[:], pattern=[[32, 4]],
                                      compare_op=ALU.is_ge, fill=0.0, base=31, channel_multiplier=-1))
            c.done(pool.tensor_copy(ident_b[:], ident[:]))
            c.done(pool.memset(small_mask_b[:], 0.0))
            c.done(pool.affine_select(out=small_mask_b[:], in_=small_mask_b[:],
                                      pattern=[[-SINKS, B], [0, H], [-1, SINKS]], compare_op=ALU.is_ge,
                                      fill=MASKED, base=0, channel_multiplier=1))
            c.done(pool.affine_select(out=small_mask_b[:], in_=small_mask_b[:],
                                      pattern=[[SINKS, B], [0, H], [0, SINKS]], compare_op=ALU.is_ge,
                                      fill=MASKED, base=SINKS - 1, channel_multiplier=-1))
            c.done(pool.memset(causal_b[:], 0.0))
            c.done(pool.affine_select(out=causal_b[:], in_=causal_b[:], pattern=[[-1, P]], compare_op=ALU.is_ge,
                                      fill=MASKED, base=0, channel_multiplier=1))
            c.done(pool.memset(pick[:], 0.0))
            c.done(pool.affine_select(out=pick[:], in_=pick[:], pattern=[[-1, B], [0, P]],
                                      compare_op=ALU.not_equal, fill=1.0, base=0, channel_multiplier=1))
            c.done(pool.memset(pick_rows[:], 0.0))
            c.done(pool.affine_select(out=pick_rows[:], in_=pick_rows[:], pattern=[[-1, B], [0, SINKS]],
                                      compare_op=ALU.not_equal, fill=1.0, base=0, channel_multiplier=1))
            c.done(pool.memset(before_b[:], 0.0))
            c.done(pool.affine_select(out=before_b[:], in_=before_b[:], pattern=[[-1, P]], compare_op=ALU.is_ge,
                                      fill=1.0, base=0, channel_multiplier=1))
            c.done(pool.memset(ones_b[:], 1.0))
            c.done(pool.memset(v_aug[:], 1.0))
            c.done(pool.memset(counted_b[:], 0.0))
            c.done(pool.memset(pads[:], 0.0))
            c.done(pool.memset(pads[:, D:D + 1], PAD))
            c.done(pool.iota(token2[:], pattern=[[2 * P, TILES]], base=0, channel_multiplier=2,
                             allow_small_or_imprecise_dtypes=True))
            c.done(pool.iota(pad_row[:], pattern=[[P, TABLE]], base=TOPK * B * T, channel_multiplier=1,
                             allow_small_or_imprecise_dtypes=True))
            c.done(pool.memset(ones_row[:], 1.0))
            c.done(pool.iota(expert_no[:], pattern=[[1, NE]], base=0, channel_multiplier=0,
                             allow_small_or_imprecise_dtypes=True))
            c.done(pool.iota(expert_row[:], pattern=[[CAP * P, NE]], base=0, channel_multiplier=0,
                             allow_small_or_imprecise_dtypes=True))
            c.done(pool.iota(steps_no[:], pattern=[[1, TABLE]], base=0, channel_multiplier=0,
                             allow_small_or_imprecise_dtypes=True))
            c.done(pool.iota(row_no[:], pattern=[[P, CAP - 1]], base=0, channel_multiplier=0,
                             allow_small_or_imprecise_dtypes=True))
            assert c.n == N_CONST

            pool.wait_ge(S["mod_ps"], 1)
            c.done(pool.memset(kt_flat, 0.0))
            pool.wait_ge(S["ld_ws"], 48)
            pool.wait_ge(S["bc_sb"], 2 * B)

            def rsqrt(b, n, r):
                pool.wait_ge(S["ln_veps"], b * 4 + n + 2)
                pool.tensor_tensor(rstd[:, r], veps[:, r], minus_half[:, r], ALU.pow).then_inc(S["ln_rstd"], 1)

            def scatter(j):
                for k in range(TOPK):
                    pool.indirect_dma_start(
                        out=slots, out_offset=bass.IndirectOffsetOnAxis(ap=slot_i[:, k, j:j + 1], axis=0),
                        in_=h_sb[:, j, :], in_offset=None).then_inc(scattered[j // 2], 16)

            def route_batch(b, first=False):
                pool.wait_ge(S["ln_veps"], b * 4 + 1)
                pool.tensor_tensor(at_rs[:, 1:2], at_rs[:, 0:1], minus_half[:, 0:1], ALU.pow)\
                    .then_inc(S["ln_rstd"], 1)
                rsqrt(b, 0, NORMED[0])
                rsqrt(b, 1, NORMED[1])
                if not first:
                    wait_apart(pool, S["slots_ready"], b * GPB)
                    scatter(GROUP)
                    scatter(GROUP + 1)
                    pool.wait_ge(S["y_ps"], b * TPB)
                pool.tensor_tensor(wsd_gated[:], wsd_sb[:], mbc(b, GB), ALU.mult).then_inc(S["wsd_ready"], 1)
                if not first:
                    scatter(GROUP + 2)
                    scatter(GROUP + 3)
                wait_apart(pool, S["slots_ready"], b * GPB + 1)
                scatter(0)
                scatter(1)
                rsqrt(b, 2, NORMED[2])
                scatter(2)
                scatter(3)

            route_batch(0, first=True)
            with pool.Fori(1, B) as b:
                route_batch(b)
            pool.wait_ge(S["slots_ready"], B * GPB)
            for j in range(GROUP, TPB):
                scatter(j)

            pool.wait_ge(S["tables"], 2)
            last4, fours = tile_count(pool)

            def put(t, k, u, n):
                wait_apart(pool, row_ready[k], n * 2)
                if u is not None:
                    wait_apart(pool, y_out[k], u * 16)
                pool.tensor_copy(row_i[:, k:k + 1], row_all[:, ds(t, 1)]).then_inc(S["row_copied"], 1)
                wait_apart(pool, ex_y_sb[k], n)
                wait_apart(pool, S["row_copied"], t + 1)
                pool.indirect_dma_start(out=ys, out_offset=bass.IndirectOffsetOnAxis(ap=row_i[:, k:k + 1], axis=0),
                                        in_=y_sb[:, k, :], in_offset=None).then_inc(y_out[k], 16)

            for k in range(UNROLL):
                put(k, k, None, 1)
            with pool.Fori(1, fours) as u:
                n = pool.snap(u + 1)
                for k in range(UNROLL):
                    put(u * UNROLL + k, k, u, n)

            for t in range(TILES):
                pool.wait_ge(S["gated_ready"], t + 1)
                pool.tensor_tensor(xcols(t), xcols(t), got[:, t % (RING * QUAD), 0, :], ALU.add)\
                    .then_inc(S["out_ready"], 1)

        @block.scalar
        def _(act):
            copy = lambda o, i: act.activation(o, i, ACT.Copy)
            act.dma_start(wmod_sb[:], w_mod.rearrange("(c p) n -> p c n", p=P)).then_inc(S["ld_wmod"], 16)
            for b in range(B):
                act.dma_start(sm_q[b * SINKS:(b + 1) * SINKS, :], x[b, T - P - SINKS:T - P, :])\
                    .then_inc(S["ld_small"], 16)
            act.wait_ge(S["ld_cond"], 16)
            act.activation(cond_act[:], cond_in[:], ACT.Silu).then_inc(S["cond_ready"], 1)
            act.wait_ge(S["setup_t"], 1)
            copy(cond_t[:].rearrange("p c b -> p (c b)"), bank[0][:, 0:C * B]).then_inc(S["cond_ready"], 1)
            for n in range(2 * B):
                act.wait_ge(S["bc_ps"], n + 1)
                copy(mod_bc[:, n * 2 * D:(n + 1) * 2 * D], bank[4 + n % 2][:]).then_inc(S["bc_sb"], 1)
            act.wait_ge(S["bc_ps"], 2 * B + 1)
            copy(sm_ga[:], bank[6][0:NB, 0:D]).then_inc(S["bc_sb"], 1)
            act.wait_ge(S["sm_sub"], 1)
            act.activation(sm_p[:], sm_p[:], ACT.Exp, scale=SCALE).then_inc(S["sm_exp"], 1)
            act.wait_ge(S["sm_ptp"], 1)
            copy(sm_pt[:].rearrange("p b n -> p (b n)"), bank[5][0:H * SINKS, 0:B * NB]).then_inc(S["sm_ptr"], 1)
            act.wait_ge(S["sm_otp"], 1)
            copy(sm_ot[:].rearrange("p c n -> p (c n)"), bank[7][:, 0:C * NB]).then_inc(S["sm_otr"], 1)
            act.wait_ge(S["const"], N_CONST)

            def tanh(b, j):
                act.wait_ge(S["gu_ps"], b * TPB + j)
                act.activation(sg[:, (j - 1) % UNROLL, :], bank[1][:, NE:NE + M], ACT.Tanh, scale=0.5)\
                    .then_inc(S["tanh_ready"], 1)

            def act_copy(b, j):
                act.wait_ge(S["aps_ready"], b * TPB + j - 1)
                copy(act_t[:, (j - 2) % UNROLL, :], bank[2][:, 0:P]).then_inc(S["act_t_sb"], 1)

            def h_copy(b, j):
                act.wait_ge(S["tr_ps"], b * TPB + j + 1)
                copy(ht[:, j % UNROLL, :, :].rearrange("p c n -> p (c n)"), bank[0][:, 0:D]).then_inc(S["tr_sb"], 1)

            def at_exp(b, g):
                act.wait_ge(S["at_sub"], b * (HG + 1) + g + 1)
                p = p_win[:, 4 * g:4 * g + 4, :] if g < HG else p_sink[:]
                act.activation(p, p, ACT.Exp, scale=SCALE).then_inc(S["at_exp"], 1)

            def at_probs(b, g):
                act.wait_ge(S["at_pt"], b * (HG + 1) + g + 1)
                if g < HG:
                    copy(pt_win[:, 4 * g:4 * g + 4, :].rearrange("p h n -> p (h n)"), bank[PT_BANK[g]][:])\
                        .then_inc(S["at_pts"], 1)
                else:
                    copy(pt_sink[:], bank[PT_BANK[g]][0:H * SINKS, 0:P]).then_inc(S["at_pts"], 1)

            def batch(b, first=False):
                if not first:
                    tanh(b, 0)
                    act_copy(b, 0)
                h_copy(b, 0)
                tanh(b, 1)
                act.wait_ge(S["at_q"], b + 1)
                copy(qt[:].rearrange("p g n -> p (g n)"), bank[4][:]).then_inc(S["at_qs"], 1)
                act.wait_ge(S["at_k"], b + 1)
                for i in (2, 3):
                    r = slice(32 * i, 32 * i + 32)
                    copy(kt_bd[r, :, i, :], bank[5][r, :].rearrange("p (g n) -> p g n", g=HG)).then_inc(S["at_kas"], 1)
                if not first:
                    act_copy(b, 1)
                act.wait_ge(S["at_v"], b + 1)
                copy(v_aug[:, :, 0:DH], bank[6][:, 0:D].rearrange("p (h s) -> p h s", s=DH)).then_inc(S["at_vs"], 1)
                h_copy(b, 1)
                tanh(b, 2)
                act_copy(b, 2)
                h_copy(b, 2)
                at_exp(b, 0)
                tanh(b, 3)
                at_probs(b, 0)
                act_copy(b, 3)
                at_exp(b, 1)
                h_copy(b, 3)
                at_exp(b, 2)
                tanh(b, 4)
                at_probs(b, 1)
                act_copy(b, 4)
                h_copy(b, 4)
                at_exp(b, 3)
                at_exp(b, 4)
                at_probs(b, 2)
                tanh(b, 5)
                at_probs(b, 3)
                at_probs(b, 4)
                act_copy(b, 5)
                h_copy(b, 5)
                tanh(b, 6)
                act.wait_ge(S["at_ot"], b + 1)
                copy(o_t[:].rearrange("p c n -> p (c n)"), bank[6][:, 0:D]).then_inc(S["at_ots"], 1)
                act_copy(b, 6)
                h_copy(b, 6)
                tanh(b, 7)
                act_copy(b, 7)
                h_copy(b, 7)

            batch(0, first=True)
            with act.Fori(1, B) as b:
                batch(b)
            tanh(B, 0)
            act_copy(B, 0)
            act_copy(B, 1)

            act.wait_ge(S["tables"], 1)
            pad_experts(act, mybir.EngineType.Activation, NE // 2)
            act.activation(e_neg[:], val_all[:].rearrange("p k t -> p (k t)"), ACT.Exp, scale=-1.0)\
                .then_inc(S["e_ready"], 1)
            act.wait_ge(S["tables"], 2)
            last4, fours = tile_count(act)

            def ex_h(k, n):
                act.wait_ge(ex_tr_ps[k], n)
                copy(ht[:, k, :, :].rearrange("p c n -> p (c n)"), bank[k % 2][:, 0:D]).then_inc(ex_ht[k], 1)

            def ex_s(k, n):
                act.wait_ge(ex_gu_ps[k], n)
                act.activation(sg[:, k, :], bank[2 + k % 2][:, 0:M], ACT.Silu).then_inc(ex_silu[k], 1)

            ex_h(0, 1)
            for k in range(UNROLL):
                ex_h((k + 1) % UNROLL, 1 if k < UNROLL - 1 else 2)
                ex_s(k, 1)
            with act.Fori(1, fours) as u:
                n = act.snap(u + 1)
                for k in range(UNROLL - 1):
                    ex_h(k + 1, n)
                    ex_s(k, n)
                ex_h(0, n + 1)
                ex_s(UNROLL - 1, n)

            for t in range(TILES):
                q, k = t // QUAD, t % (RING * QUAD)
                act.wait_ge(got_in[q % RING], 16 * (q // RING + 1))
                act.activation(got[:, k, 0, :], got[:, k, 0, :], ACT.Copy, scale=w_tok[:, t:t + 1])\
                    .then_inc(S["part_ready"], 1)

        @block.tensor
        def _(pe):
            mm = nc.tensor.matmul

            def transpose(o, i):
                n = i.shape[0]
                return nc.tensor.transpose(o, i, ident[0:n, 0:n])

            pe.wait_ge(S["const"], 2)
            pe.wait_ge(S["cond_ready"], 1)
            for k in range(C):
                last = transpose(bank[0][:, k * B:(k + 1) * B], cond_act[:, k * P:(k + 1) * P])
            last.then_inc(S["setup_t"], 1)
            pe.wait_ge(S["cond_ready"], 2)
            pe.wait_ge(S["ld_wmod"], 16)
            for s in range(2 * C):
                for k in range(C):
                    last = mm(bank[2][:, s * B:(s + 1) * B], wmod_sb[:, k, s * P:(s + 1) * P], cond_t[:, k, :],
                              start=(k == 0), stop=(k == C - 1))
            last.then_inc(S["col_ps"], 1)
            for n in range(3):
                for k in range(C):
                    last = mm(bank[4 + n][0:B, :], cond_t[:, k, :], wmod_sb[:, k, n * 2 * D:(n + 1) * 2 * D],
                              start=(k == 0), stop=(k == C - 1))
            last.then_inc(S["mod_ps"], 1)
            pe.wait_ge(S["ld_wqk"], 48)
            for k in range(C):
                last = transpose(bank[1][:, k * NE:(k + 1) * NE], gate_in[:, k * P:(k + 1) * P])
            last.then_inc(S["setup_t"], 1)
            pe.wait_ge(S["sm_xnr"], 1)
            for k in range(C):
                last = transpose(bank[0][:, k * 2 * NB:(k + 1) * 2 * NB], sm_xn[:, k * P:(k + 1) * P])
            last.then_inc(S["setup_t"], 1)
            pe.wait_ge(S["sm_hr"], C * B)
            pe.wait_ge(S["w_padded"], 2 * C)
            pe.wait_ge(S["col_ready"], 3)
            for n, w in enumerate((wk_pad, wq_pad)):
                for g in range(HG):
                    o = (n * HG + g) * NB
                    for k in range(C):
                        last = mm(bank[1][:, o:o + NB], w[:, k, g * P:(g + 1) * P],
                                  sm_h[:, k, n, :, :].rearrange("p b i -> p (b i)"), start=(k == 0),
                                  stop=(k == C - 1))
            last.then_inc(S["sm_proj"], 1)
            pe.wait_ge(S["ld_wv"], 32)
            pe.wait_ge(S["sm_hr"], C * B + C)
            for b in range(B):
                for k in range(C):
                    last = mm(bank[2 + b // 2][0:H * SINKS, (b % 2) * D:(b % 2 + 1) * D],
                              sm_hrep[:, (k * B + b) * H * SINKS:(k * B + b + 1) * H * SINKS], wv_sb[:, k, :],
                              start=(k == 0), stop=(k == C - 1))
            last.then_inc(S["sm_vps"], 1)
            pe.wait_ge(S["mod_ready"], 1)
            pe.wait_ge(S["const"], N_CONST)
            for n in range(2 * B):
                if n >= 2:
                    pe.wait_ge(S["bc_sb"], n - 1)
                mm(bank[4 + n % 2][:], pick[:, n // 2, :], mod[:, (2 + 2 * (n % 2)) * D:(4 + 2 * (n % 2)) * D],
                   start=True, stop=True).then_inc(S["bc_ps"], 1)
            mm(bank[6][0:NB, 0:D], pick_rows[:], mod[:, 2 * D:3 * D], start=True, stop=True)\
                .then_inc(S["bc_ps"], 1)
            pe.wait_ge(S["bc_sb"], 2 * B)
            pe.wait_ge(S["sm_kqr"], 1 + HG)
            logits = bank[4][0:NB, 0:B * H * SINKS].rearrange("q (b h k) -> q b h k", b=B, h=H)
            mm(bank[4][0:NB, 0:B * H * SINKS], ident_b[0:NB, 0:NB], small_mask_b[:], start=True, stop=False,
               skip_group_check=True)
            for g in range(HG):
                last = mm(logits.rearrange("q b (i g) k -> q g i b k", g=HG)[:, g], sm_q_t[:, g, :],
                          sink_kt[:, g, :, :].rearrange("p i (b k) -> p i b k", b=B), start=False,
                          stop=(g == HG - 1), skip_group_check=True)
            last.then_inc(S["sm_log"], 1)
            pe.wait_ge(S["sm_exp"], 1)
            for b in range(B):
                last = transpose(bank[5][0:H * SINKS, b * NB:(b + 1) * NB], sm_p[:, b, :, :].rearrange("q h k -> q (h k)"))
            last.then_inc(S["sm_ptp"], 1)
            pe.wait_ge(S["sm_ptr"], 1)
            pe.wait_ge(S["sm_vr"], B + 1)
            pe.wait_ge(S["bc_sb"], 2 * B + 1)
            for b in range(B):
                last = mm(bank[6][0:NB, 0:H * DA], sm_pt[:, b, :], sink_v[:, b * H * DA:(b + 1) * H * DA],
                          start=(b == 0), stop=(b == B - 1))
            last.then_inc(S["sm_ops"], 1)
            pe.wait_ge(S["sm_or"], 1)
            for k in range(C):
                last = transpose(bank[7][:, k * NB:(k + 1) * NB],
                                 sm_o[:].rearrange("q h s -> q (h s)")[:, k * P:(k + 1) * P])
            last.then_inc(S["sm_otp"], 1)
            pe.wait_ge(S["sm_otr"], 1)
            for k in range(C):
                last = mm(bank[7][0:NB, 0:D], sm_ot[:, k, :], wo_sb[:, k, :], start=(k == 0), stop=(k == C - 1))
            last.then_inc(S["sm_out"], 1)

            pe.wait_ge(S["ld_ws"], 48)
            def at_tr(b):
                pe.wait_ge(S["at_xn"], b + 1)
                for k in range(C):
                    last = transpose(bank[7][:, k * P:(k + 1) * P], at_xn_sb[:, k * P:(k + 1) * P])
                last.then_inc(S["at_xnt"], 1)

            def at_qkv(b):
                pe.wait_ge(S["at_h"], b * C + C)
                for w, o, s in ((wq_pad, bank[4], "at_q"), (wk_pad, bank[5], "at_k")):
                    for g in range(HG):
                        for k in range(C):
                            last = mm(o[:, g * P:(g + 1) * P], w[:, k, g * P:(g + 1) * P], at_ht[:, k, :],
                                      start=(k == 0), stop=(k == C - 1))
                    last.then_inc(S[s], 1)
                for k in range(C):
                    last = mm(bank[6][:, 0:D], at_ht[:, k, :], wv_sb[:, k, :], start=(k == 0), stop=(k == C - 1))
                last.then_inc(S["at_v"], 1)

            def at_sinks(b):
                pe.wait_ge(S["at_qs"], b + 1)
                for g in range(HG):
                    last = mm(bank[7][:, g * 4 * SINKS:(g + 1) * 4 * SINKS], qt[:, g, :],
                              sink_kt[:, g, :, ds(b * SINKS, SINKS)], start=True, stop=True)
                last.then_inc(S["at_log"], 1)

            def at_logits(b, g):
                o = bank[4 + g % 2][:]
                if g >= 2:
                    pe.wait_ge(S["at_sub"], b * (HG + 1) + g - 1)
                mm(o, ident_b[:], causal_b[:].unsqueeze(1).to_broadcast([P, 4, P]), start=True, stop=False,
                   skip_group_check=True)
                mm(o, qt[:, g, :], kt_bd[:, g, :, :].rearrange("p i n -> p (i n)"), start=False, stop=True,
                   skip_group_check=True).then_inc(S["at_log"], 1)

            def at_probs_t(b, g):
                (wait_apart if g == HG else type(pe).wait_ge)(pe, S["at_exp"], b * (HG + 1) + g + 1)
                if g in (1, 3):
                    pe.wait_ge(S["at_pts"], b * (HG + 1) + (g + 1) // 2)
                if g == HG:
                    transpose(bank[PT_BANK[g]][0:H * SINKS, 0:P], p_sink[:].rearrange("q h k -> q (h k)"))\
                        .then_inc(S["at_pt"], 1)
                    return
                for i in range(4):
                    last = transpose(bank[PT_BANK[g]][:, i * P:(i + 1) * P], p_win[:, 4 * g + i, :])
                last.then_inc(S["at_pt"], 1)

            def at_values(b):
                wait_apart(pe, S["at_pts"], b * (HG + 1) + HG + 1)
                mm(bank[7][:, 0:H * DA], pt_sink[:], sink_v[:, ds(b * (H * DA), H * DA)], start=True, stop=False,
                   skip_group_check=True)
                for n in range(H):
                    h = 4 * (n % 4) + n // 4
                    last = mm(bank[7][:, h * DA:(h + 1) * DA], pt_win[:, n, :], v_aug[:, h, :], start=False,
                              stop=(n == H - 1), skip_group_check=True)
                last.then_inc(S["at_o"], 1)

            def at_out_t(b):
                pe.wait_ge(S["at_on"], b + 1)
                for k in range(C):
                    last = transpose(bank[6][:, k * P:(k + 1) * P],
                                     o_n[:].rearrange("q h s -> q (h s)")[:, k * P:(k + 1) * P])
                last.then_inc(S["at_ot"], 1)

            def at_project(b):
                pe.wait_ge(S["at_ots"], b + 1)
                for k in range(C):
                    last = mm(bank[5][:, 0:D], o_t[:, k, :], wo_sb[:, k, :], start=(k == 0), stop=(k == C - 1))
                last.then_inc(S["at_out"], 1)

            def tr(b, j):
                pe.wait_ge(S["h_ready"], b * TPB + j + 1)
                for k in range(C):
                    last = transpose(bank[0][:, k * P:(k + 1) * P], h_sb[:, j, k * P:(k + 1) * P])
                last.then_inc(S["tr_ps"], 1)

            def gate_up(b, j, first=False):
                pe.wait_ge(S["tr_sb"], b * TPB + j)
                if not first or j >= 2:
                    pe.wait_ge(S["act_ready"], b * TPB + j - 1)
                    pe.wait_ge(S["lg_ready"], b * TPB + j - 1)
                for k in range(C):
                    last = mm(bank[1][:, 0:NR], ht[:, (j - 1) % UNROLL, k, :], w_route[:, k, :],
                              start=(k == 0), stop=(k == C - 1))
                last.then_inc(S["gu_ps"], 1)

            def act_tr(b, j, first=False):
                pe.wait_ge(S["act_ready"], b * TPB + j - 1)
                if not first or j >= 3:
                    pe.wait_ge(S["act_t_sb"], b * TPB + j - 2)
                transpose(bank[2][:, 0:P], act_sb[:, (j - 2) % UNROLL, :]).then_inc(S["aps_ready"], 1)

            def down(b, j, first=False):
                pe.wait_ge(S["act_t_sb"], b * TPB + j - 2)
                if j == 3:
                    pe.wait_ge(S["wsd_ready"], b + 1)
                if not first or j >= 4:
                    pe.wait_ge(S["y_added"], b * TPB + j - 3)
                if j == 2 or j == GROUP + 2:
                    pe.wait_ge(S["rank_read"], b * GPB + j // GROUP)
                mm(bank[3][:, 0:D], act_t[:, (j - 3) % UNROLL, :], wsd_gated[:], start=True, stop=True)\
                    .then_inc(S["y_ps"], 1)

            def rank(b, j):
                g = 1 if j == 1 else 0
                pe.wait_ge(S["masks"], b * GPB + 1 - g)
                pe.wait_ge(S["y_added"], b * TPB + j - 3)
                o = bank[3][:, D:D + GROUP * NE]
                mm(o, ones_b[:], counted_b[:, g, :].unsqueeze(1).to_broadcast([P, GROUP, NE]), start=True,
                   stop=False, skip_group_check=True)
                last = mm(o, before_b[:], mask_b[:].rearrange("p t e -> p (t e)"), start=False, stop=False,
                          skip_group_check=True)
                for i in range(GROUP - 1):
                    last = mm(bank[3][:, D + (i + 1) * NE:D + GROUP * NE], ones_b[:],
                              mask_b[:, i:i + 1, :].to_broadcast([P, GROUP - 1 - i, NE]), start=False,
                              stop=(i == GROUP - 2), skip_group_check=True)
                last.then_inc(S["rank_ps"], 1)

            def batch(b, first=False):
                for j in range(TPB):
                    before = not first
                    if before or j >= 1:
                        gate_up(b, j, first)
                    if j == 1:
                        at_qkv(b)
                    elif j == 2:
                        at_sinks(b)
                        pe.wait_ge(S["at_ks"], b * 2 + 2)
                        pe.wait_ge(S["at_kas"], b * 2 + 2)
                        at_logits(b, 0)
                        at_logits(b, 1)
                    elif j == 3:
                        at_logits(b, 2)
                        pe.wait_ge(S["at_vs"], b + 1)
                        at_probs_t(b, 0)
                    elif j == 4:
                        at_logits(b, 3)
                        at_probs_t(b, 1)
                    elif j == 5:
                        at_probs_t(b, 3)
                        at_probs_t(b, 4)
                    elif j == 6:
                        at_out_t(b)
                    if before or j >= 2:
                        act_tr(b, j, first)
                    if (before and j == 1) or j == GROUP + 1:
                        rank(b, j)
                    if j == 6:
                        at_project(b)
                    late = j in (0, TPB - 1)
                    if late and (before or j >= 3):
                        down(b, j, first)
                    if j == 0:
                        at_tr(b)
                    tr(b, j)
                    if not late and (before or j >= 3):
                        down(b, j, first)
                    if j == 4:
                        at_probs_t(b, 2)
                    elif j == 5:
                        at_values(b)

            batch(0, first=True)
            with pe.Fori(1, B) as b:
                batch(b)
            gate_up(B, 0)
            act_tr(B, 0)
            down(B, 0)
            act_tr(B, 1)
            rank(B, 1)
            down(B, 1)
            down(B, 2)

            pe.wait_ge(S["rank_read"], B * GPB)
            pe.wait_ge(S["rt_ch"], RT_CH * GPB * B)
            mm(bank[0][:, 0:NE], ones_b[:], counted_b[:, 0, :], start=True, stop=True).then_inc(S["cnt_ps"], 1)

            pe.wait_ge(S["tables"], 2)
            pe.wait_ge(S["ld_exp"], 16 * (2 * C + 1))
            last4, fours = tile_count(pe)

            def ex_tr(k, n):
                pe.wait_ge(xt_in[k], n * 16)
                for c in range(C):
                    last = transpose(bank[k % 2][:, c * P:(c + 1) * P], xt[:, k, c * P:(c + 1) * P])
                last.then_inc(ex_tr_ps[k], 1)

            def ex_gu(k, e, n):
                pe.wait_ge(ex_ht[k], n)
                for c in range(C):
                    last = mm(bank[2 + k % 2][:, 0:2 * M], ht[:, k, c, :], w_gu[:, ds(e + c * NE * 2 * M, 2 * M)],
                              start=(c == 0), stop=(c == C - 1))
                last.then_inc(ex_gu_ps[k], 1)

            def ex_at(k, n):
                pe.wait_ge(ex_act_sb[k], n)
                transpose(bank[4 + k % 2][:, 0:P], act_sb[:, k, :]).then_inc(ex_at_ps[k], 1)

            def ex_dn(k, e, n):
                pe.wait_ge(ex_at_sb[k], n)
                mm(bank[6 + k % 2][:, 0:D], act_t[:, k, :], w_dn[:, ds(e, D)], start=True, stop=True)\
                    .then_inc(ex_y_ps[k], 1)

            e = table(PE, 0, UNROLL, (NE - 1) * 2 * M)
            ex_tr(0, 1)
            for k in range(UNROLL):
                ex_tr((k + 1) % UNROLL, 1 if k < UNROLL - 1 else 2)
                ex_gu(k, e[k], 1)
                if k >= 1:
                    ex_at(k - 1, 1)
                if k >= 2:
                    ex_dn(k - 2, e[k - 2], 1)
            with pe.Fori(1, fours) as u:
                e = table(PE, u * UNROLL - 2, UNROLL + 2, (NE - 1) * 2 * M)
                n = pe.snap(u + 1)
                for k in range(UNROLL):
                    ex_tr((k + 1) % UNROLL, n if k < UNROLL - 1 else n + 1)
                    ex_gu(k, e[k + 2], n)
                    ex_at((k - 1) % UNROLL, n if k >= 1 else u)
                    ex_dn((k - 2) % UNROLL, e[k], n if k >= 2 else u)
            e = table(PE, last4 * UNROLL + 2, 2, (NE - 1) * 2 * M)
            ex_at(UNROLL - 1, fours)
            ex_dn(UNROLL - 2, e[0], fours)
            ex_dn(UNROLL - 1, e[1], fours)

        @block.vector
        def _(dve):
            v = nc.vector
            dve.wait_ge(S["ld_small"], 48 * B)
            ch = Chain(dve, S["sm_chain"])
            ch.done(v.bn_stats(sm_stats[:], sm_in))
            ch.done(v.bn_aggr(sm_mv[:], sm_stats[:]))
            v.tensor_scalar(sm_rstd[:, 0:1], sm_mv[:, 1:2], EPS, None, ALU.add).then_inc(S["sm_veps"], 1)
            dve.wait_ge(S["sm_rs"], 1)
            v.tensor_scalar(sm_xn, sm_in, sm_mv[:, 0:1], sm_rstd[:, 1:2], ALU.subtract, ALU.mult)\
                .then_inc(S["sm_xnr"], 1)
            dve.wait_ge(S["col_ps"], 1)
            v.tensor_copy(mod_col[:, 0:C * B], bank[2][:, 0:C * B]).then_inc(S["col_ready"], 1)
            v.tensor_scalar(mod_col[:, C * B:2 * C * B], bank[2][:, C * B:2 * C * B], 1.0, None, ALU.add)\
                .then_inc(S["col_ready"], 1)
            dve.wait_ge(S["setup_t"], 2)
            v.tensor_copy(w_route[:, :, 0:NE], bank[1][:, 0:C * NE].rearrange("p (c e) -> p c e", c=C))\
                .then_inc(S["col_ready"], 1)
            dve.wait_ge(S["col_ready"], 3)
            dve.wait_ge(S["setup_t"], 3)
            for k in range(C):
                view = bank[0][:, k * 2 * NB:(k + 1) * 2 * NB].rearrange("p (n b i) -> p n b i", n=2, b=B)
                for b in range(B):
                    v.tensor_scalar(sm_h[:, k, :, b, :], view[:, :, b, :],
                                    mod_col[:, (C + k) * B + b:(C + k) * B + b + 1],
                                    mod_col[:, k * B + b:k * B + b + 1], ALU.mult, ALU.add).then_inc(S["sm_hr"], 1)
            dve.wait_ge(S["sm_hr"], C * B)
            for k in range(C):
                rep = sm_hrep[:, k * B * H * SINKS:(k + 1) * B * H * SINKS]
                v.tensor_copy(rep.rearrange("p (b h i) -> p b h i", b=B, h=H),
                              sm_h[:, k, 0, :, :].unsqueeze(2).to_broadcast([P, B, H, SINKS]))\
                    .then_inc(S["sm_hr"], 1)
            dve.wait_ge(S["mod_ps"], 1)
            for n in range(3):
                v.tensor_copy(mod[:, n * 2 * D:(n + 1) * 2 * D], bank[4 + n][0:B, :]).then_inc(S["mod_rows"], 1)
            dve.wait_ge(S["mod_rows"], 3)
            g = Chain(dve, S["mod_rows"], at=3)
            gates = mod.rearrange("b (s d) -> b s d", d=D)[:, 2::3, :]
            g.done(v.scalar_tensor_tensor(gabs, gates, -1.0, gates, ALU.mult, ALU.max))
            g.done(v.tensor_scalar(gsign, gates, 0.0, 2.0, ALU.is_ge, ALU.mult))
            g.done(v.tensor_scalar(gabs, gabs, 0.25, None, ALU.max))
            g.done(v.scalar_tensor_tensor(gates, gsign, -1.0, gabs, ALU.add, ALU.mult))
            v.tensor_scalar(mod[:, 4 * D:5 * D], mod[:, 4 * D:5 * D], 1.0, None, ALU.add)\
                .then_inc(S["mod_ready"], 1)
            dve.wait_ge(S["sm_proj"], 1)
            dve.wait_ge(S["const"], N_CONST)
            v.tensor_copy(sm_q_t[:].rearrange("p g q -> p (g q)"), bank[1][:, HG * NB:2 * HG * NB])\
                .then_inc(S["sm_kqr"], 1)
            for g in range(HG):
                v.tensor_tensor(sink_kt[:, g, :, :],
                                bank[1][:, g * NB:(g + 1) * NB].unsqueeze(1).to_broadcast([P, 4, NB]),
                                quarter[:].unsqueeze(2).to_broadcast([P, 4, NB]), ALU.mult)\
                    .then_inc(S["sm_kqr"], 1)
            dve.wait_ge(S["sm_vps"], 1)
            dve.wait_ge(S["const"], N_CONST)
            sv = sink_v[:].rearrange("p (b h s) -> p b h s", b=B, h=H)
            for b in range(B):
                src = bank[2 + b // 2][0:H * SINKS, (b % 2) * D:(b % 2 + 1) * D]
                v.tensor_tensor(sv[:, b, :, 0:DH], src.rearrange("p (h s) -> p h s", h=H),
                                head_block[:].unsqueeze(2).to_broadcast([H * SINKS, H, DH]), ALU.mult)\
                    .then_inc(S["sm_vr"], 1)
            v.tensor_copy(sv[:, :, :, DH], head_block[:].unsqueeze(1).to_broadcast([H * SINKS, B, H]))\
                .then_inc(S["sm_vr"], 1)
            dve.wait_ge(S["sm_log"], 1)
            lg = bank[4][0:NB, 0:B * H * SINKS].rearrange("q (b h k) -> q b h k", b=B, h=H)
            ch.done(v.tensor_reduce(sm_m[:], lg.rearrange("q b h k -> q h b k"), AX.XY, ALU.max))
            for b in range(B):
                last = v.tensor_tensor(sm_p[:, b, :, :], lg[:, b, :, :],
                                       sm_m[:].unsqueeze(2).to_broadcast([NB, H, SINKS]), ALU.subtract)
                if b < B - 1:
                    ch.done(last)
            last.then_inc(S["sm_sub"], 1)
            dve.wait_ge(S["sm_ops"], 1)
            so = bank[6][0:NB, 0:H * DA].rearrange("q (h s) -> q h s", h=H)
            ch.done(v.reciprocal(sm_r[:], so[:, :, DH]))
            v.tensor_tensor(sm_o[:], so[:, :, 0:DH], sm_r[:].unsqueeze(2).to_broadcast([NB, H, DH]), ALU.mult)\
                .then_inc(S["sm_or"], 1)
            dve.wait_ge(S["sm_out"], 1)
            dve.wait_ge(S["bc_sb"], 2 * B + 1)
            ch.done(v.tensor_tensor(sm_x1, bank[7][0:NB, 0:D], sm_ga[:], ALU.mult))
            v.tensor_tensor(sm_x1, sm_x1, sm_q, ALU.add).then_inc(S["sm_done"], 1)
            dve.wait_ge(S["bc_sb"], 2 * B)
            dve.wait_ge(S["ld_ws"], 48)
            for b in range(B):
                dve.wait_ge(ld_x[b], 16)

            ls = bank[7][:, 0:H * SINKS].rearrange("q (n k) -> q n k", n=H)
            lws = [bank[4 + g % 2][:].rearrange("q (h k) -> q h k", h=4) for g in range(HG)]

            def at_norm(b, at):
                at.done(v.bn_stats(at_stats[:], xcols(b * TPB + TPB - 1)), alone=True)
                at.done(v.bn_aggr(at_mv[:], at_stats[:]))
                v.tensor_scalar(at_rs[:, 0:1], at_mv[:, 1:2], EPS, None, ALU.add).then_inc(S["ln_veps"], 1)

            def at_xn(b):
                dve.wait_ge(S["ln_rstd"], b * 4 + 1)
                v.tensor_scalar(at_xn_sb[:], xcols(b * TPB + TPB - 1), at_mv[:, 0:1], at_rs[:, 1:2], ALU.subtract,
                                ALU.mult).then_inc(S["at_xn"], 1)

            def at_modulate(b):
                dve.wait_ge(S["at_xnt"], b + 1)
                for k in range(C):
                    v.tensor_scalar(at_ht[:, k, :], bank[7][:, k * P:(k + 1) * P],
                                    mod_col[:, ds(b + (C + k) * B, 1)], mod_col[:, ds(b + k * B, 1)],
                                    ALU.mult, ALU.add).then_inc(S["at_h"], 1)

            def at_keys(b):
                dve.wait_ge(S["at_k"], b + 1)
                for i in (0, 1):
                    r = slice(32 * i, 32 * i + 32)
                    v.tensor_copy(kt_bd[r, :, i, :], bank[5][r, :].rearrange("p (g n) -> p g n", g=HG))\
                        .then_inc(S["at_ks"], 1)

            def at_sink_max(b, at):
                dve.wait_ge(S["at_log"], b * (HG + 1) + 1)
                at.done(v.tensor_reduce(m_sink[:], ls, AX.X, ALU.max))

            def at_less_max(b, g, at):
                dve.wait_ge(S["at_log"], b * (HG + 1) + g + 2)
                hs = slice(4 * g, 4 * g + 4)
                at.done(v.tensor_reduce(m_win[:, hs], lws[g], AX.X, ALU.max))
                at.done(v.tensor_tensor(m_all[:, hs], m_win[:, hs], m_sink[:, hs], ALU.max))
                v.tensor_tensor(p_win[:, hs, :], lws[g], m_all[:, hs].unsqueeze(2).to_broadcast([P, 4, P]),
                                ALU.subtract).then_inc(S["at_sub"], 1)

            def at_sinks_less_max(b):
                v.tensor_tensor(p_sink[:].rearrange("q (i g) k -> q g i k", g=HG),
                                bank[7][:, 0:H * SINKS].rearrange("q (g i k) -> q g i k", g=HG, i=4),
                                m_all[:].rearrange("q (g i) -> q g i", g=HG).unsqueeze(3)
                                .to_broadcast([P, HG, 4, SINKS]), ALU.subtract).then_inc(S["at_sub"], 1)

            def at_normalise(b, at):
                dve.wait_ge(S["at_o"], b + 1)
                ob = bank[7][:, 0:H * DA].rearrange("q (h s) -> q h s", h=H)
                at.done(v.reciprocal(rden[:], ob[:, :, DH]))
                v.tensor_tensor(o_n[:], ob[:, :, 0:DH], rden[:].unsqueeze(2).to_broadcast([P, H, DH]), ALU.mult)\
                    .then_inc(S["at_on"], 1)

            def at_add(b, at):
                dve.wait_ge(S["at_out"], b + 1)
                at.done(v.tensor_tensor(o_g[:], bank[5][:, 0:D], mbc(b, GA), ALU.mult))
                tail = xcols(b * TPB + TPB - 1)
                v.tensor_tensor(tail, tail, o_g[:], ALU.add).then_inc(S["at_x"], 1)
                assert at.n == AT_CH, at.n

            def norm_stats(b, n, ln):
                r = range(TPB)[NORMED[n]]
                for j in r:
                    v.bn_stats(st[:, j, :], xcols(b * TPB + j)).then_inc(S["ln_ch"], 1)
                    ln.n += 1
                wait_apart(dve, S["ln_ch"], b * (2 * TPB) + ln.n)
                for j in r:
                    v.bn_aggr(mv[:, j, :], st[:, j, :]).then_inc(S["ln_ch"], 1)
                    ln.n += 1
                dve.wait_ge(S["ln_ch"], b * (2 * TPB) + ln.n)
                v.tensor_scalar(veps[:, NORMED[n]], mv[:, NORMED[n], 1], EPS, None, ALU.add)\
                    .then_inc(S["ln_veps"], 1)

            def h_tile(b, j, first):
                dve.wait_ge(S["ln_rstd"], b * 4 + (2 if j < 2 else 3 if j < TPB - 1 else 4))
                v.scalar_tensor_tensor(centred[:, j % 2, :], xcols(b * TPB + j), mv[:, j, 0:1], mbc(b, CB),
                                       ALU.subtract, ALU.mult).then_inc(S["h_cent"], 1)
                if not first:
                    dve.wait_ge(scattered[j // 2], b * (2 * 16 * TOPK))
                wait_apart(dve, S["h_cent"], b * TPB + j + 1)
                v.scalar_tensor_tensor(h_sb[:, j, 0:D], centred[:, j % 2, :], rstd[:, j:j + 1], mbc(b, SB_),
                                       ALU.mult, ALU.add).then_inc(S["h_ready"], 1)

            def activation(b, j):
                k = (j - 1) % TPB
                dve.wait_ge(S["tanh_ready"], b * TPB + j)
                v.scalar_tensor_tensor(act_sb[:, k % UNROLL, :], sg[:, k % UNROLL, :], 1.0, bank[1][:, NE + M:NR],
                                       ALU.add, ALU.mult).then_inc(S["act_ch"], 1)
                v.tensor_scalar(logit[:, k, :], bank[1][:, 0:NE], SATURATED, None, ALU.min)\
                    .then_inc(S["lg_ready"], 1)
                wait_apart(dve, S["act_ch"], b * TPB + j)
                v.scalar_tensor_tensor(act_sb[:, k % UNROLL, :], bank[1][:, NE:NE + M], 0.5,
                                       act_sb[:, k % UNROLL, :], ALU.mult, ALU.mult).then_inc(S["act_ready"], 1)
                wait_apart(dve, S["lg_ready"], b * TPB + j)
                v.max(top_v[:, k, :], logit[:, k, :]).then_inc(S["top_ch"], 1)
                wait_apart(dve, S["top_ch"], b * (2 * TPB) + 2 * j - 1)
                v.max_index(top_i[:, k, :], top_v[:, k, :], logit[:, k, :]).then_inc(S["top_ch"], 1)

            def add_y(b, j):
                dve.wait_ge(S["y_ps"], b * TPB + j - 2)
                x = xcols(b * TPB + j - 3)
                v.tensor_tensor(x, x, bank[3][:, 0:D], ALU.add).then_inc(S["y_added"], 1)

            def chosen(b, j):
                first = b * TPB + j - GROUP
                g = 1 if j == 0 else 0
                r = slice(g * GROUP, (g + 1) * GROUP)
                rt = Chain(dve, S["rt_ch"], b, GPB * RT_CH, -g * RT_CH)
                dve.wait_ge(S["top_ch"], b * (2 * TPB) + 2 * j)
                v.tensor_copy(val_all[:, :, ds(first, GROUP)], top_v[:, r, 0:TOPK].rearrange("p t k -> p k t"))\
                    .then_inc(S["rt_ch"], 1)
                rt.n += 1
                rt.done(v.tensor_copy(top_if[:], top_i[:, r, 0:TOPK]))
                for n in range(TOPK):
                    rt.done(v.tensor_tensor(hot[:, n, :, :], expert_no[:].unsqueeze(1).to_broadcast([P, GROUP, NE]),
                                            top_if[:, :, n:n + 1].to_broadcast([P, GROUP, NE]), ALU.is_equal))
                for col, src in ((D, token2[:, ds(first, GROUP)]), (D + 1, top_if[:, :, 0])):
                    v.tensor_copy(h_sb[:, r, col], src).then_inc(S["rt_ch"], 1)
                    rt.n += 1
                v.tensor_tensor(mask_b[:], hot[:, 0, :, :], hot[:, 1, :, :], ALU.add).then_inc(S["masks"], 1)
                dve.wait_ge(S["masks"], b * GPB + 1 - g)
                rt.done(v.tensor_reduce(mask_sum[:], mask_b[:].rearrange("p t e -> p e t"), AX.X, ALU.add))
                return rt

            def placed(b, j, rt):
                g = 1 if j == 1 else 0
                dve.wait_ge(S["rank_ps"], b * GPB + 1 - g)
                wait_apart(dve, S["y_ps"], b * TPB + j - 2)
                v.tensor_tensor(place[:], bank[3][:, D:D + GROUP * NE].rearrange("p (t e) -> p t e", e=NE),
                                expert_row[:].unsqueeze(1).to_broadcast([P, GROUP, NE]), ALU.add)\
                    .then_inc(S["rank_read"], 1)
                rt.done(v.tensor_tensor(counted_b[:, 1 - g, :], counted_b[:, g, :], mask_sum[:], ALU.add))
                dve.wait_ge(S["rank_read"], b * GPB + 1 - g)
                for n in range(TOPK):
                    rt.done(v.tensor_tensor(at_place[:, n, :, :], place[:], hot[:, n, :, :], ALU.mult))
                rt.done(v.tensor_reduce(slot_f[:], at_place[:], AX.X, ALU.add))
                r = slice(g * GROUP, (g + 1) * GROUP)
                v.tensor_copy(slot_i[:, :, r], slot_f[:]).then_inc(S["slots_ready"], 1)

            def batch(b, first=False):
                at = Chain(dve, S["at_ch"], b, AT_CH)
                ln = Chain(dve, S["ln_ch"], b, 2 * TPB)
                at_norm(b, at)
                norm_stats(b, 0, ln)
                at_xn(b)
                h_tile(b, 0, first)
                if not first:
                    activation(b, 0)
                    add_y(b, 0)
                at_modulate(b)
                if not first:
                    rt = chosen(b, 0)
                h_tile(b, 1, first)
                if first:
                    dve.wait_ge(S["x_small"], 16 * B)
                norm_stats(b, 1, ln)
                activation(b, 1)
                at_keys(b)
                if not first:
                    placed(b, 1, rt)
                    add_y(b, 1)
                h_tile(b, 2, first)
                activation(b, 2)
                at_sink_max(b, at)
                at_less_max(b, 0, at)
                if not first:
                    add_y(b, 2)
                h_tile(b, 3, first)
                at_less_max(b, 1, at)
                activation(b, 3)
                at_less_max(b, 2, at)
                add_y(b, 3)
                h_tile(b, 4, first)
                activation(b, 4)
                at_less_max(b, 3, at)
                at_sinks_less_max(b)
                add_y(b, 4)
                rt = chosen(b, 4)
                h_tile(b, 5, first)
                activation(b, 5)
                placed(b, 5, rt)
                add_y(b, 5)
                h_tile(b, 6, first)
                at_normalise(b, at)
                activation(b, 6)
                at_add(b, at)
                add_y(b, 6)
                wait_apart(dve, S["at_x"], b + 1)
                norm_stats(b, 2, ln)
                activation(b, 7)
                h_tile(b, 7, first)
                add_y(b, 7)

            batch(0, first=True)
            with dve.Fori(1, B) as b:
                batch(b)
            activation(B, 0)
            add_y(B, 0)
            rt = chosen(B, 0)
            placed(B, 1, rt)
            add_y(B, 1)
            add_y(B, 2)

            dve.wait_ge(S["cnt_ps"], 1)
            dve.wait_ge(S["slots_ready"], B * GPB)
            tb = Chain(dve, S["tb"])
            tb.done(v.tensor_copy(n_e[:], bank[0][:, 0:NE]))
            v.tensor_tensor(misc[:, 0:NE], n_e[0:1, :], expert_row[0:1, :], ALU.add).then_inc(S["tables"], 1)
            tb.done(v.tensor_tensor(over[:], n_e[:].unsqueeze(2).to_broadcast([P, NE, CAP - 1]),
                                    row_no[:].unsqueeze(1).to_broadcast([P, NE, CAP - 1]), ALU.is_gt))
            tb.done(v.tensor_reduce(nt_e[:], over[:], AX.X, ALU.add))
            tb.done(v.tensor_tensor_scan(end_e[:], ones_row[:], nt_e[:], 0.0, ALU.mult, ALU.add))
            tb.done(v.tensor_scalar(jump[:], nt_e[0:1, :], -float(P), float(CAP * P), ALU.mult, ALU.add))
            tb.done(v.tensor_tensor(past, steps_no[:].unsqueeze(2).to_broadcast([P, TABLE, NE]),
                                    end_e[:].unsqueeze(1).to_broadcast([P, TABLE, NE]), ALU.is_ge))
            tb.done(v.tensor_tensor(past_jump, past[0:1, :, :], jump[:].unsqueeze(1).to_broadcast([1, TABLE, NE]),
                                    ALU.mult))
            tb.done(v.tensor_reduce(past_rows[:], past_jump, AX.X, ALU.add))
            tb.done(v.tensor_reduce(tile_e[:], past, AX.X, ALU.add))
            tb.done(v.tensor_tensor(n_over[:], end_e[0:1, NE - 1:NE].to_broadcast([1, MAX_TILES // UNROLL]),
                                    steps_no[0:1, 0:MAX_TILES:UNROLL], ALU.is_gt))
            tb.done(v.tensor_scalar(tile_e[:], tile_e[:], float(NE - 1), None, ALU.min))
            tb.done(v.tensor_reduce(n_fours[:], n_over[:], AX.X, ALU.add))
            tb.done(v.tensor_scalar(tab[:, 0:TABLE], tile_e[0:1, :], float(2 * M), None, ALU.mult))
            tb.done(v.scalar_tensor_tensor(tab[:, TABLE:2 * TABLE], steps_no[0:1, :], float(P), past_rows[:], ALU.mult,
                                           ALU.add))
            v.tensor_scalar(misc[:, NE:NE + 1], n_fours[:], -1.0, None, ALU.add).then_inc(S["tables"], 1)
            dve.wait_ge(S["e_ready"], 1)
            sc = score[:].rearrange("p k t -> p (k t)")
            tb.done(v.tensor_scalar(e_neg[:], e_neg[:], 1.0, None, ALU.add))
            tb.done(v.reciprocal(sc, e_neg[:]))
            tb.done(v.tensor_tensor(total[:], score[:, 0, :], score[:, 1, :], ALU.add))
            tb.done(v.tensor_scalar(total[:], total[:], 1e-20, None, ALU.add))
            tb.done(v.reciprocal(total[:], total[:]))
            for n in range(TOPK):
                tb.done(v.scalar_tensor_tensor(w_tok[:, n * TILES:(n + 1) * TILES], score[:, n, :], ROUTE_SCALE,
                                              total[:], ALU.mult, ALU.mult))
            dve.wait_ge(S["tables"], 2)
            last4, fours = tile_count(dve)

            def ex_act(k, n):
                dve.wait_ge(ex_silu[k], n)
                v.tensor_tensor(act_sb[:, k, :], bank[2 + k % 2][:, M:2 * M], sg[:, k, :], ALU.mult)\
                    .then_inc(ex_act_sb[k], 1)

            def ex_at(k, n):
                dve.wait_ge(ex_at_ps[k], n)
                v.tensor_copy(act_t[:, k, :], bank[4 + k % 2][:, 0:P]).then_inc(ex_at_sb[k], 1)

            def ex_y(k, n, stored):
                dve.wait_ge(ex_y_ps[k], n)
                if stored is not None:
                    dve.wait_ge(y_out[k], stored * 16)
                v.tensor_copy(y_sb[:, k, :], bank[6 + k % 2][:, 0:D]).then_inc(ex_y_sb[k], 1)

            def rows(t, k, n):
                dve.wait_ge(xt_in[k], n * 16)
                v.scalar_tensor_tensor(row_f[:, k:k + 1], xt[:, k, D + 1:DX], tile_e[:, ds(t, 1)],
                                       xt[:, k, D:D + 1], ALU.not_equal, ALU.add).then_inc(row_ready[k], 1)
                wait_apart(dve, row_ready[k], n * 2 - 1)
                v.tensor_tensor(row_all[:, ds(t, 1)], row_f[:, k:k + 1], pad_row[:, ds(t, 1)], ALU.min)\
                    .then_inc(row_ready[k], 1)

            for t in range(2 * UNROLL):
                k, n = t % UNROLL, t // UNROLL + 1
                rows(t, k, n)
                ex_act(k, n)
                if t >= 1:
                    ex_at((t - 1) % UNROLL, (t - 1) // UNROLL + 1)
                if t >= 2:
                    ex_y((t - 2) % UNROLL, (t - 2) // UNROLL + 1, 1 if t - 2 >= UNROLL else None)
            with dve.Fori(2, fours) as u:
                n = dve.snap(u + 1)
                for k in range(UNROLL):
                    rows(u * UNROLL + k, k, n)
                    ex_act(k, n)
                    ex_at((k - 1) % UNROLL, n if k >= 1 else u)
                    ex_y((k - 2) % UNROLL, n if k >= 2 else u, u if k >= 2 else u - 1)
            ex_at(UNROLL - 1, fours)
            ex_y(UNROLL - 2, fours, last4)
            ex_y(UNROLL - 1, fours, last4)

            for t in range(TILES):
                k = t % (RING * QUAD)
                dve.wait_ge(S["part_ready"], t + 1)
                v.scalar_tensor_tensor(got[:, k, 1, :], got[:, k, 1, :], w_tok[:, t + TILES:t + TILES + 1],
                                       got[:, k, 0, :], ALU.mult, ALU.add).then_inc(S["both_ready"], 1)
                dve.wait_ge(S["both_ready"], t + 1)
                v.tensor_tensor(got[:, k, 0, :], got[:, k, 1, :], mbc(t // TPB, GB), ALU.mult)\
                    .then_inc(S["gated_ready"], 1)


N_CONST = 35
AT_CH = 13
RT_CH = 11

_INS = ["L0_attn_x", "L0_attn_Wq", "L0_attn_Wk", "L0_attn_Wv", "L0_attn_Wo", "L0_ffn_gate_w", "L0_ffn_w_gate",
        "L0_ffn_w_up", "L0_ffn_w_down", "L0_ffn_ws_gate", "L0_ffn_ws_up", "L0_ffn_ws_down", "L0_c", "L0_wmod"]
_OUTS = [((4, 1024, 256), "float32")]


def kernel(**inputs):
    import numpy as _np
    import concourse.bacc as _bacc
    from concourse import mybir as _mybir
    from concourse.bass_utils import run_bass_kernel_spmd as _run

    nc = _bacc.Bacc("TRN2", target_bir_lowering=False, num_devices=1)
    arrays, args = {}, []
    for name in _INS:
        a = _np.ascontiguousarray(inputs[name])
        arrays[f"in_{name}_dram"] = a
        args.append(nc.dram_tensor(f"in_{name}_dram", a.shape, _mybir.dt.from_np(a.dtype), kind="ExternalInput").ap())
    for i, (shape, dtype) in enumerate(_OUTS):
        dt = _mybir.dt.from_np(_np.dtype(dtype))
        args.append(nc.dram_tensor(f"out_{i}_dram", shape, dt, kind="ExternalOutput").ap())
    bass_adaln_attention_moe(nc, *args)
    r = _run(nc, [arrays], core_ids=[0])
    got = tuple(r.results[0][f"out_{i}_dram"] for i in range(len(_OUTS)))
    return got[0]
```

```python
from contextlib import ExitStack

import concourse.bass as bass
from concourse import mybir

ALU = mybir.AluOpType
ACT = mybir.ActivationFunctionType
AX = mybir.AxisListType
F32 = mybir.dt.float32
BF16 = mybir.dt.bfloat16
I32 = mybir.dt.int32
U32 = mybir.dt.uint32
ds = bass.ds
SP, PE = mybir.EngineType.SP, mybir.EngineType.PE

P = 128
MASKED = -1e30
EPS = 1e-5
SATURATED = 16.6355
UNROLL = 4
SPARE = 2 * UNROLL


def bass_adaln_attention_moe(nc, x, wq, wk, wv, wo, gate_w, w_gate, w_up, w_down, ws_gate, ws_up,
                             ws_down, cond, w_mod, out):
    B, T, D = x.shape
    NE, _, M = w_gate.shape
    H, SINKS, WINDOW = 16, 4, 128
    DH = D // H
    SCALE = DH ** -0.5
    TOPK, ROUTE_SCALE = 2, 2.5
    C = D // P
    CH = H // C
    HG = H // 4
    TPB = T // P
    TILES = B * TPB
    GROUP = 4
    GPB = TPB // GROUP
    CAP = B * T // P + 1
    MAX_TILES = (B * T * TOPK - NE) // P + NE
    MAX_TILES += -MAX_TILES % UNROLL
    MIN_TILES = B * T * TOPK // P
    TABLE = MAX_TILES + UNROLL
    ROWS = (NE * CAP + SPARE) * P
    NB = B * SINKS
    DA = DH + 1
    DX = D + 2
    PAD = 2.0 ** 20
    NR = NE + 2 * M
    assert WINDOW == P and D == 2 * P and M == P and H * SINKS == 64

    with ExitStack() as ctx:
        def sb(name, shape, dt=F32):
            return ctx.enter_context(nc.sbuf_tensor(name, shape, dt))

        def sem(name):
            return ctx.enter_context(nc.semaphore(name))

        slots = nc.dram_tensor("slots", (ROWS, DX), F32, kind="Internal").ap()
        ys = nc.dram_tensor("ys", (TOPK * B * T + TABLE * P, D), F32, kind="Internal").ap()

        mod_rows_out = nc.dram_tensor("mod_rows_out", (B, 4 * D), F32, kind="Internal").ap()

        bank = [ctx.enter_context(nc.psum_tensor(f"bank{i}", [P, 512], F32)) for i in range(8)]

        ident = sb("ident", [P, P])
        ident_b = sb("ident_b", [P, P], BF16)
        before_b = sb("before_b", [P, P], BF16)
        ones_b = sb("ones_b", [P, P], BF16)
        causal_b = sb("causal_b", [P, P], BF16)
        small_mask_b = sb("small_mask_b", [NB, B * H * SINKS], BF16)
        head_block = sb("head_block", [H * SINKS, H])
        own_rows = sb("own_rows", [P, CH])
        pick_rows = sb("pick_rows", [B, NB])
        expert_no = sb("expert_no", [P, NE])
        expert_row = sb("expert_row", [P, NE])
        minus_half = sb("minus_half", [P, 8])
        pads = sb("pads", [P, DX])
        token2 = sb("token2", [P, TILES])
        pad_row = sb("pad_row", [P, TABLE])
        h_sb = sb("h_sb", [P, TPB, DX])
        ht = sb("ht", [P, UNROLL, C, P])
        h_flat = h_sb[:].rearrange("p j d -> p (j d)")
        gabs, gsign = [h_flat[0:B, (4 + 2 * n) * D:(6 + 2 * n) * D].rearrange("p (s d) -> p s d", s=2)
                       for n in range(2)]
        ht_flat = ht[:].rearrange("p k c n -> p (k c n)")
        sm_in, sm_xn = [ht_flat[0:2 * NB, n * D:(n + 1) * D] for n in range(2)]
        sm_q, sm_x1 = [ht_flat[0:NB, n * D:(n + 1) * D] for n in range(2, 4)]
        wq_sb = sb("wq_sb", [P, C, D])
        wk_sb = sb("wk_sb", [P, C, D])
        wv_sb = sb("wv_sb", [P, C, D])
        wo_sb = sb("wo_sb", [P, C, D])
        gate_in = sb("gate_in", [NE, D])
        w_route = sb("w_route", [P, C, NR])
        wsd_sb = sb("wsd_sb", [P, D])
        wsd_gated = sb("wsd_gated", [P, D])
        w_gu = sb("w_gu", [P, NE * C * 2 * M])
        w_dn = sb("w_dn", [P, NE * D])
        w_now = sb("w_now", [P, 2, C, 2 * M])
        cond_in = sb("cond_in", [B, D])
        cond_act = sb("cond_act", [B, D])
        cond_t = sb("cond_t", [P, C, B])
        wmod_sb = sb("wmod_sb", [P, C, 6 * D])
        wmod_flat = wmod_sb[:].rearrange("p c n -> p (c n)")
        kt_bd = wmod_flat[:, 0:H * P].rearrange("p (c i n) -> p c i n", c=C, i=CH)
        mod_col = sb("mod_col", [P, 2 * C * B])
        GA, SB_, CB, GB = range(4)
        NORMED = slice(0, 2), slice(2, TPB - 1), slice(TPB - 1, TPB)
        norms = ["a0", "00", "10"]
        for b in range(B):
            norms += [f"a{b + 1}", f"0{b + 1}", f"2{b}", f"1{b + 1}"] if b + 1 < B else [f"2{b}"]

        def norm_no(b, n):
            return norms.index(f"{n}{b}") + 1
        PT_BANK = 6, 6, 4, 6, 5
        mod_bc = sb("mod_bc", [P, B * 4 * D])
        xs = sb("xs", [P, TILES * D])
        sm_stats = sb("sm_stats", [2 * NB, 6])
        sm_mv = sb("sm_mv", [2 * NB, 2])
        sm_rstd = sb("sm_rstd", [2 * NB, 2])
        sm_h = sb("sm_h", [P, C, 2, B, SINKS])
        sm_q_t = sb("sm_q_t", [P, C, NB])
        sink_kt = sb("sink_kt", [P, C, CH, NB])
        sink_v = sb("sink_v", [H * SINKS, B * H * DA])
        sm_m = sb("sm_m", [NB, H])
        sm_p = sb("sm_p", [NB, B, H, SINKS])
        sm_pt = sb("sm_pt", [H * SINKS, B, NB])
        sm_r = sb("sm_r", [NB, H])
        sm_o = sb("sm_o", [NB, H, DH])
        sm_ot = sb("sm_ot", [P, C, NB])
        sm_ga = sb("sm_ga", [NB, D])
        at_stats = sb("at_stats", [P, 6])
        at_mv = sb("at_mv", [P, 2])
        at_rs = sb("at_rs", [P, 2])
        at_xn_sb = sb("at_xn_sb", [P, D])
        at_ht = sb("at_ht", [P, C, P])
        qt = sb("qt", [P, C, P])
        v_aug = sb("v_aug", [P, H, DA])
        m_sink = sb("m_sink", [P, H])
        m_win = sb("m_win", [P, H])
        m_all = sb("m_all", [P, H])
        less_max = sb("less_max", [P, H])
        p_sink = sb("p_sink", [P, H, SINKS])
        p_win = sb("p_win", [P, H, P])
        p_flat = p_win[:].rearrange("p h n -> p (h n)")
        mod = p_flat[0:B, 0:6 * D]
        pt_sink = sb("pt_sink", [H * SINKS, P])
        pt_win = sb("pt_win", [P, H, P])
        rden = sb("rden", [P, H])
        o_n = sb("o_n", [P, H, DH])
        o_t = sb("o_t", [P, C, P])
        o_g = sb("o_g", [P, D])
        st = sb("st", [P, TPB, 6])
        mv = sb("mv", [P, TPB, 2])
        veps = sb("veps", [P, TPB])
        rstd = sb("rstd", [P, TPB])
        centred = sb("centred", [P, 2, D])
        sm_hrep = centred[:].rearrange("p a d -> p (a d)")
        sg = sb("sg", [P, UNROLL, M])
        act_sb = sb("act_sb", [P, UNROLL, M])
        act_t = sb("act_t", [P, UNROLL, P])
        logit = sb("logit", [P, TPB, NE])
        top_v = sb("top_v", [P, TPB, 8])
        top_i = sb("top_i", [P, TPB, 8], U32)
        top_if = sb("top_if", [P, GROUP, TOPK])
        hot = sb("hot", [P, TOPK, GROUP, NE])
        mask_b = sb("mask_b", [P, GROUP, NE], BF16)
        mask_sum = sb("mask_sum", [P, NE])
        counted_b = sb("counted_b", [P, 2, NE], BF16)
        place = sb("place", [P, GROUP, NE])
        at_place = sb("at_place", [P, TOPK, GROUP, NE])
        slot_f = sb("slot_f", [P, TOPK, GROUP])
        slot_i = sb("slot_i", [P, TOPK, TPB], I32)
        val_all = sb("val_all", [P, TOPK, TILES])
        e_neg = sb("e_neg", [P, TOPK * TILES])
        score = sb("score", [P, TOPK, TILES])
        total = sb("total", [P, TILES])
        w_tok = sb("w_tok", [P, TOPK * TILES])
        steps_no = sb("steps_no", [P, TABLE])
        row_no = sb("row_no", [P, CAP - 1])
        n_e = sb("n_e", [P, NE])
        over = sb("over", [P, NE, CAP - 1])
        nt_e = sb("nt_e", [P, NE])
        ones_row = sb("ones_row", [P, NE])
        end_e = sb("end_e", [P, NE])
        tile_e = sb("tile_e", [P, TABLE])
        jump = sb("jump", [1, NE])
        past = wmod_flat[:, 0:TABLE * NE].rearrange("p (t e) -> p t e", e=NE)
        past_jump = wmod_flat[0:1, TABLE * NE:2 * TABLE * NE].rearrange("p (t e) -> p t e", e=NE)
        past_rows = sb("past_rows", [1, TABLE])
        n_over = sb("n_over", [1, MAX_TILES // UNROLL])
        n_fours = sb("n_fours", [1, 1])
        silu_first = sb("silu_first", [1, 1])
        tab = sb("tab", [1, 2 * TABLE], I32)
        misc = sb("misc", [1, NE + 1], I32)
        xt = p_flat[:, 0:UNROLL * DX].rearrange("p (k d) -> p k d", d=DX)
        pt_flat = pt_win[:].rearrange("p h n -> p (h n)")
        y_sb = pt_flat[:, 0:UNROLL * D].rearrange("p (k d) -> p k d", d=D)
        row_f = sb("row_f", [P, UNROLL])
        row_all = sb("row_all", [P, TABLE], I32)
        row_i = sb("row_i", [P, UNROLL], I32)
        QUAD = 4
        RING = NE * C * 2 * M // (QUAD * TOPK * D)
        LAST_QUAD = TILES - QUAD
        got = w_gu[:].rearrange("p (t n d) -> p t n d", n=TOPK, d=D)

        names = """
        ld_cond ld_wmod ld_small ld_wqk ld_wv ld_ws ld_exp x_small pad_dmas
        const setup_t cond_ready mod_ps mod_rows mod_ready col_ps
        col_ready mod_out mod_in sm_gate_ps sm_gate_sb
        sm_veps sm_rs sm_xnr sm_chain sm_hr sm_proj sm_vps sm_kqr sm_vr sm_log sm_sub sm_exp sm_ptp sm_ptr
        sm_ops sm_or sm_otp sm_otr sm_out sm_done
        at_ch at_xn at_xnt at_h at_q at_k at_v at_qs at_ks at_vs at_log at_sub
        at_exp at_pt at_pts at_o at_on at_ot at_ots at_out at_x
        ln_ch ln_veps ln_rstd h_cent h_ready wsd_ready 
        tr_ps tr_sb gu_ps tanh_ready act_ch act_ready aps_ready act_t_sb y_ps y_added lg_ready top_ch rt_ch masks rank_ps
        rank_read slots_ready
        cnt_ps tb tables row_copied waited_apart e_ready part_ready both_ready gated_ready out_ready saved
        """.split()
        S = {n: sem(n) for n in names}
        ld_x = [sem(f"ld_x{b}") for b in range(B)]
        (xt_in, ex_tr_ps, ex_ht, ex_gu_ps, ex_silu, ex_act_sb, ex_w, ex_y_ps, ex_y_sb, row_ready,
         y_out, got_in) = [
            [sem(f"{n}{k}") for k in range(UNROLL)] for n in """
            xt_in ex_tr_ps ex_ht ex_gu_ps ex_silu ex_act_sb ex_w ex_y_ps ex_y_sb row_ready
            y_out got_in""".split()]
        scattered = [sem(f"scattered{j}") for j in range(0, TPB, 2)]

        got_last = ld_x

        def xcols(t):
            return xs[:, ds(t * D, D)]

        def mbc(b, kind, n=1):
            return mod_bc[:, ds(b * (4 * D) + kind * D, n * D)]

        class Chain:

            def __init__(self, eng, s, i=0, per=0, at=0):
                self.eng, self.s, self.i, self.per, self.n = eng, s, i, per, at

            def done(self, ins, alone=False):
                ins.then_inc(self.s, 1)
                self.n += 1
                wait = wait_apart if alone else type(self.eng).wait_ge
                wait(self.eng, self.s, self.i * self.per + self.n)

        def wait_apart(eng, s, value):
            eng.wait_ge(s, value)
            if not isinstance(value, int):
                eng.sem_inc(S["waited_apart"], 1)

        def pad_experts(eng, engine, first):
            rows = nc.values_load_multi_w_load_instructions(
                misc[0:1, first:first + NE // 2], (engine,), min_val=0, max_val=ROWS - P,
                skip_runtime_bounds_check_because="a count of at most all tokens, on its expert's first row")[1]
            for row in rows:
                eng.dma_start(slots[ds(row, P), :], pads[:]).then_inc(S["pad_dmas"], 16)

        def tile_count(eng):
            last4 = eng.value_load(misc[0:1, NE:NE + 1], min_val=MIN_TILES // UNROLL - 1,
                                   max_val=MAX_TILES // UNROLL - 1)
            return last4, eng.snap(last4 + 1)

        def table(engine, first, n, top):
            return nc.values_load_multi_w_load_instructions(
                tab[0:1, ds(first, n)], (engine,), min_val=0, max_val=top,
                skip_runtime_bounds_check_because="the experts' numbers and tiles are clamped where the table is made")[1]

        block = ctx.enter_context(nc.Block())

        @block.sync
        def _(sp):
            chunks = lambda w: w.rearrange("(c p) n -> p c n", p=P)
            sp.dma_start(cond_in[:], cond).then_inc(S["ld_cond"], 16)
            for b in range(B):
                sp.dma_start(sm_in[b * SINKS:(b + 1) * SINKS, :], x[b, 0:SINKS, :]).then_inc(S["ld_small"], 16)
                late = x[b, T - P - SINKS:T - P, :]
                sp.dma_start(sm_in[NB + b * SINKS:NB + (b + 1) * SINKS, :], late).then_inc(S["ld_small"], 16)
            sp.dma_start(wq_sb[:], chunks(wq)).then_inc(S["ld_wqk"], 16)
            sp.dma_start(wk_sb[:], chunks(wk)).then_inc(S["ld_wqk"], 16)
            sp.dma_start(wv_sb[:], chunks(wv)).then_inc(S["ld_wv"], 16)
            sp.dma_start(wo_sb[:], chunks(wo)).then_inc(S["ld_wv"], 16)
            sp.dma_start(gate_in[:], gate_w).then_inc(S["ld_wqk"], 16)
            for b in range(B):
                dst = xs[:, b * TPB * D:(b + 1) * TPB * D].rearrange("p (j d) -> p j d", d=D)
                sp.dma_start(dst, x[b].rearrange("(j p) d -> p j d", p=P)).then_inc(ld_x[b], 16)
                if b == 0:
                    sp.dma_start(w_route[:, :, NE:NE + M], chunks(ws_gate)).then_inc(S["ld_ws"], 16)
                    sp.dma_start(w_route[:, :, NE + M:NR], chunks(ws_up)).then_inc(S["ld_ws"], 16)
                    sp.dma_start(wsd_sb[:], ws_down).then_inc(S["ld_ws"], 16)
            sp.wait_ge(S["mod_ready"], 1)
            sp.dma_start(mod_rows_out, mod[:, 2 * D:6 * D]).then_inc(S["mod_out"], 16)
            sp.wait_ge(S["mod_out"], 16)
            for b in range(B):
                sp.dma_start(mod_bc[:, b * 4 * D:(b + 1) * 4 * D],
                             mod_rows_out[b:b + 1, :].to_broadcast([P, 4 * D])).then_inc(S["mod_in"], 16)
            sp.wait_ge(S["sm_done"], 1)
            for b in range(B):
                sp.wait_ge(ld_x[b], 16)
                j = b * TPB + TPB - 2
                sp.dma_start(xs[P - SINKS:P, j * D:(j + 1) * D],
                             sm_x1[b * SINKS:(b + 1) * SINKS, :]).then_inc(S["x_small"], 16)
            gu = w_gu[:].rearrange("p (c e m) -> p e c m", c=C, m=2 * M)
            for n, w in enumerate((w_gate, w_up)):
                for c in range(C):
                    sp.dma_start(gu[:, :, c, n * M:(n + 1) * M],
                                 w[:, c * P:(c + 1) * P, :].rearrange("e p m -> p e m")).then_inc(S["ld_exp"], 16)
            sp.dma_start(w_dn[:].rearrange("p (e n) -> p e n", n=D),
                         w_down.rearrange("e p n -> p e n")).then_inc(S["ld_exp"], 16)
            sp.wait_ge(S["const"], N_CONST)
            for s in range(SPARE):
                r = (NE * CAP + s) * P
                sp.dma_start(slots[r:r + P, :], pads[:]).then_inc(S["pad_dmas"], 16)

            sp.wait_ge(S["tables"], 1)
            pad_experts(sp, SP, 0)
            sp.wait_ge(S["tables"], 2)
            last4, fours = tile_count(sp)
            sp.wait_ge(S["pad_dmas"], 16 * (SPARE + NE))
            for s in scattered:
                sp.wait_ge(s, 2 * 16 * TOPK * B)

            def load(row, k):
                sp.dma_start(xt[:, k, :], slots[ds(row, P), :]).then_inc(xt_in[k], 16)

            for k, row in enumerate(table(SP, TABLE, UNROLL, ROWS - P)):
                load(row, k)
            with sp.Fori(0, fours) as u:
                rows = table(SP, u * UNROLL + TABLE + UNROLL, UNROLL, ROWS - P)
                n = sp.snap(u + 1)
                for k in range(UNROLL):
                    wait_apart(sp, ex_tr_ps[k], n)
                    wait_apart(sp, row_ready[k], n * 2)
                    load(rows[k], k)
            for k in range(UNROLL):
                wait_apart(sp, y_out[k], fours * 16)
                wait_apart(sp, xt_in[k], fours * 16 + 16)

            def load_rows(t, n):
                at = t % (RING * QUAD)
                sp.dma_start(got[:, at:at + n, :, :],
                             ys[t * TOPK * P:(t + n) * TOPK * P, :].rearrange("(t p n) d -> p t n d", t=n, n=TOPK))\
                    .then_inc(got_in[t // QUAD % RING] if n == QUAD else got_last[t - LAST_QUAD], 16)

            def save(t, n):
                sp.wait_ge(S["out_ready"], t + n)
                b, j = divmod(t, TPB)
                sp.dma_start(out[b, j * P:(j + n) * P, :].rearrange("(t p) d -> p t d", p=P),
                             xs[:, t * D:(t + n) * D].rearrange("p (t d) -> p t d", d=D)).then_inc(S["saved"], 16)

            for q in range(RING):
                load_rows(q * QUAD, QUAD)
            for t in range(0, LAST_QUAD, QUAD):
                save(t, QUAD)
                ahead = t + RING * QUAD
                if ahead < LAST_QUAD:
                    load_rows(ahead, QUAD)
                elif ahead == LAST_QUAD:
                    for i in range(QUAD):
                        load_rows(ahead + i, 1)
            for t in range(LAST_QUAD, TILES):
                save(t, 1)
            sp.wait_ge(S["saved"], 16 * (LAST_QUAD // QUAD + QUAD))

        @block.gpsimd
        def _(pool):
            c = Chain(pool, S["const"])
            c.done(pool.memset(ident[:], 0.0))
            c.done(pool.affine_select(out=ident[:], in_=ident[:], pattern=[[-1, P]], compare_op=ALU.not_equal,
                                        fill=1.0, base=0, channel_multiplier=1))
            c.done(pool.memset(minus_half[:], -0.5))
            c.done(pool.memset(head_block[:], 1.0))
            c.done(pool.affine_select(out=head_block[:], in_=head_block[:], pattern=[[-SINKS, H]],
                                      compare_op=ALU.is_ge, fill=0.0, base=0, channel_multiplier=1))
            c.done(pool.affine_select(out=head_block[:], in_=head_block[:], pattern=[[SINKS, H]],
                                      compare_op=ALU.is_ge, fill=0.0, base=SINKS - 1, channel_multiplier=-1))
            c.done(pool.memset(own_rows[:], 1.0))
            c.done(pool.affine_select(out=own_rows[:], in_=own_rows[:], pattern=[[-DH, CH]],
                                      compare_op=ALU.is_ge, fill=0.0, base=0, channel_multiplier=1))
            c.done(pool.affine_select(out=own_rows[:], in_=own_rows[:], pattern=[[DH, CH]],
                                      compare_op=ALU.is_ge, fill=0.0, base=DH - 1, channel_multiplier=-1))
            c.done(pool.tensor_copy(ident_b[:], ident[:]))
            c.done(pool.memset(small_mask_b[:], 0.0))
            c.done(pool.affine_select(out=small_mask_b[:], in_=small_mask_b[:],
                                      pattern=[[-SINKS, B], [0, H], [-1, SINKS]], compare_op=ALU.is_ge,
                                      fill=MASKED, base=0, channel_multiplier=1))
            c.done(pool.affine_select(out=small_mask_b[:], in_=small_mask_b[:],
                                      pattern=[[SINKS, B], [0, H], [0, SINKS]], compare_op=ALU.is_ge,
                                      fill=MASKED, base=SINKS - 1, channel_multiplier=-1))
            pool.wait_ge(S["sm_veps"], 1)
            pool.tensor_tensor(sm_rstd[:, 1:2], sm_rstd[:, 0:1], minus_half[0:2 * NB, 0:1], ALU.pow)\
                .then_inc(S["sm_rs"], 1)
            c.done(pool.memset(causal_b[:], 0.0))
            c.done(pool.affine_select(out=causal_b[:], in_=causal_b[:], pattern=[[-1, P]], compare_op=ALU.is_ge,
                                      fill=MASKED, base=0, channel_multiplier=1))
            c.done(pool.memset(pick_rows[:], 0.0))
            c.done(pool.affine_select(out=pick_rows[:], in_=pick_rows[:], pattern=[[-1, B], [0, SINKS]],
                                      compare_op=ALU.not_equal, fill=1.0, base=0, channel_multiplier=1))
            c.done(pool.memset(before_b[:], 0.0))
            c.done(pool.affine_select(out=before_b[:], in_=before_b[:], pattern=[[-1, P]], compare_op=ALU.is_ge,
                                      fill=1.0, base=0, channel_multiplier=1))
            c.done(pool.memset(ones_b[:], 1.0))
            c.done(pool.memset(v_aug[:], 1.0))
            c.done(pool.memset(counted_b[:], 0.0))
            c.done(pool.memset(pads[:], 0.0))
            c.done(pool.memset(pads[:, D:D + 1], PAD))
            c.done(pool.iota(token2[:], pattern=[[2 * P, TILES]], base=0, channel_multiplier=2,
                             allow_small_or_imprecise_dtypes=True))
            c.done(pool.iota(pad_row[:], pattern=[[P, TABLE]], base=TOPK * B * T, channel_multiplier=1,
                             allow_small_or_imprecise_dtypes=True))
            c.done(pool.memset(ones_row[:], 1.0))
            c.done(pool.iota(expert_no[:], pattern=[[1, NE]], base=0, channel_multiplier=0,
                             allow_small_or_imprecise_dtypes=True))
            c.done(pool.iota(expert_row[:], pattern=[[CAP * P, NE]], base=0, channel_multiplier=0,
                             allow_small_or_imprecise_dtypes=True))
            c.done(pool.iota(steps_no[:], pattern=[[1, TABLE]], base=0, channel_multiplier=0,
                             allow_small_or_imprecise_dtypes=True))
            c.done(pool.iota(row_no[:], pattern=[[P, CAP - 1]], base=0, channel_multiplier=0,
                             allow_small_or_imprecise_dtypes=True))
            assert c.n == N_CONST


            def rsqrt(b, n, r):
                pool.wait_ge(S["ln_veps"], norm_no(b, n))
                pool.tensor_tensor(rstd[:, r], veps[:, r], minus_half[:, r], ALU.pow).then_inc(S["ln_rstd"], 1)

            def scatter(j):
                for k in range(TOPK):
                    pool.indirect_dma_start(
                        out=slots, out_offset=bass.IndirectOffsetOnAxis(ap=slot_i[:, k, j:j + 1], axis=0),
                        in_=h_sb[:, j, :], in_offset=None).then_inc(scattered[j // 2], 16)

            def norms_ahead(b):
                pool.wait_ge(S["ln_veps"], norm_no(b, "a"))
                pool.tensor_tensor(at_rs[:, 1:2], at_rs[:, 0:1], minus_half[:, 0:1], ALU.pow)\
                    .then_inc(S["ln_rstd"], 1)
                rsqrt(b, 0, NORMED[0])

            norms_ahead(0)
            pool.wait_ge(S["ld_ws"], 48)
            pool.wait_ge(S["mod_in"], 16 * B)
            for b in range(B):
                rsqrt(b, 1, NORMED[1])
                if b > 0:
                    pool.wait_ge(S["slots_ready"], b * GPB)
                    scatter(GROUP)
                    scatter(GROUP + 1)
                    pool.wait_ge(S["y_ps"], b * TPB)
                pool.tensor_tensor(wsd_gated[:], wsd_sb[:], mbc(b, GB), ALU.mult).then_inc(S["wsd_ready"], 1)
                if b > 0:
                    scatter(GROUP + 2)
                    scatter(GROUP + 3)
                if b + 1 < B:
                    norms_ahead(b + 1)
                rsqrt(b, 2, NORMED[2])
                pool.wait_ge(S["slots_ready"], b * GPB + 1)
                scatter(0)
                scatter(1)
                scatter(2)
                scatter(3)
            pool.wait_ge(S["slots_ready"], B * GPB)
            for j in range(GROUP, TPB):
                scatter(j)
            pool.wait_ge(S["tables"], 2)
            last4, fours = tile_count(pool)

            def put(t, k, u, n):
                wait_apart(pool, row_ready[k], n * 2)
                if u is not None:
                    wait_apart(pool, y_out[k], u * 16)
                pool.tensor_copy(row_i[:, k:k + 1], row_all[:, ds(t, 1)]).then_inc(S["row_copied"], 1)
                wait_apart(pool, ex_y_sb[k], n)
                wait_apart(pool, S["row_copied"], t + 1)
                pool.indirect_dma_start(out=ys, out_offset=bass.IndirectOffsetOnAxis(ap=row_i[:, k:k + 1], axis=0),
                                        in_=y_sb[:, k, :], in_offset=None).then_inc(y_out[k], 16)

            for k in range(UNROLL):
                put(k, k, None, 1)
            with pool.Fori(1, fours) as u:
                n = pool.snap(u + 1)
                for k in range(UNROLL):
                    put(u * UNROLL + k, k, u, n)

            for t in range(TILES):
                pool.wait_ge(S["gated_ready"], t + 1)
                pool.tensor_tensor(xcols(t), xcols(t), got[:, t % (RING * QUAD), 0, :], ALU.add)\
                    .then_inc(S["out_ready"], 1)

        @block.scalar
        def _(act):
            copy = lambda o, i: act.activation(o, i, ACT.Copy)
            act.dma_start(wmod_sb[:], w_mod.rearrange("(c p) n -> p c n", p=P)).then_inc(S["ld_wmod"], 16)
            for b in range(B):
                act.dma_start(sm_q[b * SINKS:(b + 1) * SINKS, :], x[b, T - P - SINKS:T - P, :])\
                    .then_inc(S["ld_small"], 16)
            act.wait_ge(S["ld_cond"], 16)
            act.activation(cond_act[:], cond_in[:], ACT.Silu).then_inc(S["cond_ready"], 1)
            act.wait_ge(S["setup_t"], 1)
            copy(cond_t[:].rearrange("p c b -> p (c b)"), bank[0][:, 0:C * B]).then_inc(S["cond_ready"], 1)
            act.wait_ge(S["sm_gate_ps"], 1)
            copy(sm_ga[:], bank[6][0:NB, 0:D]).then_inc(S["sm_gate_sb"], 1)
            act.wait_ge(S["sm_sub"], 1)
            act.activation(sm_p[:], sm_p[:], ACT.Exp, scale=SCALE).then_inc(S["sm_exp"], 1)
            act.wait_ge(S["sm_ptp"], 1)
            copy(sm_pt[:].rearrange("p b n -> p (b n)"), bank[5][0:H * SINKS, 0:B * NB]).then_inc(S["sm_ptr"], 1)
            act.wait_ge(S["sm_otp"], 1)
            copy(sm_ot[:].rearrange("p c n -> p (c n)"), bank[7][:, 0:C * NB]).then_inc(S["sm_otr"], 1)
            act.wait_ge(S["const"], N_CONST)

            def tanh(b, j):
                act.wait_ge(S["gu_ps"], b * TPB + j)
                act.activation(sg[:, (j - 1) % UNROLL, :], bank[1][:, NE:NE + M], ACT.Tanh, scale=0.5)\
                    .then_inc(S["tanh_ready"], 1)

            def act_copy(b, j):
                act.wait_ge(S["aps_ready"], b * TPB + j - 1)
                copy(act_t[:, (j - 2) % UNROLL, :], bank[2][:, 0:P]).then_inc(S["act_t_sb"], 1)

            def h_copy(b, j):
                act.wait_ge(S["tr_ps"], b * TPB + j + 1)
                copy(ht[:, j % UNROLL, :, :].rearrange("p c n -> p (c n)"), bank[0][:, 0:D]).then_inc(S["tr_sb"], 1)

            def at_exp(b, g):
                act.wait_ge(S["at_sub"], b * (HG + 1) + g + 1)
                if g == HG:
                    act.activation(p_sink[:], p_sink[:], ACT.Exp, scale=SCALE).then_inc(S["at_exp"], 1)
                    return
                for i in range(4):
                    h = 4 * g + i
                    last = act.activation(p_win[:, h, :], bank[4 + g % 2][:, i * P:(i + 1) * P], ACT.Exp, scale=SCALE,
                                          bias=less_max[:, h:h + 1])
                last.then_inc(S["at_exp"], 1)

            def at_probs(b, g):
                act.wait_ge(S["at_pt"], b * (HG + 1) + g + 1)
                if g < HG:
                    copy(pt_win[:, 4 * g:4 * g + 4, :].rearrange("p h n -> p (h n)"), bank[PT_BANK[g]][:])\
                        .then_inc(S["at_pts"], 1)
                else:
                    copy(pt_sink[:], bank[PT_BANK[g]][0:H * SINKS, 0:P]).then_inc(S["at_pts"], 1)

            def second_keys(b, heads):
                for i in heads:
                    last = act.activation(kt_bd[:, 1, i, :], bank[4][:, 2 * P:3 * P], ACT.Copy,
                                          scale=own_rows[:, i:i + 1])
                if i == CH - 1:
                    last.then_inc(S["at_qs"], 1)

            for b in range(B):
                if b > 0:
                    tanh(b, 0)
                act.wait_ge(S["at_q"], b + 1)
                copy(qt[:].rearrange("p c n -> p (c n)"), bank[4][:, 0:D]).then_inc(S["at_qs"], 1)
                second_keys(b, range(0, 3))
                if b > 0:
                    act_copy(b, 0)
                h_copy(b, 0)
                second_keys(b, range(3, CH))
                act.wait_ge(S["at_v"], b + 1)
                copy(v_aug[:, :, 0:DH], bank[6][:, 0:D].rearrange("p (h s) -> p h s", s=DH))\
                    .then_inc(S["at_vs"], 1)
                tanh(b, 1)
                if b > 0:
                    act_copy(b, 1)
                h_copy(b, 1)
                at_exp(b, 0)
                tanh(b, 2)
                at_probs(b, 0)
                act_copy(b, 2)
                h_copy(b, 2)
                at_exp(b, 1)
                at_exp(b, 2)
                tanh(b, 3)
                at_probs(b, 1)
                act_copy(b, 3)
                h_copy(b, 3)
                at_exp(b, 3)
                at_exp(b, 4)
                at_probs(b, 2)
                tanh(b, 4)
                at_probs(b, 3)
                at_probs(b, 4)
                act_copy(b, 4)
                h_copy(b, 4)
                tanh(b, 5)
                act.wait_ge(S["at_ot"], b + 1)
                copy(o_t[:].rearrange("p c n -> p (c n)"), bank[6][:, 0:D]).then_inc(S["at_ots"], 1)
                act_copy(b, 5)
                h_copy(b, 5)
                tanh(b, 6)
                act_copy(b, 6)
                h_copy(b, 6)
                tanh(b, 7)
                act_copy(b, 7)
                h_copy(b, 7)
            tanh(B, 0)
            act_copy(B, 0)
            act_copy(B, 1)

            act.wait_ge(S["tables"], 1)
            pad_experts(act, mybir.EngineType.Activation, NE // 2)
            act.activation(e_neg[:], val_all[:].rearrange("p k t -> p (k t)"), ACT.Exp, scale=-1.0)\
                .then_inc(S["e_ready"], 1)
            act.activation(silu_first[:], ones_row[0:1, 0:1], ACT.Silu)
            act.wait_ge(S["tables"], 2)
            last4, fours = tile_count(act)

            def ex_h(k, n):
                act.wait_ge(ex_tr_ps[k], n)
                copy(ht[:, k, :, :].rearrange("p c n -> p (c n)"), bank[k % 2][:, 0:D]).then_inc(ex_ht[k], 1)

            def ex_weights(k, e):
                copy(w_now[:, k % 2, :, :], w_gu[:].rearrange("p (c n) -> p c n", c=C)[:, :, ds(e, 2 * M)])\
                    .then_inc(ex_w[k], 1)

            def ex_s(k, n):
                act.wait_ge(ex_gu_ps[k], n)
                act.activation(sg[:, k, :], bank[2 + k % 2][:, 0:P], ACT.Silu).then_inc(ex_silu[k], 1)

            act.wait_ge(S["ld_exp"], 16 * (2 * C + 1))
            e = table(mybir.EngineType.Activation, 0, UNROLL + 1, (NE - 1) * 2 * M)
            ex_weights(0, e[0])
            ex_h(0, 1)
            for k in range(UNROLL):
                ex_weights((k + 1) % UNROLL, e[k + 1])
                ex_h((k + 1) % UNROLL, 1 if k < UNROLL - 1 else 2)
                ex_s(k, 1)
            with act.Fori(1, fours) as u:
                e = table(mybir.EngineType.Activation, u * UNROLL + 1, UNROLL, (NE - 1) * 2 * M)
                n = act.snap(u + 1)
                for k in range(UNROLL - 1):
                    ex_weights(k + 1, e[k])
                    ex_h(k + 1, n)
                    ex_s(k, n)
                ex_weights(0, e[UNROLL - 1])
                ex_h(0, n + 1)
                ex_s(UNROLL - 1, n)

            for t in range(TILES):
                q, k = t // QUAD, t % (RING * QUAD)
                if t < LAST_QUAD:
                    act.wait_ge(got_in[q % RING], 16 * (q // RING + 1))
                else:
                    act.wait_ge(got_last[t - LAST_QUAD], 2 * 16)
                act.activation(got[:, k, 0, :], got[:, k, 0, :], ACT.Copy, scale=w_tok[:, t:t + 1])\
                    .then_inc(S["part_ready"], 1)

        @block.tensor
        def _(pe):
            mm = nc.tensor.matmul

            def transpose(o, i):
                n = i.shape[0]
                return nc.tensor.transpose(o, i, ident[0:n, 0:n])

            def at_tr(b):
                pe.wait_ge(S["at_xn"], b + 1)
                for k in range(C):
                    last = transpose(bank[7][:, k * P:(k + 1) * P], at_xn_sb[:, k * P:(k + 1) * P])
                last.then_inc(S["at_xnt"], 1)

            pe.wait_ge(S["const"], 2)
            pe.wait_ge(S["cond_ready"], 1)
            for k in range(C):
                last = transpose(bank[0][:, k * B:(k + 1) * B], cond_act[:, k * P:(k + 1) * P])
            last.then_inc(S["setup_t"], 1)
            pe.wait_ge(S["cond_ready"], 2)
            pe.wait_ge(S["ld_wmod"], 16)
            for s in range(2 * C):
                for k in range(C):
                    last = mm(bank[2][:, s * B:(s + 1) * B], wmod_sb[:, k, s * P:(s + 1) * P], cond_t[:, k, :],
                              start=(k == 0), stop=(k == C - 1))
            last.then_inc(S["col_ps"], 1)
            pe.wait_ge(S["sm_xnr"], 1)
            for k in range(C):
                last = transpose(bank[0][:, k * 2 * NB:(k + 1) * 2 * NB], sm_xn[:, k * P:(k + 1) * P])
            last.then_inc(S["setup_t"], 1)
            for n in (1, 2):
                for k in range(C):
                    last = mm(bank[4 + n][0:B, :], cond_t[:, k, :], wmod_sb[:, k, n * 2 * D:(n + 1) * 2 * D],
                              start=(k == 0), stop=(k == C - 1))
            last.then_inc(S["mod_ps"], 1)
            pe.wait_ge(S["ld_wqk"], 48)
            for k in range(C):
                last = transpose(bank[7][:, k * NE:(k + 1) * NE], gate_in[:, k * P:(k + 1) * P])
            last.then_inc(S["setup_t"], 1)
            pe.wait_ge(S["sm_hr"], C * B)
            for n, w in enumerate((wk_sb, wq_sb)):
                for c in range(C):
                    o = (n * C + c) * NB
                    for k in range(C):
                        last = mm(bank[1][:, o:o + NB], w[:, k, c * P:(c + 1) * P],
                                  sm_h[:, k, n, :, :].rearrange("p b i -> p (b i)"), start=(k == 0),
                                  stop=(k == C - 1))
            last.then_inc(S["sm_proj"], 1)
            pe.wait_ge(S["ld_wv"], 32)
            pe.wait_ge(S["sm_hr"], C * B + C)
            for b in range(B):
                for k in range(C):
                    last = mm(bank[2 + b // 2][0:H * SINKS, (b % 2) * D:(b % 2 + 1) * D],
                              sm_hrep[:, (k * B + b) * H * SINKS:(k * B + b + 1) * H * SINKS], wv_sb[:, k, :],
                              start=(k == 0), stop=(k == C - 1))
            last.then_inc(S["sm_vps"], 1)
            pe.wait_ge(S["mod_ready"], 1)
            pe.wait_ge(S["const"], N_CONST)
            mm(bank[6][0:NB, 0:D], pick_rows[:], mod[:, 2 * D:3 * D], start=True, stop=True)\
                .then_inc(S["sm_gate_ps"], 1)
            pe.wait_ge(S["sm_kqr"], 1 + C)
            logits = bank[4][0:NB, 0:B * H * SINKS].rearrange("q (b h k) -> q b h k", b=B, h=H)
            mm(bank[4][0:NB, 0:B * H * SINKS], ident_b[0:NB, 0:NB], small_mask_b[:], start=True, stop=False,
               skip_group_check=True)
            for c in range(C):
                last = mm(logits.rearrange("q b (c i) k -> q c i b k", c=C)[:, c], sm_q_t[:, c, :],
                          sink_kt[:, c, :, :].rearrange("p i (b k) -> p i b k", b=B), start=False,
                          stop=(c == C - 1), skip_group_check=True)
            last.then_inc(S["sm_log"], 1)
            pe.wait_ge(S["sm_exp"], 1)
            for b in range(B):
                last = transpose(bank[5][0:H * SINKS, b * NB:(b + 1) * NB], sm_p[:, b, :, :].rearrange("q h k -> q (h k)"))
            last.then_inc(S["sm_ptp"], 1)
            at_tr(0)
            pe.wait_ge(S["sm_ptr"], 1)
            pe.wait_ge(S["sm_vr"], B + 1)
            pe.wait_ge(S["sm_gate_sb"], 1)
            for b in range(B):
                last = mm(bank[6][0:NB, 0:H * DA], sm_pt[:, b, :], sink_v[:, b * H * DA:(b + 1) * H * DA],
                          start=(b == 0), stop=(b == B - 1))
            last.then_inc(S["sm_ops"], 1)
            pe.wait_ge(S["sm_or"], 1)
            pe.wait_ge(S["at_h"], C)
            for k in range(C):
                last = transpose(bank[7][:, k * NB:(k + 1) * NB],
                                 sm_o[:].rearrange("q h s -> q (h s)")[:, k * P:(k + 1) * P])
            last.then_inc(S["sm_otp"], 1)
            pe.wait_ge(S["sm_otr"], 1)
            for k in range(C):
                last = mm(bank[7][0:NB, 0:D], sm_ot[:, k, :], wo_sb[:, k, :], start=(k == 0), stop=(k == C - 1))
            last.then_inc(S["sm_out"], 1)

            pe.wait_ge(S["ld_ws"], 48)
            def at_qkv(b):
                pe.wait_ge(S["at_h"], b * C + C)
                for w, c, o, s in ((wk_sb, 0, bank[5][:, 0:P], "at_k"), (wq_sb, 0, bank[4][:, 0:P], None),
                                   (wq_sb, 1, bank[4][:, P:2 * P], None), (wk_sb, 1, bank[4][:, 2 * P:3 * P], "at_q")):
                    for k in range(C):
                        last = mm(o, w[:, k, c * P:(c + 1) * P], at_ht[:, k, :], start=(k == 0), stop=(k == C - 1))
                    if s:
                        last.then_inc(S[s], 1)
                for k in range(C):
                    last = mm(bank[6][:, 0:D], at_ht[:, k, :], wv_sb[:, k, :], start=(k == 0), stop=(k == C - 1))
                last.then_inc(S["at_v"], 1)

            def at_sinks(b):
                pe.wait_ge(S["at_qs"], b * 2 + 1)
                for c in range(C):
                    last = mm(bank[7][:, c * CH * SINKS:(c + 1) * CH * SINKS], qt[:, c, :],
                              sink_kt[:, c, :, ds(b * SINKS, SINKS)], start=True, stop=True)
                last.then_inc(S["at_log"], 1)

            def at_logits(b, g):
                o = bank[4 + g % 2][:]
                if g >= 2:
                    pe.wait_ge(S["at_exp"], b * (HG + 1) + g - 1)
                if g == 0:
                    pe.wait_ge(S["at_ks"], b + 1)
                    pe.wait_ge(S["at_qs"], b * 2 + 2)
                mm(o, ident_b[:], causal_b[:].unsqueeze(1).to_broadcast([P, 4, P]), start=True, stop=False,
                   skip_group_check=True)
                c, i = divmod(4 * g, CH)
                mm(o, qt[:, c, :], kt_bd[:, c, i:i + 4, :].rearrange("p i n -> p (i n)"), start=False, stop=True,
                   skip_group_check=True).then_inc(S["at_log"], 1)

            def at_probs_t(b, g):
                (wait_apart if g == HG else type(pe).wait_ge)(pe, S["at_exp"], b * (HG + 1) + g + 1)
                if g in (1, 3):
                    pe.wait_ge(S["at_pts"], b * (HG + 1) + (g + 1) // 2)
                if g == HG:
                    transpose(bank[PT_BANK[g]][0:H * SINKS, 0:P], p_sink[:].rearrange("q h k -> q (h k)"))\
                        .then_inc(S["at_pt"], 1)
                    return
                for i in range(4):
                    last = transpose(bank[PT_BANK[g]][:, i * P:(i + 1) * P], p_win[:, 4 * g + i, :])
                last.then_inc(S["at_pt"], 1)

            def at_values(b):
                wait_apart(pe, S["at_pts"], b * (HG + 1) + HG + 1)
                mm(bank[7][:, 0:H * DA], pt_sink[:], sink_v[:, ds(b * (H * DA), H * DA)], start=True, stop=False,
                   skip_group_check=True)
                for h in range(H):
                    last = mm(bank[7][:, h * DA:(h + 1) * DA], pt_win[:, h, :], v_aug[:, h, :], start=False,
                              stop=(h == H - 1), skip_group_check=True)
                last.then_inc(S["at_o"], 1)

            def at_out_t(b):
                pe.wait_ge(S["at_on"], b + 1)
                for k in range(C):
                    last = transpose(bank[6][:, k * P:(k + 1) * P],
                                     o_n[:].rearrange("q h s -> q (h s)")[:, k * P:(k + 1) * P])
                last.then_inc(S["at_ot"], 1)

            def at_project(b):
                pe.wait_ge(S["at_ots"], b + 1)
                for k in range(C):
                    last = mm(bank[5][:, 0:D], o_t[:, k, :], wo_sb[:, k, :], start=(k == 0), stop=(k == C - 1))
                last.then_inc(S["at_out"], 1)

            def tr(b, j):
                pe.wait_ge(S["h_ready"], b * TPB + j + 1)
                for k in range(C):
                    last = transpose(bank[0][:, k * P:(k + 1) * P], h_sb[:, j, k * P:(k + 1) * P])
                last.then_inc(S["tr_ps"], 1)

            def gate_up(b, j, first=False):
                pe.wait_ge(S["tr_sb"], b * TPB + j)
                if not first or j >= 2:
                    pe.wait_ge(S["act_ready"], b * TPB + j - 1)
                    pe.wait_ge(S["lg_ready"], b * TPB + j - 1)
                for k in range(C):
                    last = mm(bank[1][:, 0:NR], ht[:, (j - 1) % UNROLL, k, :], w_route[:, k, :],
                              start=(k == 0), stop=(k == C - 1))
                last.then_inc(S["gu_ps"], 1)

            def act_tr(b, j, first=False):
                pe.wait_ge(S["act_ready"], b * TPB + j - 1)
                if not first or j >= 3:
                    pe.wait_ge(S["act_t_sb"], b * TPB + j - 2)
                transpose(bank[2][:, 0:P], act_sb[:, (j - 2) % UNROLL, :]).then_inc(S["aps_ready"], 1)

            def down(b, j, first=False):
                pe.wait_ge(S["act_t_sb"], b * TPB + j - 2)
                if j == 3:
                    pe.wait_ge(S["wsd_ready"], b + 1)
                if not first or j >= 4:
                    pe.wait_ge(S["y_added"], b * TPB + j - 3)
                if j == 2 or j == GROUP + 2:
                    pe.wait_ge(S["rank_read"], b * GPB + j // GROUP)
                mm(bank[3][:, 0:D], act_t[:, (j - 3) % UNROLL, :], wsd_gated[:], start=True, stop=True)\
                    .then_inc(S["y_ps"], 1)

            def rank(b, j):
                g = 1 if j == 1 else 0
                pe.wait_ge(S["masks"], b * GPB + 1 - g)
                pe.wait_ge(S["y_added"], b * TPB + j - 3)
                o = bank[3][:, D:D + GROUP * NE]
                mm(o, ones_b[:], counted_b[:, g, :].unsqueeze(1).to_broadcast([P, GROUP, NE]), start=True,
                   stop=False, skip_group_check=True)
                last = mm(o, before_b[:], mask_b[:].rearrange("p t e -> p (t e)"), start=False, stop=False,
                          skip_group_check=True)
                for i in range(GROUP - 1):
                    last = mm(bank[3][:, D + (i + 1) * NE:D + GROUP * NE], ones_b[:],
                              mask_b[:, i:i + 1, :].to_broadcast([P, GROUP - 1 - i, NE]), start=False,
                              stop=(i == GROUP - 2), skip_group_check=True)
                last.then_inc(S["rank_ps"], 1)

            for b in range(B):
                if b > 0:
                    gate_up(b, 0, b == 0)
                at_qkv(b)
                if b > 0:
                    act_tr(b, 0, b == 0)
                tr(b, 0)
                if b > 0:
                    down(b, 0, b == 0)
                gate_up(b, 1, b == 0)
                at_sinks(b)
                at_logits(b, 0)
                at_logits(b, 1)
                if b > 0:
                    act_tr(b, 1, b == 0)
                    rank(b, 1)
                tr(b, 1)
                if b > 0:
                    down(b, 1, b == 0)
                gate_up(b, 2, b == 0)
                at_logits(b, 2)
                pe.wait_ge(S["at_vs"], b + 1)
                at_probs_t(b, 0)
                act_tr(b, 2, b == 0)
                tr(b, 2)
                if b > 0:
                    down(b, 2, b == 0)
                gate_up(b, 3, b == 0)
                at_logits(b, 3)
                at_probs_t(b, 1)
                act_tr(b, 3, b == 0)
                tr(b, 3)
                down(b, 3, b == 0)
                at_probs_t(b, 2)
                gate_up(b, 4, b == 0)
                at_probs_t(b, 3)
                at_probs_t(b, 4)
                act_tr(b, 4, b == 0)
                tr(b, 4)
                down(b, 4, b == 0)
                at_values(b)
                gate_up(b, 5, b == 0)
                at_out_t(b)
                act_tr(b, 5, b == 0)
                rank(b, 5)
                at_project(b)
                tr(b, 5)
                down(b, 5, b == 0)
                gate_up(b, 6, b == 0)
                act_tr(b, 6, b == 0)
                tr(b, 6)
                down(b, 6, b == 0)
                act_tr(b, 7, b == 0)
                gate_up(b, 7, b == 0)
                if b + 1 < B:
                    at_tr(b + 1)
                tr(b, 7)
                down(b, 7, b == 0)
            gate_up(B, 0)
            act_tr(B, 0)
            down(B, 0)
            act_tr(B, 1)
            rank(B, 1)
            down(B, 1)
            pe.wait_ge(S["rt_ch"], RT_CH * GPB * B - AFTER_COUNTED)
            mm(bank[0][:, 0:NE], ones_b[:], counted_b[:, 0, :], start=True, stop=True).then_inc(S["cnt_ps"], 1)
            down(B, 2)

            pe.wait_ge(S["tables"], 2)
            pe.wait_ge(S["ld_exp"], 16 * (2 * C + 1))
            last4, fours = tile_count(pe)

            def ex_tr(k, n):
                pe.wait_ge(xt_in[k], n * 16)
                for c in range(C):
                    last = transpose(bank[k % 2][:, c * P:(c + 1) * P], xt[:, k, c * P:(c + 1) * P])
                last.then_inc(ex_tr_ps[k], 1)

            def ex_gu(k, n):
                wait_apart(pe, ex_w[k], n)
                pe.wait_ge(ex_ht[k], n)
                for half in range(2):
                    for c in range(C):
                        last = mm(bank[2 + k % 2][:, half * P:(half + 1) * P],
                                  w_now[:, k % 2, c, half * M:(half + 1) * M],
                                  ht[:, k, c, :], start=(c == 0), stop=(c == C - 1))
                last.then_inc(ex_gu_ps[k], 1)

            def ex_dn(k, e, n):
                pe.wait_ge(ex_act_sb[k], n)
                mm(bank[6 + k % 2][:, 0:D], act_t[:, k, :], w_dn[:, ds(e, D)], start=True, stop=True)\
                    .then_inc(ex_y_ps[k], 1)

            e = table(PE, 0, UNROLL, (NE - 1) * 2 * M)
            ex_tr(0, 1)
            for k in range(UNROLL):
                ex_tr((k + 1) % UNROLL, 1 if k < UNROLL - 1 else 2)
                ex_gu(k, 1)
                if k >= 1:
                    ex_dn(k - 1, e[k - 1], 1)
            with pe.Fori(1, fours) as u:
                e = table(PE, u * UNROLL - 1, UNROLL + 1, (NE - 1) * 2 * M)
                n = pe.snap(u + 1)
                for k in range(UNROLL):
                    ex_tr((k + 1) % UNROLL, n if k < UNROLL - 1 else n + 1)
                    ex_gu(k, n)
                    ex_dn((k - 1) % UNROLL, e[k], n if k >= 1 else u)
            e = table(PE, last4 * UNROLL + UNROLL - 1, 1, (NE - 1) * 2 * M)
            ex_dn(UNROLL - 1, e[0], fours)

        @block.vector
        def _(dve):
            v = nc.vector
            ls = bank[7][:, 0:H * SINKS].rearrange("q (h k) -> q h k", h=H)
            lws = [bank[4 + g % 2][:].rearrange("q (h k) -> q h k", h=4) for g in range(HG)]

            def at_norm(b, at):
                at.done(v.bn_stats(at_stats[:], xcols(b * TPB + TPB - 1)), alone=True)
                at.done(v.bn_aggr(at_mv[:], at_stats[:]))
                v.tensor_scalar(at_rs[:, 0:1], at_mv[:, 1:2], EPS, None, ALU.add).then_inc(S["ln_veps"], 1)

            def at_xn(b):
                dve.wait_ge(S["ln_rstd"], norm_no(b, "a"))
                v.tensor_scalar(at_xn_sb[:], xcols(b * TPB + TPB - 1), at_mv[:, 0:1], at_rs[:, 1:2], ALU.subtract,
                                ALU.mult).then_inc(S["at_xn"], 1)

            def at_modulate(b):
                dve.wait_ge(S["at_xnt"], b + 1)
                for k in range(C):
                    v.tensor_scalar(at_ht[:, k, :], bank[7][:, k * P:(k + 1) * P],
                                    mod_col[:, ds(b + (C + k) * B, 1)], mod_col[:, ds(b + k * B, 1)],
                                    ALU.mult, ALU.add).then_inc(S["at_h"], 1)

            def at_keys(b):
                dve.wait_ge(S["at_k"], b + 1)
                v.tensor_tensor(kt_bd[:, 0, :, :], bank[5][:, 0:P].unsqueeze(1).to_broadcast([P, CH, P]),
                                own_rows[:].unsqueeze(2).to_broadcast([P, CH, P]), ALU.mult).then_inc(S["at_ks"], 1)

            def at_sink_max(b, at):
                dve.wait_ge(S["at_log"], b * (HG + 1) + 1)
                at.done(v.tensor_reduce(m_sink[:], ls, AX.X, ALU.max))

            def at_less_max(b, g, at):
                dve.wait_ge(S["at_log"], b * (HG + 1) + g + 2)
                hs = slice(4 * g, 4 * g + 4)
                at.done(v.tensor_reduce(m_win[:, hs], lws[g], AX.X, ALU.max))
                at.done(v.tensor_tensor(m_all[:, hs], m_win[:, hs], m_sink[:, hs], ALU.max))
                v.tensor_scalar(less_max[:, hs], m_all[:, hs], -SCALE, None, ALU.mult).then_inc(S["at_sub"], 1)

            def at_sinks_less_max(b):
                v.tensor_tensor(p_sink[:], ls, m_all[:].unsqueeze(2).to_broadcast([P, H, SINKS]), ALU.subtract)\
                    .then_inc(S["at_sub"], 1)

            def at_normalise(b, at):
                dve.wait_ge(S["at_o"], b + 1)
                ob = bank[7][:, 0:H * DA].rearrange("q (h s) -> q h s", h=H)
                at.done(v.reciprocal(rden[:], ob[:, :, DH]))
                v.tensor_tensor(o_n[:], ob[:, :, 0:DH], rden[:].unsqueeze(2).to_broadcast([P, H, DH]), ALU.mult)\
                    .then_inc(S["at_on"], 1)

            def at_add(b, at):
                dve.wait_ge(S["at_out"], b + 1)
                at.done(v.tensor_tensor(o_g[:], bank[5][:, 0:D], mbc(b, GA), ALU.mult))
                tail = xcols(b * TPB + TPB - 1)
                v.tensor_tensor(tail, tail, o_g[:], ALU.add).then_inc(S["at_x"], 1)

            def norm_stats(b, n, ln):
                r = range(TPB)[NORMED[n]]
                for j in r:
                    v.bn_stats(st[:, j, :], xcols(b * TPB + j)).then_inc(S["ln_ch"], 1)
                    ln.n += 1
                dve.wait_ge(S["ln_ch"], ln.n)
                for j in r:
                    v.bn_aggr(mv[:, j, :], st[:, j, :]).then_inc(S["ln_ch"], 1)
                    ln.n += 1
                dve.wait_ge(S["ln_ch"], ln.n)
                v.tensor_scalar(veps[:, NORMED[n]], mv[:, NORMED[n], 1], EPS, None, ALU.add)\
                    .then_inc(S["ln_veps"], 1)

            def h_tile(b, j, first):
                dve.wait_ge(S["ln_rstd"], norm_no(b, 0 if j < 2 else 1 if j < TPB - 1 else 2))
                v.scalar_tensor_tensor(centred[:, j % 2, :], xcols(b * TPB + j), mv[:, j, 0:1], mbc(b, CB),
                                       ALU.subtract, ALU.mult).then_inc(S["h_cent"], 1)
                if not first:
                    dve.wait_ge(scattered[j // 2], b * (2 * 16 * TOPK))
                wait_apart(dve, S["h_cent"], b * TPB + j + 1)
                v.scalar_tensor_tensor(h_sb[:, j, 0:D], centred[:, j % 2, :], rstd[:, j:j + 1], mbc(b, SB_),
                                       ALU.mult, ALU.add).then_inc(S["h_ready"], 1)

            def activation(b, j):
                k = (j - 1) % TPB
                dve.wait_ge(S["tanh_ready"], b * TPB + j)
                v.scalar_tensor_tensor(act_sb[:, k % UNROLL, :], sg[:, k % UNROLL, :], 1.0, bank[1][:, NE + M:NR],
                                       ALU.add, ALU.mult).then_inc(S["act_ch"], 1)
                v.tensor_scalar(logit[:, k, :], bank[1][:, 0:NE], SATURATED, None, ALU.min)\
                    .then_inc(S["lg_ready"], 1)
                wait_apart(dve, S["act_ch"], b * TPB + j)
                v.scalar_tensor_tensor(act_sb[:, k % UNROLL, :], bank[1][:, NE:NE + M], 0.5,
                                       act_sb[:, k % UNROLL, :], ALU.mult, ALU.mult).then_inc(S["act_ready"], 1)
                wait_apart(dve, S["lg_ready"], b * TPB + j)
                v.max(top_v[:, k, :], logit[:, k, :]).then_inc(S["top_ch"], 1)
                wait_apart(dve, S["top_ch"], b * (2 * TPB) + 2 * j - 1)
                v.max_index(top_i[:, k, :], top_v[:, k, :], logit[:, k, :]).then_inc(S["top_ch"], 1)

            def add_y(b, j):
                dve.wait_ge(S["y_ps"], b * TPB + j - 2)
                x = xcols(b * TPB + j - 3)
                v.tensor_tensor(x, x, bank[3][:, 0:D], ALU.add).then_inc(S["y_added"], 1)

            def chosen(b, j):
                first = b * TPB + j - GROUP
                g = 1 if j == 0 else 0
                r = slice(g * GROUP, (g + 1) * GROUP)
                rt = Chain(dve, S["rt_ch"], b, GPB * RT_CH, -g * RT_CH)
                dve.wait_ge(S["top_ch"], b * (2 * TPB) + 2 * j)
                v.tensor_copy(val_all[:, :, ds(first, GROUP)], top_v[:, r, 0:TOPK].rearrange("p t k -> p k t"))\
                    .then_inc(S["rt_ch"], 1)
                rt.n += 1
                rt.done(v.tensor_copy(top_if[:], top_i[:, r, 0:TOPK]))
                for n in range(TOPK):
                    rt.done(v.tensor_tensor(hot[:, n, :, :], expert_no[:].unsqueeze(1).to_broadcast([P, GROUP, NE]),
                                            top_if[:, :, n:n + 1].to_broadcast([P, GROUP, NE]), ALU.is_equal))
                for col, src in ((D, token2[:, ds(first, GROUP)]), (D + 1, top_if[:, :, 0])):
                    v.tensor_copy(h_sb[:, r, col], src).then_inc(S["rt_ch"], 1)
                    rt.n += 1
                v.tensor_tensor(mask_b[:], hot[:, 0, :, :], hot[:, 1, :, :], ALU.add).then_inc(S["masks"], 1)
                dve.wait_ge(S["masks"], b * GPB + 1 - g)
                rt.done(v.tensor_reduce(mask_sum[:], mask_b[:].rearrange("p t e -> p e t"), AX.X, ALU.add))
                return rt

            def ranked(b, j, rt):
                g = 1 if j == 1 else 0
                def count():
                    rt.done(v.tensor_tensor(counted_b[:, 1 - g, :], counted_b[:, g, :], mask_sum[:], ALU.add))

                if b == B:
                    count()
                dve.wait_ge(S["rank_ps"], b * GPB + 1 - g)
                wait_apart(dve, S["y_ps"], b * TPB + j - 2)
                v.tensor_tensor(place[:], bank[3][:, D:D + GROUP * NE].rearrange("p (t e) -> p t e", e=NE),
                                expert_row[:].unsqueeze(1).to_broadcast([P, GROUP, NE]), ALU.add)\
                    .then_inc(S["rank_read"], 1)
                if b < B:
                    count()

            def placed(b, j, rt):
                g = 1 if j == 1 else 0
                dve.wait_ge(S["rank_read"], b * GPB + 1 - g)
                for n in range(TOPK):
                    rt.done(v.tensor_tensor(at_place[:, n, :, :], place[:], hot[:, n, :, :], ALU.mult))
                rt.done(v.tensor_reduce(slot_f[:], at_place[:], AX.X, ALU.add))
                r = slice(g * GROUP, (g + 1) * GROUP)
                v.tensor_copy(slot_i[:, :, r], slot_f[:]).then_inc(S["slots_ready"], 1)

            dve.wait_ge(S["ld_small"], 48 * B)
            ch = Chain(dve, S["sm_chain"])
            ch.done(v.bn_stats(sm_stats[:], sm_in))
            ch.done(v.bn_aggr(sm_mv[:], sm_stats[:]))
            v.tensor_scalar(sm_rstd[:, 0:1], sm_mv[:, 1:2], EPS, None, ALU.add).then_inc(S["sm_veps"], 1)
            dve.wait_ge(S["sm_rs"], 1)
            v.tensor_scalar(sm_xn, sm_in, sm_mv[:, 0:1], sm_rstd[:, 1:2], ALU.subtract, ALU.mult)\
                .then_inc(S["sm_xnr"], 1)
            dve.wait_ge(S["col_ps"], 1)
            v.tensor_copy(mod_col[:, 0:C * B], bank[2][:, 0:C * B]).then_inc(S["col_ready"], 1)
            v.tensor_scalar(mod_col[:, C * B:2 * C * B], bank[2][:, C * B:2 * C * B], 1.0, None, ALU.add)\
                .then_inc(S["col_ready"], 1)
            dve.wait_ge(S["col_ready"], 2)
            dve.wait_ge(S["setup_t"], 2)
            for k in range(C):
                view = bank[0][:, k * 2 * NB:(k + 1) * 2 * NB].rearrange("p (n b i) -> p n b i", n=2, b=B)
                for b in range(B):
                    v.tensor_scalar(sm_h[:, k, :, b, :], view[:, :, b, :],
                                    mod_col[:, (C + k) * B + b:(C + k) * B + b + 1],
                                    mod_col[:, k * B + b:k * B + b + 1], ALU.mult, ALU.add).then_inc(S["sm_hr"], 1)
            dve.wait_ge(S["sm_hr"], C * B)
            for k in range(C):
                rep = sm_hrep[:, k * B * H * SINKS:(k + 1) * B * H * SINKS]
                v.tensor_copy(rep.rearrange("p (b h i) -> p b h i", b=B, h=H),
                              sm_h[:, k, 0, :, :].unsqueeze(2).to_broadcast([P, B, H, SINKS]))\
                    .then_inc(S["sm_hr"], 1)
            dve.wait_ge(S["mod_ps"], 1)
            for n in (1, 2):
                v.tensor_copy(mod[:, n * 2 * D:(n + 1) * 2 * D], bank[4 + n][0:B, :]).then_inc(S["mod_rows"], 1)
            dve.wait_ge(S["mod_rows"], 2)
            g = Chain(dve, S["mod_rows"], at=2)
            gates = mod.rearrange("b (s d) -> b s d", d=D)[:, 2::3, :]
            g.done(v.scalar_tensor_tensor(gabs, gates, -1.0, gates, ALU.mult, ALU.max))
            g.done(v.tensor_scalar(gsign, gates, 0.0, 2.0, ALU.is_ge, ALU.mult))
            g.done(v.tensor_scalar(gabs, gabs, 0.25, None, ALU.max))
            g.done(v.scalar_tensor_tensor(gates, gsign, -1.0, gabs, ALU.add, ALU.mult))
            v.tensor_scalar(mod[:, 4 * D:5 * D], mod[:, 4 * D:5 * D], 1.0, None, ALU.add)\
                .then_inc(S["mod_ready"], 1)
            dve.wait_ge(S["setup_t"], 3)
            v.tensor_copy(w_route[:, :, 0:NE], bank[7][:, 0:C * NE].rearrange("p (c e) -> p c e", c=C))\
                .then_inc(S["col_ready"], 1)
            dve.wait_ge(S["sm_proj"], 1)
            dve.wait_ge(S["const"], N_CONST)
            v.tensor_copy(sm_q_t[:].rearrange("p c q -> p (c q)"), bank[1][:, C * NB:2 * C * NB])\
                .then_inc(S["sm_kqr"], 1)
            for c in range(C):
                v.tensor_tensor(sink_kt[:, c, :, :],
                                bank[1][:, c * NB:(c + 1) * NB].unsqueeze(1).to_broadcast([P, CH, NB]),
                                own_rows[:].unsqueeze(2).to_broadcast([P, CH, NB]), ALU.mult)\
                    .then_inc(S["sm_kqr"], 1)
            dve.wait_ge(S["sm_vps"], 1)
            dve.wait_ge(S["const"], N_CONST)
            sv = sink_v[:].rearrange("p (b h s) -> p b h s", b=B, h=H)
            for b in range(B):
                src = bank[2 + b // 2][0:H * SINKS, (b % 2) * D:(b % 2 + 1) * D]
                v.tensor_tensor(sv[:, b, :, 0:DH], src.rearrange("p (h s) -> p h s", h=H),
                                head_block[:].unsqueeze(2).to_broadcast([H * SINKS, H, DH]), ALU.mult)\
                    .then_inc(S["sm_vr"], 1)
            v.tensor_copy(sv[:, :, :, DH], head_block[:].unsqueeze(1).to_broadcast([H * SINKS, B, H]))\
                .then_inc(S["sm_vr"], 1)
            dve.wait_ge(S["sm_log"], 1)
            lg = bank[4][0:NB, 0:B * H * SINKS].rearrange("q (b h k) -> q b h k", b=B, h=H)
            ch.done(v.tensor_reduce(sm_m[:], lg.rearrange("q b h k -> q h b k"), AX.XY, ALU.max))
            for b in range(B):
                last = v.tensor_tensor(sm_p[:, b, :, :], lg[:, b, :, :],
                                       sm_m[:].unsqueeze(2).to_broadcast([NB, H, SINKS]), ALU.subtract)
                if b < B - 1:
                    ch.done(last)
            last.then_inc(S["sm_sub"], 1)
            dve.wait_ge(ld_x[0], 16)
            at, ln = Chain(dve, S["at_ch"]), Chain(dve, S["ln_ch"])
            at_norm(0, at)
            norm_stats(0, 0, ln)
            at_xn(0)
            at_modulate(0)
            dve.wait_ge(S["sm_ops"], 1)
            so = bank[6][0:NB, 0:H * DA].rearrange("q (h s) -> q h s", h=H)
            ch.done(v.reciprocal(sm_r[:], so[:, :, DH]))
            v.tensor_tensor(sm_o[:], so[:, :, 0:DH], sm_r[:].unsqueeze(2).to_broadcast([NB, H, DH]), ALU.mult)\
                .then_inc(S["sm_or"], 1)
            dve.wait_ge(S["sm_out"], 1)
            dve.wait_ge(S["sm_gate_sb"], 1)
            ch.done(v.tensor_tensor(sm_x1, bank[7][0:NB, 0:D], sm_ga[:], ALU.mult))
            v.tensor_tensor(sm_x1, sm_x1, sm_q, ALU.add).then_inc(S["sm_done"], 1)
            dve.wait_ge(S["mod_in"], 16 * B)
            dve.wait_ge(S["ld_ws"], 48)

            for b in range(B):
                first = b == 0
                h_tile(b, 0, first)
                if not first:
                    add_y(b - 1, 7)
                    activation(b, 0)
                at_keys(b)
                if not first:
                    rt = chosen(b, 0)
                h_tile(b, 1, first)
                if not first:
                    add_y(b, 0)
                if first:
                    dve.wait_ge(S["x_small"], 16 * B)
                    norm_stats(b, 1, ln)
                at_sink_max(b, at)
                activation(b, 1)
                at_less_max(b, 0, at)
                if not first:
                    ranked(b, 1, rt)
                h_tile(b, 2, first)
                if not first:
                    placed(b, 1, rt)
                    add_y(b, 1)
                at_less_max(b, 1, at)
                activation(b, 2)
                at_less_max(b, 2, at)
                h_tile(b, 3, first)
                if not first:
                    add_y(b, 2)
                at_less_max(b, 3, at)
                activation(b, 3)
                at_sinks_less_max(b)
                h_tile(b, 4, first)
                add_y(b, 3)
                activation(b, 4)
                if b + 1 < B:
                    dve.wait_ge(ld_x[b + 1], 16)
                    at_norm(b + 1, at)
                    norm_stats(b + 1, 0, ln)
                rt = chosen(b, 4)
                h_tile(b, 5, first)
                add_y(b, 4)
                at_normalise(b, at)
                activation(b, 5)
                h_tile(b, 6, first)
                at_add(b, at)
                if b + 1 < B:
                    at_xn(b + 1)
                ranked(b, 5, rt)
                dve.wait_ge(S["at_x"], b + 1)
                norm_stats(b, 2, ln)
                placed(b, 5, rt)
                add_y(b, 5)
                activation(b, 6)
                h_tile(b, 7, first)
                add_y(b, 6)
                if b + 1 < B:
                    at_modulate(b + 1)
                activation(b, 7)
                if b + 1 < B:
                    norm_stats(b + 1, 1, ln)
            add_y(B - 1, 7)
            activation(B, 0)
            add_y(B, 0)
            rt = chosen(B, 0)
            ranked(B, 1, rt)
            placed(B, 1, rt)

            dve.wait_ge(S["cnt_ps"], 1)
            dve.wait_ge(S["slots_ready"], B * GPB)
            tb = Chain(dve, S["tb"])
            tb.done(v.tensor_copy(n_e[:], bank[0][:, 0:NE]))
            v.tensor_tensor(misc[:, 0:NE], n_e[0:1, :], expert_row[0:1, :], ALU.add).then_inc(S["tables"], 1)
            add_y(B, 1)
            tb.done(v.tensor_tensor(over[:], n_e[:].unsqueeze(2).to_broadcast([P, NE, CAP - 1]),
                                    row_no[:].unsqueeze(1).to_broadcast([P, NE, CAP - 1]), ALU.is_gt))
            tb.done(v.tensor_reduce(nt_e[:], over[:], AX.X, ALU.add))
            tb.done(v.tensor_tensor_scan(end_e[:], ones_row[:], nt_e[:], 0.0, ALU.mult, ALU.add))
            tb.done(v.tensor_scalar(jump[:], nt_e[0:1, :], -float(P), float(CAP * P), ALU.mult, ALU.add))
            tb.done(v.tensor_tensor(past, steps_no[:].unsqueeze(2).to_broadcast([P, TABLE, NE]),
                                    end_e[:].unsqueeze(1).to_broadcast([P, TABLE, NE]), ALU.is_ge))
            tb.done(v.tensor_tensor(past_jump, past[0:1, :, :], jump[:].unsqueeze(1).to_broadcast([1, TABLE, NE]),
                                    ALU.mult))
            tb.done(v.tensor_reduce(past_rows[:], past_jump, AX.X, ALU.add))
            tb.done(v.tensor_reduce(tile_e[:], past, AX.X, ALU.add))
            tb.done(v.tensor_tensor(n_over[:], end_e[0:1, NE - 1:NE].to_broadcast([1, MAX_TILES // UNROLL]),
                                    steps_no[0:1, 0:MAX_TILES:UNROLL], ALU.is_gt))
            tb.done(v.tensor_scalar(tile_e[:], tile_e[:], float(NE - 1), None, ALU.min))
            tb.done(v.tensor_reduce(n_fours[:], n_over[:], AX.X, ALU.add))
            tb.done(v.tensor_scalar(tab[:, 0:TABLE], tile_e[0:1, :], float(2 * M), None, ALU.mult))
            tb.done(v.scalar_tensor_tensor(tab[:, TABLE:2 * TABLE], steps_no[0:1, :], float(P), past_rows[:], ALU.mult,
                                           ALU.add))
            add_y(B, 2)
            v.tensor_scalar(misc[:, NE:NE + 1], n_fours[:], -1.0, None, ALU.add).then_inc(S["tables"], 1)
            dve.wait_ge(S["e_ready"], 1)
            sc = score[:].rearrange("p k t -> p (k t)")
            tb.done(v.tensor_scalar(e_neg[:], e_neg[:], 1.0, None, ALU.add))
            tb.done(v.reciprocal(sc, e_neg[:]))
            tb.done(v.tensor_tensor(total[:], score[:, 0, :], score[:, 1, :], ALU.add))
            tb.done(v.tensor_scalar(total[:], total[:], 1e-20, None, ALU.add))
            tb.done(v.reciprocal(total[:], total[:]))
            for n in range(TOPK):
                tb.done(v.scalar_tensor_tensor(w_tok[:, n * TILES:(n + 1) * TILES], score[:, n, :], ROUTE_SCALE,
                                              total[:], ALU.mult, ALU.mult))
            dve.wait_ge(S["tables"], 2)
            last4, fours = tile_count(dve)

            def ex_act(k, n):
                dve.wait_ge(ex_silu[k], n)
                v.tensor_tensor(act_t[:, k, :], bank[2 + k % 2][:, P:2 * P], sg[:, k, :], ALU.mult)\
                    .then_inc(ex_act_sb[k], 1)

            def ex_y(k, n, stored):
                dve.wait_ge(ex_y_ps[k], n)
                if stored is not None:
                    dve.wait_ge(y_out[k], stored * 16)
                v.tensor_copy(y_sb[:, k, :], bank[6 + k % 2][:, 0:D]).then_inc(ex_y_sb[k], 1)

            def rows(t, k, n):
                dve.wait_ge(xt_in[k], n * 16)
                v.scalar_tensor_tensor(row_f[:, k:k + 1], xt[:, k, D + 1:DX], tile_e[:, ds(t, 1)],
                                       xt[:, k, D:D + 1], ALU.not_equal, ALU.add).then_inc(row_ready[k], 1)
                wait_apart(dve, row_ready[k], n * 2 - 1)
                v.tensor_tensor(row_all[:, ds(t, 1)], row_f[:, k:k + 1], pad_row[:, ds(t, 1)], ALU.min)\
                    .then_inc(row_ready[k], 1)

            for t in range(2 * UNROLL):
                k, n = t % UNROLL, t // UNROLL + 1
                rows(t, k, n)
                if t >= 2:
                    ex_y((t - 2) % UNROLL, (t - 2) // UNROLL + 1, 1 if t - 2 >= UNROLL else None)
                ex_act(k, n)
            with dve.Fori(2, fours) as u:
                n = dve.snap(u + 1)
                for k in range(UNROLL):
                    rows(u * UNROLL + k, k, n)
                    ex_y((k - 2) % UNROLL, n if k >= 2 else u, u if k >= 2 else u - 1)
                    ex_act(k, n)
            ex_y(UNROLL - 2, fours, last4)
            ex_y(UNROLL - 1, fours, last4)

            for t in range(TILES):
                k = t % (RING * QUAD)
                dve.wait_ge(S["part_ready"], t + 1)
                v.scalar_tensor_tensor(got[:, k, 1, :], got[:, k, 1, :], w_tok[:, t + TILES:t + TILES + 1],
                                       got[:, k, 0, :], ALU.mult, ALU.add).then_inc(S["both_ready"], 1)
                dve.wait_ge(S["both_ready"], t + 1)
                v.tensor_tensor(got[:, k, 0, :], got[:, k, 1, :], mbc(t // TPB, GB), ALU.mult)\
                    .then_inc(S["gated_ready"], 1)


N_CONST = 31
RT_CH = 11
AFTER_COUNTED = 3

_INS = ["L0_attn_x", "L0_attn_Wq", "L0_attn_Wk", "L0_attn_Wv", "L0_attn_Wo", "L0_ffn_gate_w", "L0_ffn_w_gate",
        "L0_ffn_w_up", "L0_ffn_w_down", "L0_ffn_ws_gate", "L0_ffn_ws_up", "L0_ffn_ws_down", "L0_c", "L0_wmod"]
_OUTS = [((4, 1024, 256), "float32")]


def kernel(**inputs):
    import numpy as _np
    import concourse.bacc as _bacc
    from concourse import mybir as _mybir
    from concourse.bass_utils import run_bass_kernel_spmd as _run

    nc = _bacc.Bacc("TRN2", target_bir_lowering=False, num_devices=1)
    arrays, args = {}, []
    for name in _INS:
        a = _np.ascontiguousarray(inputs[name])
        arrays[f"in_{name}_dram"] = a
        args.append(nc.dram_tensor(f"in_{name}_dram", a.shape, _mybir.dt.from_np(a.dtype), kind="ExternalInput").ap())
    for i, (shape, dtype) in enumerate(_OUTS):
        dt = _mybir.dt.from_np(_np.dtype(dtype))
        args.append(nc.dram_tensor(f"out_{i}_dram", shape, dt, kind="ExternalOutput").ap())
    bass_adaln_attention_moe(nc, *args)
    r = _run(nc, [arrays], core_ids=[0])
    got = tuple(r.results[0][f"out_{i}_dram"] for i in range(len(_OUTS)))
    return got[0]
```
